# Optimizing a Trainium2 kernel written in Bass

```python
import numpy as np
import jax
import jax.numpy as jnp

def _softmax(x, axis=-1):
    return jax.nn.softmax(x, axis=axis)

def _gelu(x):
    return jax.nn.gelu(x, approximate=True)

def _silu(x):
    return jax.nn.silu(x)

def _sigmoid(x):
    return jax.nn.sigmoid(x)

def _layernorm(x, axis=-1, eps=1e-05):
    m = jnp.mean(x, axis=axis, keepdims=True)
    v = jnp.var(x, axis=axis, keepdims=True)
    return (x - m) / jnp.sqrt(v + eps)

def _scatter_add(tgt, idx, src, axis=0):
    return tgt.at[idx].add(src)

def _segment_sum(src, seg, n):
    return jax.ops.segment_sum(src, seg, n)
kernel_name = 'mk_prb_d1_jaxref_r8_91dd50'

def setup_inputs(seed: int=0):
    np.random.seed(seed)
    _w = jnp.asarray

    def _L0_attn_setup():
        import jax, jax.numpy as jnp
        import numpy as np
        D_MODEL = 128
        D_STATE = 128
        EXPAND = 2
        HEADDIM = 64
        NGROUPS = 1
        D_INNER = EXPAND * D_MODEL
        NHEADS = D_INNER // HEADDIM
        N_ANGLES = D_STATE // 2 // 2
        CHUNK = 64
        DT_MIN, DT_MAX, DT_FLOOR, A_FLOOR = (0.001, 0.1, 0.0001, 0.0001)
        EPS = 1e-05
        BATCH, SEQLEN = (2, 256)

        def _rope(t, theta):
            na = theta.shape[-1]
            x1, x2, rest = (t[..., :na], t[..., na:2 * na], t[..., 2 * na:])
            c, s = (jnp.cos(theta), jnp.sin(theta))
            return jnp.concatenate([x1 * c - x2 * s, x1 * s + x2 * c, rest], axis=-1)

        def _rmsnorm(t, w):
            var = jnp.mean(t * t, axis=-1, keepdims=True)
            return t * jax.lax.rsqrt(var + EPS) * w

        def _forward(u, W_in, W_out, dt_bias, B_bias, C_bias, B_norm_w, C_norm_w, D):
            b, L, _ = u.shape
            proj = u @ W_in
            sizes = [D_INNER, D_INNER, D_STATE * NGROUPS, D_STATE * NGROUPS, NHEADS, NHEADS, NHEADS, N_ANGLES]
            z, x, Bg, Cg, dd_dt, dd_A, trap, angles = jnp.split(proj, np.cumsum(sizes)[:-1], axis=-1)
            z = z.reshape(b, L, NHEADS, HEADDIM)
            x = x.reshape(b, L, NHEADS, HEADDIM)
            a = jnp.minimum(-jax.nn.softplus(dd_A), -A_FLOOR)
            dt = jax.nn.softplus(dd_dt + dt_bias)
            adt = a * dt
            theta = jnp.cumsum(angles[:, :, None, :] * dt[..., None], axis=1)
            Bn = _rmsnorm(Bg, B_norm_w)
            Cn = _rmsnorm(Cg, C_norm_w)
            K = _rope(Bn[:, :, None, :] + B_bias, theta)
            Q = _rope(Cn[:, :, None, :] + C_bias, theta)
            beta = jax.nn.sigmoid(trap)
            g1 = beta * dt
            dt_prev = jnp.pad(dt[:, :-1], ((0, 0), (1, 0), (0, 0)))
            g2 = (1.0 - beta) * jnp.exp(adt) * dt_prev
            Kp = jnp.pad(K[:, :-1], ((0, 0), (1, 0), (0, 0), (0, 0)))
            xp = jnp.pad(x[:, :-1], ((0, 0), (1, 0), (0, 0), (0, 0)))
            nc = L // CHUNK
            ch = lambda t: t.reshape(b, nc, CHUNK, *t.shape[2:])
            Qc, Kc, Kpc, xc, xpc = (ch(Q), ch(K), ch(Kp), ch(x), ch(xp))
            g1c, g2c, adtc = (ch(g1), ch(g2), ch(adt))
            ell = jnp.cumsum(adtc, axis=2)
            decay = jnp.exp(ell[:, :, :, None, :] - ell[:, :, None, :, :])
            mask = jnp.tril(jnp.ones((CHUNK, CHUNK), bool))
            decay = jnp.where(mask[None, None, :, :, None], decay, 0.0)
            S1 = jnp.einsum('bcihn,bcjhn->bcijh', Qc, Kc) * g1c[:, :, None, :, :] * decay
            S2 = jnp.einsum('bcihn,bcjhn->bcijh', Qc, Kpc) * g2c[:, :, None, :, :] * decay
            y_intra = jnp.einsum('bcijh,bcjhp->bcihp', S1, xc) + jnp.einsum('bcijh,bcjhp->bcihp', S2, xpc)
            dec_end = jnp.exp(ell[:, :, -1:, :] - ell)
            Wsum = jnp.einsum('bcjh,bcjhp,bcjhn->bchpn', g1c * dec_end, xc, Kc) + jnp.einsum('bcjh,bcjhp,bcjhn->bchpn', g2c * dec_end, xpc, Kpc)
            chunk_decay = jnp.exp(ell[:, :, -1, :])

            def step(Hprev, inp):
                wc, cd = inp
                return (cd[:, :, None, None] * Hprev + wc, Hprev)
            H0 = jnp.zeros((b, NHEADS, HEADDIM, D_STATE), u.dtype)
            _, Hprevs = jax.lax.scan(step, H0, (jnp.moveaxis(Wsum, 1, 0), jnp.moveaxis(chunk_decay, 1, 0)))
            Hprevs = jnp.moveaxis(Hprevs, 0, 1)
            y_inter = jnp.einsum('bcihn,bcih,bchpn->bcihp', Qc, jnp.exp(ell), Hprevs)
            y = (y_intra + y_inter).reshape(b, L, NHEADS, HEADDIM)
            y = y + D[None, None, :, None] * x
            y = y * jax.nn.silu(z)
            return y.reshape(b, L, D_INNER) @ W_out
        key = jax.random.key(seed)
        ks = jax.random.split(key, 4)
        d_in_proj = 2 * D_INNER + 2 * D_STATE * NGROUPS + 3 * NHEADS + N_ANGLES
        u = jax.random.normal(ks[0], (BATCH, SEQLEN, D_MODEL), jnp.float32)
        W_in = jax.random.normal(ks[1], (D_MODEL, d_in_proj), jnp.float32) * 0.02
        W_out = jax.random.normal(ks[2], (D_INNER, D_MODEL), jnp.float32) * 0.02
        _dt = jnp.exp(jax.random.uniform(ks[3], (NHEADS,), jnp.float32) * (np.log(DT_MAX) - np.log(DT_MIN)) + np.log(DT_MIN))
        _dt = jnp.maximum(_dt, DT_FLOOR)
        dt_bias = _dt + jnp.log(-jnp.expm1(-_dt))
        return dict(u=u, W_in=W_in, W_out=W_out, dt_bias=dt_bias, B_bias=jnp.ones((NHEADS, D_STATE), jnp.float32), C_bias=jnp.ones((NHEADS, D_STATE), jnp.float32), B_norm_w=jnp.ones((D_STATE,), jnp.float32), C_norm_w=jnp.ones((D_STATE,), jnp.float32), D=jnp.ones((NHEADS,), jnp.float32))
    _L0_attn_in = _L0_attn_setup()

    def _L0_ffn_setup():
        import jax, jax.numpy as jnp
        import numpy as np
        K = 2
        key = jax.random.key(seed)
        ks = jax.random.split(key, 6)
        B, S, D, U, E = (2, 256, 128, 512, 8)
        return {'x': jax.random.normal(ks[0], (B, S, D), dtype=jnp.float32), 'w_router': jax.random.normal(ks[1], (E, D), dtype=jnp.float32), 'w_up': jax.random.normal(ks[2], (E, U, D), dtype=jnp.float32), 'b_up': jax.random.normal(ks[3], (E, U), dtype=jnp.float32), 'w_down': jax.random.normal(ks[4], (E, D, U), dtype=jnp.float32), 'b_down': jax.random.normal(ks[5], (E, D), dtype=jnp.float32)}
    _L0_ffn_in = _L0_ffn_setup()
    _d = {'L0_attn_u': _L0_attn_in['u'], 'L0_attn_W_in': _L0_attn_in['W_in'], 'L0_attn_W_out': _L0_attn_in['W_out'], 'L0_attn_dt_bias': _L0_attn_in['dt_bias'], 'L0_attn_B_bias': _L0_attn_in['B_bias'], 'L0_attn_C_bias': _L0_attn_in['C_bias'], 'L0_attn_B_norm_w': _L0_attn_in['B_norm_w'], 'L0_attn_C_norm_w': _L0_attn_in['C_norm_w'], 'L0_attn_D': _L0_attn_in['D'], 'L0_ffn_w_router': _L0_ffn_in['w_router'], 'L0_ffn_w_up': _L0_ffn_in['w_up'], 'L0_ffn_b_up': _L0_ffn_in['b_up'], 'L0_ffn_w_down': _L0_ffn_in['w_down'], 'L0_ffn_b_down': _L0_ffn_in['b_down']}
    _x0 = _d['L0_attn_u']
    _d['L0_attn_u'] = jax.random.normal(jax.random.fold_in(jax.random.key(seed), 1), (8, 512, 128), dtype=_x0.dtype)
    del _x0
    return _d

def reference(L0_attn_u, L0_attn_W_in, L0_attn_W_out, L0_attn_dt_bias, L0_attn_B_bias, L0_attn_C_bias, L0_attn_B_norm_w, L0_attn_C_norm_w, L0_attn_D, L0_ffn_w_router, L0_ffn_w_up, L0_ffn_b_up, L0_ffn_w_down, L0_ffn_b_down):

    def _L0_attn_ref(u, W_in, W_out, dt_bias, B_bias, C_bias, B_norm_w, C_norm_w, D):
        import jax, jax.numpy as jnp
        import numpy as np
        D_MODEL = 128
        D_STATE = 128
        EXPAND = 2
        HEADDIM = 64
        NGROUPS = 1
        D_INNER = EXPAND * D_MODEL
        NHEADS = D_INNER // HEADDIM
        N_ANGLES = D_STATE // 2 // 2
        CHUNK = 64
        DT_MIN, DT_MAX, DT_FLOOR, A_FLOOR = (0.001, 0.1, 0.0001, 0.0001)
        EPS = 1e-05
        BATCH, SEQLEN = (2, 256)

        def _rope(t, theta):
            na = theta.shape[-1]
            x1, x2, rest = (t[..., :na], t[..., na:2 * na], t[..., 2 * na:])
            c, s = (jnp.cos(theta), jnp.sin(theta))
            return jnp.concatenate([x1 * c - x2 * s, x1 * s + x2 * c, rest], axis=-1)

        def _rmsnorm(t, w):
            var = jnp.mean(t * t, axis=-1, keepdims=True)
            return t * jax.lax.rsqrt(var + EPS) * w

        def _forward(u, W_in, W_out, dt_bias, B_bias, C_bias, B_norm_w, C_norm_w, D):
            b, L, _ = u.shape
            proj = u @ W_in
            sizes = [D_INNER, D_INNER, D_STATE * NGROUPS, D_STATE * NGROUPS, NHEADS, NHEADS, NHEADS, N_ANGLES]
            z, x, Bg, Cg, dd_dt, dd_A, trap, angles = jnp.split(proj, np.cumsum(sizes)[:-1], axis=-1)
            z = z.reshape(b, L, NHEADS, HEADDIM)
            x = x.reshape(b, L, NHEADS, HEADDIM)
            a = jnp.minimum(-jax.nn.softplus(dd_A), -A_FLOOR)
            dt = jax.nn.softplus(dd_dt + dt_bias)
            adt = a * dt
            theta = jnp.cumsum(angles[:, :, None, :] * dt[..., None], axis=1)
            Bn = _rmsnorm(Bg, B_norm_w)
            Cn = _rmsnorm(Cg, C_norm_w)
            K = _rope(Bn[:, :, None, :] + B_bias, theta)
            Q = _rope(Cn[:, :, None, :] + C_bias, theta)
            beta = jax.nn.sigmoid(trap)
            g1 = beta * dt
            dt_prev = jnp.pad(dt[:, :-1], ((0, 0), (1, 0), (0, 0)))
            g2 = (1.0 - beta) * jnp.exp(adt) * dt_prev
            Kp = jnp.pad(K[:, :-1], ((0, 0), (1, 0), (0, 0), (0, 0)))
            xp = jnp.pad(x[:, :-1], ((0, 0), (1, 0), (0, 0), (0, 0)))
            nc = L // CHUNK
            ch = lambda t: t.reshape(b, nc, CHUNK, *t.shape[2:])
            Qc, Kc, Kpc, xc, xpc = (ch(Q), ch(K), ch(Kp), ch(x), ch(xp))
            g1c, g2c, adtc = (ch(g1), ch(g2), ch(adt))
            ell = jnp.cumsum(adtc, axis=2)
            decay = jnp.exp(ell[:, :, :, None, :] - ell[:, :, None, :, :])
            mask = jnp.tril(jnp.ones((CHUNK, CHUNK), bool))
            decay = jnp.where(mask[None, None, :, :, None], decay, 0.0)
            S1 = jnp.einsum('bcihn,bcjhn->bcijh', Qc, Kc) * g1c[:, :, None, :, :] * decay
            S2 = jnp.einsum('bcihn,bcjhn->bcijh', Qc, Kpc) * g2c[:, :, None, :, :] * decay
            y_intra = jnp.einsum('bcijh,bcjhp->bcihp', S1, xc) + jnp.einsum('bcijh,bcjhp->bcihp', S2, xpc)
            dec_end = jnp.exp(ell[:, :, -1:, :] - ell)
            Wsum = jnp.einsum('bcjh,bcjhp,bcjhn->bchpn', g1c * dec_end, xc, Kc) + jnp.einsum('bcjh,bcjhp,bcjhn->bchpn', g2c * dec_end, xpc, Kpc)
            chunk_decay = jnp.exp(ell[:, :, -1, :])

            def step(Hprev, inp):
                wc, cd = inp
                return (cd[:, :, None, None] * Hprev + wc, Hprev)
            H0 = jnp.zeros((b, NHEADS, HEADDIM, D_STATE), u.dtype)
            _, Hprevs = jax.lax.scan(step, H0, (jnp.moveaxis(Wsum, 1, 0), jnp.moveaxis(chunk_decay, 1, 0)))
            Hprevs = jnp.moveaxis(Hprevs, 0, 1)
            y_inter = jnp.einsum('bcihn,bcih,bchpn->bcihp', Qc, jnp.exp(ell), Hprevs)
            y = (y_intra + y_inter).reshape(b, L, NHEADS, HEADDIM)
            y = y + D[None, None, :, None] * x
            y = y * jax.nn.silu(z)
            return y.reshape(b, L, D_INNER) @ W_out
        return _forward(u, W_in, W_out, dt_bias, B_bias, C_bias, B_norm_w, C_norm_w, D)

    def _L0_ffn_ref(x, w_router, w_up, b_up, w_down, b_down):
        import jax, jax.numpy as jnp
        import numpy as np
        K = 2
        logits = jnp.einsum('bsd,ed->bse', x, w_router)
        top_logits, idx = jax.lax.top_k(logits, K)
        router_weights = jax.nn.softmax(top_logits, axis=-1)
        h = jnp.einsum('eud,bsd->bseu', w_up, x) + b_up[None, None]
        h = jax.nn.gelu(h, approximate=False)
        y = jnp.einsum('edu,bseu->bsed', w_down, h) + b_down[None, None]
        y_k = jnp.take_along_axis(y, idx[..., None], axis=2)
        out = jnp.einsum('bskd,bsk->bsd', y_k, router_weights)
        return out
    x = L0_attn_u
    xn = _layernorm(x, axis=-1)
    x = x + _L0_attn_ref(xn, L0_attn_W_in, L0_attn_W_out, L0_attn_dt_bias, L0_attn_B_bias, L0_attn_C_bias, L0_attn_B_norm_w, L0_attn_C_norm_w, L0_attn_D) + _L0_ffn_ref(xn, L0_ffn_w_router, L0_ffn_w_up, L0_ffn_b_up, L0_ffn_w_down, L0_ffn_b_down)
    return x

_drawn_inputs = setup_inputs


def setup_inputs(seed=0):
    import zlib

    import numpy as np

    out = dict(_drawn_inputs(seed))
    spreads = {'L0_attn_B_bias': (1.0, 0.6),
     'L0_attn_C_bias': (1.0, 0.6),
     'L0_attn_B_norm_w': (1.0, 0.6),
     'L0_attn_C_norm_w': (1.0, 0.6),
     'L0_attn_D': (1.0, 0.6)}
    factors = {'L0_attn_W_in': 8.0, 'L0_attn_W_out': 8.0, 'L0_attn_dt_bias': 64.0, 'L0_ffn_b_down': 8.0}
    for name, (base, spread) in spreads.items():
        noise = np.random.default_rng([zlib.crc32(name.encode()), seed]).standard_normal(out[name].shape)
        drawn = base * np.exp(spread * noise) if base else spread * noise
        out[name] = jnp.asarray(drawn.astype(out[name].dtype))
    for name, factor in factors.items():
        out[name] = (out[name] * factor).astype(out[name].dtype)
    return out
```

```python
import math
from contextlib import ExitStack

import concourse.bass as bass
from concourse import mybir

ALU = mybir.AluOpType
ACT = mybir.ActivationFunctionType
AX_X = mybir.AxisListType.X
F32 = mybir.dt.float32
F16 = mybir.dt.float16
I32 = mybir.dt.int32

P = 128
B, L, DM = 8, 512, 128
T = B * L // P
TB = L // P
NH, HD = 4, 64
DI = NH * HD
NA = 32
NE = 8
U = 512
UC = U // P
XT = 2 * T + NE
XPAD = XT + 4
BP1 = 4
EPS = 1e-5
A_FLOOR = 1e-4
C_B, C_C, C_UB, C_UC, C_DT, C_A, C_TRAP, C_ANG, C_RT = 0, 128, 256, 260, 264, 268, 272, 276, 308
NP1 = C_RT + NE
NP2 = 2 * DI
TWO_PI_HI = 6.28125
TWO_PI_LO = 2 * math.pi - TWO_PI_HI
NEVER = -1e30
R_DIFF, R_CHOSEN, R_ALL = 12, 13, 35
ROUND = 1.5 * 2.0 ** 23


def build(nc, x, w_in, cols, rows, w_out, w_up, b_up, w_dn, b_dn, out):
    xv = x.rearrange("(b t p) d -> b p t d", t=TB, p=P)
    ov = out.rearrange("(b t p) d -> b p t d", t=TB, p=P)
    ell_dram = nc.dram_tensor("ell_rows", ((T + TB) * NH, P), F32, kind="Internal").ap()
    xg_dram = nc.dram_tensor("rows_by_expert", (XPAD * P, P), F32, kind="Internal").ap()
    yg_dram = nc.dram_tensor("results_by_expert", (XT * P, P), F32, kind="Internal").ap()

    with ExitStack() as ctx:
        def sb(name, shape, dt=F32):
            return ctx.enter_context(nc.sbuf_tensor(name, shape, dt))

        def sem(name):
            return ctx.enter_context(nc.semaphore(name))

        bank = [ctx.enter_context(nc.psum_tensor(f"bank{n}", [P, 512], F32)) for n in range(8)]

        ident = sb("ident", [P, P])
        upper = sb("upper", [P, P])
        ones = sb("ones", [P, P])
        shift = sb("shift", [P, P])
        wrap = sb("wrap", [P, P])
        zero4 = sb("zero4", [TB * NH, P])
        before = sb("before", [P, P])
        tile_row = sb("tile_row", [P, XPAD])
        full_row = sb("full_row", [P, T])
        first_row = sb("first_row", [P, NE])
        rt_m1, rt_m2, rt_k = (sb(n, [P, T]) for n in ("rt_m1", "rt_m2", "rt_k"))
        rt_tiles, rt_end, rt_start = (sb(n, [P, NE]) for n in ("rt_tiles", "rt_end", "rt_start"))
        gate = sb("gate", [P, 2, T])
        slot = sb("slot", [P, T, 2])
        tile_expert = sb("tile_expert", [P, XPAD], I32)
        tile_bias = sb("tile_bias", [P, XPAD], I32)
        wf = sb("wf", [P, NP1 + NP2])
        wh = sb("wh", [P, NP1 + NP2], F16)
        wl = sb("wl", [P, NP1 + NP2], F16)
        colp = sb("colp", [P, 2 * P + 2 + 2 * NH])
        NROW = 2 * P + 2 * NH * P + NH + NH
        rowp = sb("rowp", [P, NROW])
        wo = sb("wo", [P, 2, P])
        wbt, wct = colp[:, 0:P], colp[:, P:2 * P]
        wn_b, wn_c = colp[:, 256:257], colp[:, 257:258]
        bb_t, cb_t = colp[:, 258:262], colp[:, 262:266]
        nw_b, nw_c = rowp[:, 0:P], rowp[:, P:2 * P]
        kq_bias = rowp[:, 256:1280]
        dtb_r, d_r = rowp[:, 1280:1284], rowp[:, 1284:1288]
        nw_bc = sb("nw_bc", [P, P])
        bias8 = sb("bias8", [P, 2 * NH])
        cross = sb("cross", [P, 3 * NH])
        kappa = sb("kappa", [P, NH])
        x_all = sb("x_all", [P, T * P])
        xh = sb("xh", [P, (T + 1) * P], F16)
        xl = sb("xl", [P, (T + 1) * P], F16)
        proj = sb("proj", [P, (T + 1) * NP1])
        cs = sb("cs", [P, (T + 1) * 2 * P])
        ao_view = cs[:, 0:T * 2 * P].rearrange("p (t c) -> p t c", c=2 * P)
        stats = sb("stats", [P, T * 6])
        mean, ve, rstd, nmr, ln_t = (sb(n, [P, T]) for n in ("mean", "ve", "rstd", "nmr", "ln_t"))
        ss = sb("ss", [P, 2, T + 1])
        bc0 = sb("bc0", [P, T])
        r_bc = sb("r_bc", [P, 2, T + 1])
        r_t = sb("r_t", [P, 2, T + 1])
        TH = T * NH
        dt_all, adt, beta, omega, gg = (sb(n, [P, TH + NH]) for n in ("dt_all", "adt", "beta", "omega", "gg"))
        ell, expell, ge, coef, cd, nell = (sb(n, [P, TH + NH]) for n in ("ell", "expell", "ge", "coef", "cd", "nell"))
        dece, u1, u2 = (sb(n, [P, TH]) for n in ("dece", "u1", "u2"))
        ellt = sb("ellt", [P, P])
        bu = sb("bu", [P, NE * UC])
        bds = sb("bds", [33, NE * P])
        sel = sb("sel", [P, P], F16)
        sx = sb("sx", [P, 2, 2 * P])
        sidx = sb("sidx", [P, 2, 4], I32)
        junk = sb("junk", [P, 2, P])
        bcn = sb("bcn", [P, 2 * P])
        kq = sb("kq", [P, 2, 2 * NH * P])
        rp = sb("rp", [P, 4, 2 * NH * NA])
        kqt = sb("kqt", [P, 2, NH * P])
        el = sb("el", [P, TB, NH * P])
        ee = sb("ee", [P, 2, NH * P])
        ang, th, tk, ta = (kq[:, k // 2, (k % 2) * 512:(k % 2 + 1) * 512] for k in range(4))
        xn, bw = (ee[:, k, :].rearrange("p (t n) -> p t n", t=TB) for k in range(2))
        v8, e8, s8, q8 = (el[:, k, 0:T * 2 * NH].rearrange("p (t n) -> p t n", t=T) for k in range(4))
        p8 = el[:, 0, 256:512].rearrange("p (t n) -> p t n", t=T)
        em = sb("em", [P, 2, NH * P])
        mm = sb("mm", [P, NH * P])
        zt = sb("zt", [P, DI])
        xs_raw = sb("xs_raw", [P, 2, DI])
        sz = sb("sz", [P, 2, DI])
        xg = sb("xg", [P, 2, DI])
        xw = sb("xw", [P, 2, DI])
        xc = sb("xc", [P, 2, DI])
        st = sb("st", [P, 2, DI])
        std = sb("std", [P, DI])
        zeros = cs[:, 0:4 * P]
        stage = [rp[:, :, :].rearrange("p a n -> p (a n)"), kq[:, 1, :]]
        xback = [a.rearrange("p (t d) -> p t d", t=TB) for a in (kq[:, 0, 0:512], kq[:, 0, 512:1024], kq[:, 1, 0:512], kq[:, 1, 512:1024],
                                                                 el[:, 0, :], el[:, 1, :], el[:, 2, :], el[:, 3, :])]
        x16, p16 = x_all[:, :].bitcast(F16), proj[:, :].bitcast(F16)
        NU = NE * U
        wu_h, wu_l = x16[:, 0:NU], x16[:, NU:2 * NU]
        wd_h, wd_l = p16[:, 0:NU], p16[:, NU:2 * NU]
        bd = p16[:, 2 * NU:2 * NU + NE * P]
        assert (2 * NU + NE * P) * 2 <= BP1 * TB * NP1 * 4 and 4 * NU <= T * P * 4
        xgb = rp[:, :, :].rearrange("p a (b n) -> p (a b) n", n=P)
        xgt = sb("xgt", [P, 2, 2, P], F16)
        hf = sb("hf", [P, 2, U])
        hh = sb("hh", [P, 2, 2, U], F16)
        yb = kq[:, 1, :].rearrange("p (b n) -> p b n", n=P)
        gb = [hf[:, q, :].rearrange("p (t k n) -> p t k n", t=2, k=2) for q in range(2)]
        y1, y2, y3, yg = (sb(n, [P, DI]) for n in ("y1", "y2", "y3", "yg"))
        ygt = sb("ygt", [P, DI])

        S = {n: sem(n) for n in (
            "x_in", "wf_in", "cols_in", "rows_in", "wo_in", "const_zero", "const_made", "pads",
            "cross_made", "kappa_in", "cross_mm", "cross_copied", "w_hi", "w_lo", "wo_half", "nwbc", "b8",
            "stats_done", "ln_chain", "ln_sqrt", "xn_made", "xn_t", "xh_made", "xl_made",
            "proj_mm", "proj_out", "sq_done", "bw1", "bw2", "bc0_done",
            "small", "small_act", "om_shift", "ell_mm", "ellt_mm", "ellt_sb", "ell_out", "pad_out",
            "r_sqrt", "ang_made", "theta_mm", "red1", "red2", "red3", "red4", "sin_made", "abs_made", "cos_made",
            "zx_mm", "z_tanh", "x_copied", "sz_made", "xg_made", "xw_made", "xc_made",
            "b_norm", "c_norm", "kq_biased", "rotated", "kq_first", "kq_ready",
            "kq_tr", "kt_copied", "qt_copied", "s_mm", "e_exp", "e_masked", "m_made",
            "inter_mm", "w_mm", "intra_mm", "st_decayed", "st_made", "y_a", "y_b", "y_c", "y_gated",
            "yt_mm", "yt_copied", "out_mm", "out_copied", "out_sum", "stored", "iotas", "route", "rt_mask", "rt_mm", "rt_exp", "xg_zeroed", "zeros", "staged", "xg_in0", "xg_in1",
            "w_raw0", "w_raw1", "wx_hi", "wx_lo", "bd_in", "bd_made", "bu_in", "x_t", "xg_hi", "xg_lo", "up_mm", "gelu", "h_hi", "h_lo",
            "down_mm", "y_copied", "y_out0", "y_out1", "idx_made", "combine1", "combine2", "x_again", "moe_sum", "sent")}
        scat = [sem(f"scat{n}") for n in range(2)]
        gath = [sem(f"gath{n}") for n in range(2)]
        el_in = [sem(f"el_in{n}") for n in range(TB)]

        block = ctx.enter_context(nc.Block())

        def tok(ap, n):
            return ap.unsqueeze(2).to_broadcast([P, NH, n])

        def heads(ap):
            return ap.rearrange("p (h n) -> p h n", h=NH)

        @block.sync
        def _(sp):
            sp.dma_start(wf[:, 0:2 * P], w_in[:, 0:2 * P]).then_inc(S["wf_in"], 16)
            sp.dma_start(wf[:, C_DT:], w_in[:, 2 * P:]).then_inc(S["wf_in"], 16)
            for b in range(B):
                sp.dma_start(x_all[:, b * 512:(b + 1) * 512].rearrange("p (t d) -> p t d", t=TB), xv[b]).then_inc(S["x_in"], 16)
            sp.wait_ge(S["zeros"], 1)
            sp.dma_start(xg_dram.rearrange("(c p r) d -> p c (r d)", p=P, r=4), zeros.unsqueeze(1).to_broadcast([P, XPAD // 4, 4 * P])
                         ).then_inc(S["xg_zeroed"], 16)
            sp.wait_ge(S["pads"], 1)
            sp.dma_start(ell_dram[TH:TH + TB * NH, :], zero4[:, :]).then_inc(S["pad_out"], 16)
            sp.wait_ge(S["ellt_sb"], 1)
            sp.dma_start(ell_dram[0:TH, :], ellt[:, :]).then_inc(S["ell_out"], 16)
            sp.wait_ge(S["ell_out"], 16)
            sp.wait_ge(S["pad_out"], 16)
            ell_t = ell_dram.rearrange("(t h) p -> t (h p)", h=NH)
            for j in range(TB):
                sp.dma_start(el[:, j, :], ell_t[j, :].partition_broadcast(P)).then_inc(el_in[j], 16)
            def prefetch(first, last):
                with sp.Fori(first, last) as i:
                    for j in range(TB):
                        sp.wait_ge(S["e_masked"], i * TB + (j + 1))
                        sp.dma_start(el[:, j, :], ell_t[bass.ds(i * TB + (TB + j), 1), :].rearrange("o n -> (o n)").partition_broadcast(P)
                                     ).then_inc(el_in[j], 16)

            prefetch(0, BP1)
            for n in range(2 * TB):
                src = w_up if n < TB else w_dn
                if n < 2:
                    sp.wait_ge(S["intra_mm"], BP1 * TB + 1)
                    sp.wait_ge(S["kq_ready"], BP1 * TB + 1)
                else:
                    sp.wait_ge(S["wx_lo"], n - 1)
                sp.dma_start(stage[n % 2], src[:, (n % TB) * 1024:(n % TB + 1) * 1024]).then_inc(S[f"w_raw{n % 2}"], 16)
            ygv = yg_dram.rearrange("(g t p) d -> g p t d", t=4, p=P)
            xgv = xg_dram.rearrange("(g t p) d -> g p t d", t=4, p=P)
            sp.wait_ge(S["sent"], BP1 * TB + 2)
            sp.wait_ge(S["wx_lo"], 2 * TB)
            sp.dma_start(xgb[:, 0:4, :], xgv[0]).then_inc(S["xg_in0"], 16)
            with sp.Fori(0, XT // 8) as i:
                sp.wait_ge(S["x_t"], i * 8 + 1)
                sp.dma_start(xgb[:, 4:8, :], xgv[bass.ds(i * 2 + 1, 1)].rearrange("o p t d -> (o p) t d")).then_inc(S["xg_in1"], 16)
                sp.wait_ge(S["x_t"], i * 8 + 5)
                sp.dma_start(xgb[:, 0:4, :], xgv[bass.ds(i * 2 + 2, 1)].rearrange("o p t d -> (o p) t d")).then_inc(S["xg_in0"], 16)
                for g in range(2):
                    sp.wait_ge(S["y_copied"], i * 8 + (4 * g + 4 + 2))
                    sp.dma_start(ygv[bass.ds(i * 2 + g, 1)].rearrange("o p t d -> (o p) t d"), yb[:, 4 * g:4 * g + 4, :]).then_inc(S[f"y_out{g}"], 16)
            prefetch(BP1, B)
            for b in range(B):
                if b == 0:
                    sp.wait_ge(S["out_copied"], T + 1)
                    sp.wait_ge(S["s_mm"], T + 1)
                    sp.wait_ge(S["e_masked"], T + 1)
                    for j in range(TB):
                        sp.wait_ge(el_in[j], 16 * (B + 1))
                sp.dma_start(xback[b], xv[b]).then_inc(S["x_again"], 16)
            with sp.Fori(0, B) as i:
                sp.wait_ge(S["out_sum"], i + 1)
                sp.dma_start(ov[bass.ds(i, 1)].rearrange("o p t d -> (o p) t d"),
                             ao_view[:, bass.ds(i * TB, TB), 0:P]).then_inc(S["stored"], 16)
            sp.wait_ge(S["stored"], 16 * B)

        @block.gpsimd
        def _(pool):
            pl = nc.gpsimd
            for name in ("xc_made", "y_out0", "y_out1"):
                pool.sem_inc(S[name], 1)
            for name in ("x_t", "h_lo", "down_mm", "gelu"):
                pool.sem_inc(S[name], 1)
            pool.sem_inc(S["y_copied"], 2)
            pool.sem_inc(S["combine2"], 3)
            pool.sem_inc(S["sent"], 2)
            pl.memset(ident[:, :], 0.0).then_inc(S["const_zero"], 1)
            pl.memset(upper[:, :], 1.0).then_inc(S["const_zero"], 1)
            pl.memset(shift[:, :], 0.0).then_inc(S["const_zero"], 1)
            pl.memset(wrap[:, :], 0.0).then_inc(S["const_zero"], 1)
            pl.memset(ones[:, :], 1.0).then_inc(S["const_zero"], 1)
            pool.wait_ge(S["const_zero"], 5)
            pl.affine_select(out=ident[:, :], in_=ident[:, :], compare_op=ALU.not_equal, fill=1.0, base=0,
                             pattern=[[-1, P]], channel_multiplier=1).then_inc(S["const_made"], 1)
            pl.affine_select(out=upper[:, :], in_=upper[:, :], compare_op=ALU.is_ge, fill=0.0, base=0,
                             pattern=[[1, P]], channel_multiplier=-1).then_inc(S["const_made"], 1)
            pl.affine_select(out=shift[:, :], in_=shift[:, :], compare_op=ALU.not_equal, fill=1.0, base=-1,
                             pattern=[[-1, P]], channel_multiplier=1).then_inc(S["const_made"], 1)
            pl.affine_select(out=wrap[:, :], in_=wrap[:, :], compare_op=ALU.not_equal, fill=1.0, base=-P * (P - 1),
                             pattern=[[P, P]], channel_multiplier=1).then_inc(S["const_made"], 1)
            pl.memset(zeros, 0.0).then_inc(S["zeros"], 1)
            pl.affine_select(out=before[:, :], in_=ones[:, :], compare_op=ALU.is_gt, fill=0.0, base=0,
                             pattern=[[1, P]], channel_multiplier=-1).then_inc(S["const_made"], 1)
            pl.iota(tile_row[:, :], pattern=[[1, XPAD]], base=0, channel_multiplier=0, allow_small_or_imprecise_dtypes=True).then_inc(S["iotas"], 1)
            pl.iota(full_row[:, :], pattern=[[P, T]], base=0, channel_multiplier=0, allow_small_or_imprecise_dtypes=True).then_inc(S["iotas"], 1)
            pl.iota(first_row[:, :], pattern=[[-1, NE]], base=NE, channel_multiplier=0, allow_small_or_imprecise_dtypes=True).then_inc(S["iotas"], 1)
            pl.memset(sel[:, :], 0.0).then_inc(S["bd_made"], 1)
            pl.memset(bds[:, :], 0.0).then_inc(S["bd_made"], 1)
            pool.wait_ge(S["bd_made"], 2)
            for p in (0, 32):
                pl.memset(sel[p:p + 1, :], 1.0).then_inc(S["bd_made"], 1)
                pool.dma_start(bds[p:p + 1, :], b_dn.rearrange("(o n) -> o n", o=1)).then_inc(S["bd_in"], 16)
            pool.wait_ge(S["bd_made"], 4)
            pl.memset(zero4[:, :], 0.0).then_inc(S["pads"], 1)
            pl.memset(xh[:, T * P:], 0.0).then_inc(S["pads"], 1)
            pl.memset(xl[:, T * P:], 0.0).then_inc(S["pads"], 1)
            pl.memset(proj[:, T * NP1:], 0.0).then_inc(S["pads"], 1)
            pl.memset(cs[:, T * 2 * P:], 0.0).then_inc(S["pads"], 1)
            pl.memset(ss[:, :, T:], 0.0).then_inc(S["pads"], 1)
            for a in (dt_all, omega, gg, expell, ge, coef, cd, nell):
                pl.memset(a[:, TH:], 0.0).then_inc(S["pads"], 1)
            pool.wait_ge(S["nwbc"], 1)
            with pool.Fori(0, B) as i:
                pool.wait_ge(S["proj_out"], i * TB + TB)
                pv = proj[:, bass.ds(i * (TB * NP1), TB * NP1)].rearrange("p (t n) -> p t n", t=TB)
                pool.wait_ge(S["bc0_done"], i + 1)
                pl.tensor_tensor(bw[:, :, :], pv[:, :, C_B:C_B + P], nw_bc[:, :].unsqueeze(1).to_broadcast([P, TB, P]), ALU.mult).then_inc(S["bw1"], 1)
                pool.wait_ge(S["bw1"], i + 1)
                pl.tensor_tensor(bw[:, :, :], bw[:, :, :], pv[:, :, C_C:C_C + P], ALU.mult).then_inc(S["bw2"], 1)

            pool.wait_ge(S["small"], 40)
            pool.wait_ge(el_in[0], 16)
            pl.affine_select(out=heads(ee[:, 0, :]), in_=heads(el[:, 0, :]), compare_op=ALU.is_gt,
                             fill=NEVER, base=0, pattern=[[0, NH], [1, P]], channel_multiplier=-1).then_inc(S["e_masked"], 1)

            def recurrence(first, last, moves):
                with pool.Fori(first, last) as i:
                    for j in range(TB):
                        n = i * TB + j
                        pool.wait_ge(S["e_exp"], n + 1)
                        pool.wait_ge(el_in[(j + 1) % TB], (i + (1 if j < TB - 1 else 2)) * 16)
                        moves(i, j, True)
                        pool.wait_ge(S["x_copied"], i * TB + (j + 1) + 1)
                        pl.tensor_tensor(heads(xc[:, j % 2, :]), heads(xs_raw[:, j % 2, :]), tok(coef[:, bass.ds(i * (TB * NH) + j * NH, NH)], HD), ALU.mult
                                         ).then_inc(S["xc_made"], 1)
                        pl.affine_select(out=heads(ee[:, (j + 1) % 2, :]), in_=heads(el[:, (j + 1) % TB, :]), compare_op=ALU.is_gt,
                                         fill=NEVER, base=0, pattern=[[0, NH], [1, P]], channel_multiplier=-1).then_inc(S["e_masked"], 1)
                        moves(i, j, False)
                        if j in (1, 2):
                            pool.wait_ge(S["st_made"], i * 3 + j + 1)
                            pl.tensor_tensor(heads(std[:, :]), heads(st[:, (j - 1) % 2, :]), tok(cd[:, bass.ds(i * (TB * NH) + j * NH, NH)], HD), ALU.mult
                                             ).then_inc(S["st_decayed"], 1)

            def send(i, j, ready):
                def arrived(k):
                    pool.wait_ge(scat[k % 2], i * 128 + 64 * (k // 2 + 1))
                    pool.sem_inc(S["sent"], 1)

                if ready:
                    if j:
                        arrived(j - 1)
                    pool.wait_ge(S["staged"], 3 * (i * TB + (j + 1)))
                else:
                    for t in range(2):
                        for k in range(2):
                            pool.indirect_dma_start(xg_dram, bass.IndirectOffsetOnAxis(ap=sidx[:, j % 2, 2 * t + k:2 * t + k + 1], axis=0),
                                                    sx[:, j % 2, t * P:(t + 1) * P], None).then_inc(scat[j % 2], 16)
                    if j == TB - 1:
                        arrived(j)

            def fetch(i, j, ready):
                n = (i - BP1) * TB + j
                if ready:
                    pool.wait_ge(S["idx_made"], n + 1)
                    pool.wait_ge(S["combine2"], 2 * n + 1)
                else:
                    for t in range(2):
                        for k in range(2):
                            pool.indirect_dma_start(gb[j % 2][:, t, k, :], None, yg_dram,
                                                    bass.IndirectOffsetOnAxis(ap=sidx[:, j % 2, 2 * t + k:2 * t + k + 1], axis=0)).then_inc(gath[j % 2], 16)

            pool.wait_ge(S["xg_zeroed"], 16)
            recurrence(0, BP1, send)
            for g in range(2):
                pool.wait_ge(S[f"y_out{g}"], 16 * (XT // 8) + 1)
            recurrence(BP1, B, fetch)
            pool.wait_ge(S["x_again"], 16 * B)
            for b in range(B):
                at = ao_view[:, b * TB:(b + 1) * TB, 0:P]
                pool.wait_ge(S["moe_sum"], b + 1)
                pl.tensor_tensor(at, at, xback[b], ALU.add).then_inc(S["out_sum"], 1)

        @block.scalar
        def _(act):
            sc = nc.scalar
            for name in ("sq_done", "cos_made", "sin_made", "abs_made", "e_exp", "out_copied", "x_copied"):
                act.sem_inc(S[name], 1)
            act.dma_start(colp[:, :], cols).then_inc(S["cols_in"], 16)
            act.dma_start(rowp[:, :], rows.partition_broadcast(P)).then_inc(S["rows_in"], 16)
            act.dma_start(wo[:, :, :], w_out.rearrange("(c p) d -> p c d", p=P)).then_inc(S["wo_in"], 16)
            act.dma_start(bu[:, :], b_up).then_inc(S["bu_in"], 16)
            act.wait_ge(S["cross_mm"], 1)
            sc.copy(wf[:, C_UB:C_DT], bank[0][:, 0:2 * NH]).then_inc(S["cross_copied"], 1)
            sc.copy(kappa[:, :], bank[1][:, 0:NH]).then_inc(S["cross_copied"], 1)
            act.wait_ge(S["ln_chain"], 6)
            sc.activation(ln_t[:, :], ve[:, :], ACT.Sqrt).then_inc(S["ln_sqrt"], 1)

            def high(i, j):
                act.wait_ge(S["xn_t"], i * TB + (j + 1))
                sc.copy(xh[:, bass.ds(i * 512 + j * P, P)], bank[j % 2][:, 0:P]).then_inc(S["xh_made"], 1)

            def project_out(i, j):
                act.wait_ge(S["proj_mm"], i * TB + (j + 1))
                ps = bank[2 + j % 2]
                sc.copy(proj[:, bass.ds(i * (TB * NP1) + j * NP1, NP1)], ps[:, 0:NP1]).then_inc(S["proj_out"], 1)
                act.wait_ge(S["sq_done"], 2 * (i * TB + j) + 1)
                for c in range(2):
                    sc.activation(junk[:, c, :], ps[:, c * P:(c + 1) * P], ACT.Square,
                                  accum_out=ss[:, c, bass.ds(i * TB + j, 1)]).then_inc(S["sq_done"], 1)

            with act.Fori(0, B) as i:
                high(i, 0)
                for j in range(1, TB):
                    high(i, j)
                    project_out(i, j - 1)
                project_out(i, TB - 1)

            act.wait_ge(S["small"], 2)
            sc.activation(r_t[:, :, :], ss[:, :, :], ACT.Sqrt).then_inc(S["small_act"], 1)
            act.wait_ge(S["small"], 4)
            sc.activation(e8[:, :, :], q8[:, :, :], ACT.Exp).then_inc(S["small_act"], 1)
            pr = proj[:, 0:T * NP1].rearrange("p (t n) -> p t n", t=T)
            trap = pr[:, :, C_TRAP:C_TRAP + NH]
            sc.activation(beta[:, 0:TH].rearrange("p (t h) -> p t h", h=NH), trap, ACT.Exp, scale=-1.0).then_inc(S["small_act"], 1)
            sc.activation(omega[:, 0:TH].rearrange("p (t h) -> p t h", h=NH), trap, ACT.Exp).then_inc(S["small_act"], 1)
            act.wait_ge(S["ell_mm"], 1)
            sc.copy(ell[:, 0:TH], bank[5][:, 0:TH]).then_inc(S["small_act"], 1)
            sc.activation(expell[:, 0:TH], bank[5][:, 0:TH], ACT.Exp).then_inc(S["small_act"], 1)
            sc.mul(nell[:, 0:TH], bank[5][:, 0:TH], -1.0).then_inc(S["small_act"], 1)
            sc.activation(cd[:, 0:TH], bank[6][:, 0:TH], ACT.Exp).then_inc(S["small_act"], 1)
            act.wait_ge(S["ellt_mm"], 1)
            sc.copy(ellt[:, :], bank[7][:, 0:P]).then_inc(S["ellt_sb"], 1)
            act.wait_ge(S["small"], 25)
            sc.activation(dece[:, :], dece[:, :], ACT.Exp).then_inc(S["small_act"], 1)

            act.wait_ge(S["route"], R_DIFF)
            sc.activation(rt_m2[:, :], rt_m2[:, :], ACT.Exp).then_inc(S["rt_exp"], 1)

            act.wait_ge(S["xg_zeroed"], 16)
            with act.Fori(0, B) as i:
                act.wait_ge(S["red4"], i + 1 + 1)
                cv = cs[:, bass.ds(i * (TB * 2 * P), TB * 2 * P)].rearrange("p (t c n) -> p t c n", t=TB, c=2)
                tv = th[:, :].rearrange("p (t n) -> p t n", t=TB)
                sc.activation(cv[:, :, 1, :], tv, ACT.Sin).then_inc(S["sin_made"], 1)
                act.wait_ge(S["cos_made"], i + 1)
                sc.activation(ta[:, :], th[:, :], ACT.Abs).then_inc(S["abs_made"], 1)
                act.wait_ge(S["abs_made"], i + 1 + 1)
                sc.activation(cv[:, :, 0, :], ta[:, :].rearrange("p (t n) -> p t n", t=TB), ACT.Sin, bias=math.pi / 2, scale=-1.0).then_inc(S["cos_made"], 1)

            def exps(par, col):
                for h in range(NH):
                    e = sc.activation(em[:, par, h * P:(h + 1) * P], ee[:, par, h * P:(h + 1) * P], ACT.Exp, bias=nell[:, col(h)])
                e.then_inc(S["e_exp"], 1)

            def zx_out(par, n):
                act.wait_ge(S["zx_mm"], n + 1)
                ps = bank[par]
                sc.activation(zt[:, :], ps[:, 0:DI], ACT.Tanh, scale=0.5).then_inc(S["z_tanh"], 1)
                sc.copy(xs_raw[:, par, :], ps[:, DI:2 * DI]).then_inc(S["x_copied"], 1)

            def kq_out(n):
                act.wait_ge(S["kq_tr"], n + 1)
                sc.copy(kqt[:, 0, :], bank[2][:, :]).then_inc(S["kt_copied"], 1)
                sc.copy(kqt[:, 1, :], bank[3][:, :]).then_inc(S["qt_copied"], 1)

            act.wait_ge(S["e_masked"], 1)
            act.wait_ge(S["route"], R_ALL)
            exps(0, lambda h: slice(h, h + 1))
            zx_out(0, 0)
            kq_out(0)
            def recurrence(first, last, moves):
              with act.Fori(first, last) as i:
                for j in range(TB):
                    moves(i, j)
                    t, nxt = i * TB + j, i * TB + (j + 1)
                    act.wait_ge(S["e_masked"], i * TB + (j + 2))
                    act.wait_ge(S["m_made"], t + 1)
                    exps((j + 1) % 2, lambda h: bass.ds(i * (TB * NH) + ((j + 1) * NH + h), 1))
                    act.wait_ge(S["sz_made"], nxt + 1)
                    act.wait_ge(S["xg_made"], t + 1)
                    act.wait_ge(S["xw_made"], t + 1)
                    act.wait_ge(S["xc_made"], t + 1)
                    zx_out((j + 1) % 2, nxt)
                    act.wait_ge(S["s_mm"], nxt)
                    kq_out(nxt)
                    act.wait_ge(S["yt_mm"], nxt + 1)
                    sc.copy(ygt[:, :], bank[7][:, 0:DI]).then_inc(S["yt_copied"], 1)
                    act.wait_ge(S["out_mm"], nxt)
                    sc.copy(cs[:, bass.ds(i * (TB * 2 * P) + j * 2 * P, P)], bank[7][:, DI:DI + P]).then_inc(S["out_copied"], 1)

            def stage_rows(i, j):
                act.wait_ge(S["sent"], i * TB + (j + 1))
                for t in range(2):
                    n = i * 8 + (2 * j + t)
                    sc.activation(sx[:, j % 2, t * P:(t + 1) * P], x_all[:, bass.ds(n * P, P)], ACT.Identity,
                                  bias=nmr[:, bass.ds(n, 1)], scale=rstd[:, bass.ds(n, 1)]).then_inc(S["staged"], 1)
                sc.copy(sidx[:, j % 2, :], slot[:, :, :].rearrange("p t k -> p (t k)")[:, bass.ds(i * 16 + j * 4, 4)]).then_inc(S["staged"], 1)

            def stage_places(i, j):
                i = i - BP1
                act.wait_ge(S["combine2"], i * 8 + (2 * j + 1))
                sc.copy(sidx[:, j % 2, :], slot[:, :, :].rearrange("p t k -> p (t k)")[:, bass.ds(i * 16 + j * 4, 4)]).then_inc(S["idx_made"], 1)

            recurrence(0, BP1, stage_rows)

            act.wait_ge(S["sent"], BP1 * TB + 2)
            for n in range(2 * TB):
                act.wait_ge(S[f"w_raw{n % 2}"], 16 * (n // 2 + 1))
                sc.copy((wu_h if n < TB else wd_h)[:, (n % TB) * 1024:(n % TB + 1) * 1024], stage[n % 2]).then_inc(S["wx_hi"], 1)

            def high_rows(bank_x, par, n):
                act.wait_ge(S["x_t"], n + 2)
                sc.copy(xgt[:, par, 0, :], bank_x[:, 0:P]).then_inc(S["xg_hi"], 1)

            def gelus(par, n, at, first=False):
                b = act.value_load(tile_bias[0:1, at], min_val=0, max_val=(NE - 1) * UC)
                act.wait_ge(S["up_mm"], n + 1)
                if not first:
                    act.wait_ge(S["h_lo"], n)
                for c in range(UC):
                    g = sc.activation(hf[:, par, c * P:(c + 1) * P], bank[2 + par][:, c * P:(c + 1) * P], ACT.Gelu, bias=bu[:, bass.ds(b + c, 1)])
                g.then_inc(S["gelu"], 1)

            act.wait_ge(S["bu_in"], 16)
            high_rows(bank[1], 0, 0)
            high_rows(bank[1], 1, 1)
            gelus(0, 0, slice(0, 1), True)
            with act.Fori(0, XT // 8) as i:
                for k in range(8):
                    n = i * 8 + k
                    high_rows(bank[1], k % 2, i * 8 + (k + 2))
                    gelus((k + 1) % 2, i * 8 + (k + 1), bass.ds(i * 8 + (k + 1), 1))
            recurrence(BP1, B, stage_places)

        @block.vector
        def _(dve):
            v = nc.vector
            for name in ("bc0_done", "red4", "m_made", "y_b", "st_made", "sz_made", "xg_made", "xw_made", "xl_made"):
                dve.sem_inc(S[name], 1)
            dve.wait_ge(S["cols_in"], 16)
            v.tensor_scalar(cross[:, 0:NH], cb_t, wn_b, None, ALU.mult).then_inc(S["cross_made"], 1)
            v.tensor_scalar(cross[:, NH:2 * NH], bb_t, wn_c, None, ALU.mult).then_inc(S["cross_made"], 1)
            v.tensor_tensor(cross[:, 2 * NH:], bb_t, cb_t, ALU.mult).then_inc(S["cross_made"], 1)
            dve.wait_ge(S["wf_in"], 32)
            dve.wait_ge(S["cross_copied"], 1)
            v.tensor_copy(wh[:, :], wf[:, :]).then_inc(S["w_hi"], 1)
            dve.wait_ge(S["w_hi"], 1)
            v.tensor_tensor(wl[:, :], wf[:, :], wh[:, :], ALU.subtract).then_inc(S["w_lo"], 1)
            dve.wait_ge(S["rows_in"], 16)
            v.tensor_tensor(nw_bc[:, :], nw_b, nw_c, ALU.mult).then_inc(S["nwbc"], 1)
            v.memset(bias8[:, NH:], 0.0).then_inc(S["b8"], 1)
            v.tensor_copy(bias8[:, 0:NH], dtb_r).then_inc(S["b8"], 1)
            dve.wait_ge(S["wo_in"], 16)
            v.tensor_scalar(wo[:, :, :], wo[:, :, :], 0.5, None, ALU.mult).then_inc(S["wo_half"], 1)

            dve.wait_ge(S["x_in"], 16 * B)
            with dve.Fori(0, B) as i:
                for j in range(TB):
                    v.bn_stats(stats[:, bass.ds(i * 24 + j * 6, 6)], x_all[:, bass.ds(i * 512 + j * P, P)]).then_inc(S["stats_done"], 1)
            dve.wait_ge(S["stats_done"], T)
            sv = stats[:, :].rearrange("p (t s) -> p t s", s=6)
            me, mo, ve2, vo2 = (sv[:, :, k] for k in (1, 4, 2, 5))
            v.tensor_tensor(mean[:, :], me, mo, ALU.add).then_inc(S["ln_chain"], 1)
            v.tensor_tensor(nmr[:, :], me, mo, ALU.subtract).then_inc(S["ln_chain"], 1)
            v.tensor_tensor(ve[:, :], ve2, vo2, ALU.add).then_inc(S["ln_chain"], 1)
            dve.wait_ge(S["ln_chain"], 3)
            v.scalar_tensor_tensor(out=ln_t[:, :], in0=nmr[:, :], scalar=0.25, in1=nmr[:, :], op0=ALU.mult, op1=ALU.mult).then_inc(S["ln_chain"], 1)
            dve.wait_ge(S["ln_chain"], 4)
            v.scalar_tensor_tensor(out=ve[:, :], in0=ve[:, :], scalar=1.0 / DM, in1=ln_t[:, :], op0=ALU.mult, op1=ALU.add).then_inc(S["ln_chain"], 1)
            dve.wait_ge(S["ln_chain"], 5)
            v.tensor_scalar(ve[:, :], ve[:, :], EPS, None, ALU.add).then_inc(S["ln_chain"], 1)
            dve.wait_ge(S["ln_sqrt"], 1)
            v.reciprocal(rstd[:, :], ln_t[:, :]).then_inc(S["ln_chain"], 1)
            dve.wait_ge(S["ln_chain"], 7)
            v.tensor_tensor(ln_t[:, :], rstd[:, :], rstd[:, :], ALU.mult).then_inc(S["ln_chain"], 1)
            dve.wait_ge(S["ln_chain"], 8)
            v.tensor_tensor(ln_t[:, :], ln_t[:, :], ve[:, :], ALU.mult).then_inc(S["ln_chain"], 1)
            dve.wait_ge(S["ln_chain"], 9)
            v.tensor_scalar(ln_t[:, :], ln_t[:, :], -0.5, 1.5, ALU.mult, ALU.add).then_inc(S["ln_chain"], 1)
            dve.wait_ge(S["ln_chain"], 10)
            v.tensor_tensor(rstd[:, :], rstd[:, :], ln_t[:, :], ALU.mult).then_inc(S["ln_chain"], 1)
            dve.wait_ge(S["ln_chain"], 11)
            v.scalar_tensor_tensor(out=nmr[:, :], in0=mean[:, :], scalar=-0.5, in1=rstd[:, :], op0=ALU.mult, op1=ALU.mult).then_inc(S["ln_chain"], 1)
            dve.wait_ge(S["ln_chain"], 12)

            def normalise(i, j):
                v.tensor_scalar(xn[:, j, :], x_all[:, bass.ds(i * 512 + j * P, P)], rstd[:, bass.ds(i * TB + j, 1)], nmr[:, bass.ds(i * TB + j, 1)],
                                ALU.mult, ALU.add).then_inc(S["xn_made"], 1)

            def low(i, j):
                dve.wait_ge(S["xh_made"], i * TB + (j + 1))
                at = bass.ds(i * 512 + j * P, P)
                v.tensor_tensor(xl[:, at], bank[j % 2][:, 0:P], xh[:, at], ALU.subtract).then_inc(S["xl_made"], 1)

            with dve.Fori(0, B) as i:
                normalise(i, 0)
                for j in range(1, TB):
                    normalise(i, j)
                    low(i, j - 1)
                low(i, TB - 1)
                dve.wait_ge(S["bw2"], i + 1)
                v.tensor_reduce(bc0[:, bass.ds(i * TB, TB)], bw[:, :, :], AX_X, ALU.add).then_inc(S["bc0_done"], 1)

            count = [0]

            def step(ins):
                ins.then_inc(S["small"], 1)
                count[0] += 1
                return count[0]

            def after(n):
                dve.wait_ge(S["small"], n)

            dve.wait_ge(S["pads"], 14)
            dve.wait_ge(S["b8"], 2)
            dve.wait_ge(S["sq_done"], 2 * T + 1)
            pr = proj[:, 0:T * NP1].rearrange("p (t n) -> p t n", t=T)
            n = step(v.tensor_scalar(ss[:, :, :], ss[:, :, :], 1.0 / P, EPS, ALU.mult, ALU.add))
            n = step(v.tensor_tensor(v8[:, :, :], pr[:, :, C_DT:C_DT + 2 * NH], bias8[:, :].unsqueeze(1).to_broadcast([P, T, 2 * NH]), ALU.add))
            after(2)
            n = step(v.scalar_tensor_tensor(out=q8[:, :, :], in0=v8[:, :, :], scalar=-1.0, in1=v8[:, :, :], op0=ALU.mult, op1=ALU.min))
            n = step(v.tensor_scalar(v8[:, :, :], v8[:, :, :], 0.0, None, ALU.max))
            dve.wait_ge(S["small_act"], 1)
            n = step(v.reciprocal(r_bc[:, :, :], r_t[:, :, :]))
            after(n)
            n = step(v.tensor_tensor(r_t[:, :, :], r_bc[:, :, :], r_bc[:, :, :], ALU.mult))
            after(n)
            n = step(v.tensor_tensor(r_t[:, :, :], r_t[:, :, :], ss[:, :, :], ALU.mult))
            after(n)
            n = step(v.tensor_scalar(r_t[:, :, :], r_t[:, :, :], -0.5, 1.5, ALU.mult, ALU.add))
            after(n)
            n = step(v.tensor_tensor(r_bc[:, :, :], r_bc[:, :, :], r_t[:, :, :], ALU.mult))
            dve.wait_ge(S["small_act"], 2)
            n = step(v.tensor_scalar(s8[:, :, :], e8[:, :, :], 2.0, None, ALU.add))
            after(n)
            n = step(v.reciprocal(s8[:, :, :], s8[:, :, :]))
            after(n)
            n = step(v.tensor_tensor(s8[:, :, :], s8[:, :, :], e8[:, :, :], ALU.mult))
            after(n)
            n = step(v.tensor_tensor(e8[:, :, :], s8[:, :, :], s8[:, :, :], ALU.mult))
            after(n)
            n = step(v.tensor_scalar(p8[:, :, :], e8[:, :, :], 1.0 / 15, None, ALU.mult))
            for k in (13, 11, 9, 7, 5, 3):
                after(n)
                n = step(v.scalar_tensor_tensor(out=p8[:, :, :], in0=p8[:, :, :], scalar=1.0 / k, in1=e8[:, :, :], op0=ALU.add, op1=ALU.mult))
            after(n)
            n = step(v.scalar_tensor_tensor(out=p8[:, :, :], in0=p8[:, :, :], scalar=1.0, in1=s8[:, :, :], op0=ALU.add, op1=ALU.mult))
            after(n)
            n = step(v.scalar_tensor_tensor(out=q8[:, :, :], in0=p8[:, :, :], scalar=2.0, in1=v8[:, :, :], op0=ALU.mult, op1=ALU.add))
            after(n)
            dtv = dt_all[:, 0:TH].rearrange("p (t h) -> p t h", h=NH)
            n = step(v.tensor_copy(dtv, q8[:, :, 0:NH]))
            n = step(v.tensor_scalar(q8[:, :, NH:], q8[:, :, NH:], A_FLOOR, -1.0, ALU.max, ALU.mult))
            after(24)
            v.tensor_tensor(adt[:, 0:TH].rearrange("p (t h) -> p t h", h=NH), q8[:, :, NH:], dtv, ALU.mult).then_inc(S["om_shift"], 1)
            dve.wait_ge(S["small_act"], 4)
            v.tensor_scalar(beta[:, 0:TH], beta[:, 0:TH], 1.0, None, ALU.add).then_inc(S["om_shift"], 1)
            v.tensor_scalar(omega[:, 0:TH], omega[:, 0:TH], 1.0, None, ALU.add).then_inc(S["om_shift"], 1)
            dve.wait_ge(S["om_shift"], 3)
            v.reciprocal(beta[:, 0:TH], beta[:, 0:TH]).then_inc(S["om_shift"], 1)
            v.reciprocal(omega[:, 0:TH], omega[:, 0:TH]).then_inc(S["om_shift"], 1)
            dve.wait_ge(S["small_act"], 8)
            n = step(v.tensor_tensor(dece[:, :], bank[6][:, 0:TH], ell[:, 0:TH], ALU.subtract))
            dve.wait_ge(S["ell_mm"], 2)
            n = step(v.tensor_tensor(gg[:, 0:TH], bank[4][:, 0:TH], beta[:, 0:TH], ALU.add))
            after(n)
            n = step(v.tensor_tensor(gg[:, 0:TH], gg[:, 0:TH], dt_all[:, 0:TH], ALU.mult))
            n = step(v.tensor_tensor(beta[:, 0:TH], beta[:, 0:TH], dt_all[:, 0:TH], ALU.mult))
            ub = pr[:, :, C_UB:C_UB + NH]
            uc = pr[:, :, C_UC:C_UC + NH]
            u1v, u2v = (a[:, :].rearrange("p (t h) -> p t h", h=NH) for a in (u1, u2))

            def per_tile(ap):
                return ap.unsqueeze(2).to_broadcast([P, T, NH])

            n = step(v.tensor_tensor(u1v, ub, per_tile(r_bc[:, 0, 0:T]), ALU.mult))
            n = step(v.tensor_tensor(u2v, uc, per_tile(r_bc[:, 1, 0:T]), ALU.mult))
            n = step(v.tensor_tensor(bc0[:, :], bc0[:, :], r_bc[:, 0, 0:T], ALU.mult))
            after(n)
            n = step(v.tensor_tensor(bc0[:, :], bc0[:, :], r_bc[:, 1, 0:T], ALU.mult))
            n = step(v.tensor_tensor(u1[:, :], u1[:, :], u2[:, :], ALU.add))
            after(n)
            n = step(v.tensor_tensor(u1v, u1v, per_tile(bc0[:, :]), ALU.add))
            dve.wait_ge(S["cross_copied"], 2)
            after(n)
            n = step(v.tensor_tensor(u1v, u1v, kappa[:, :].unsqueeze(1).to_broadcast([P, T, NH]), ALU.add))
            after(n)
            n = step(v.tensor_tensor(u1[:, :], u1[:, :], beta[:, 0:TH], ALU.mult))
            after(n)
            n = step(v.tensor_tensor(coef[:, 0:TH].rearrange("p (t h) -> p t h", h=NH), u1v, d_r.unsqueeze(1).to_broadcast([P, T, NH]), ALU.add))
            dve.wait_ge(S["small_act"], 9)
            n = step(v.tensor_tensor(ge[:, 0:TH], gg[:, 0:TH], dece[:, :], ALU.mult))
            after(n)
            n = step(v.memset(ta[:, 0:1], 0.0))
            n = step(v.memset(tk[:, 0:1], 0.0))
            assert n == 40

            lg = pr[:, :, C_RT:C_RT + NE]
            oh1, oh2, lg2, tmp = (em[:, k // 2, (k % 2) * 256:(k % 2 + 1) * 256].rearrange("p (t e) -> p t e", e=NE) for k in range(4))
            chosen = mm[:, 0:T * NE]
            cnt, upto, reset = y1, y2, y3
            rcount = [0]

            def rstep(ins):
                ins.then_inc(S["route"], 1)
                rcount[0] += 1
                dve.wait_ge(S["route"], rcount[0])

            def by_tile(ap):
                return ap.unsqueeze(2).to_broadcast([P, T, NE])

            def by_expert(ap):
                return ap.unsqueeze(1).to_broadcast([P, T, NE])

            def top(logits, m, oh):
                rstep(v.tensor_reduce(m, logits, AX_X, ALU.max))
                rstep(v.tensor_tensor(tmp, logits, by_tile(m), ALU.is_equal))
                rstep(v.tensor_tensor(tmp, tmp, by_expert(first_row[:, :]), ALU.mult))
                rstep(v.tensor_reduce(rt_k[:, :], tmp, AX_X, ALU.max))
                rstep(v.tensor_tensor(oh, by_tile(rt_k[:, :]), by_expert(first_row[:, :]), ALU.is_equal))

            dve.wait_ge(S["iotas"], 3)
            top(lg, rt_m1[:, :], oh1)
            rstep(v.scalar_tensor_tensor(out=lg2, in0=oh1, scalar=NEVER, in1=lg, op0=ALU.mult, op1=ALU.add))
            top(lg2, rt_m2[:, :], oh2)
            rstep(v.tensor_tensor(rt_m2[:, :], rt_m2[:, :], rt_m1[:, :], ALU.subtract))
            assert rcount[0] == R_DIFF
            rstep(v.tensor_tensor(chosen.rearrange("p (t e) -> p t e", e=NE), oh1, oh2, ALU.add))
            assert rcount[0] == R_CHOSEN
            dve.wait_ge(S["rt_exp"], 1)
            rstep(v.tensor_scalar(rt_m1[:, :], rt_m2[:, :], 1.0, None, ALU.add))
            rstep(v.reciprocal(gate[:, 0, :], rt_m1[:, :]))
            rstep(v.tensor_tensor(gate[:, 1, :], gate[:, 0, :], rt_m2[:, :], ALU.mult))
            rstep(v.memset(reset[:, :], 1.0))
            rstep(v.memset(reset[:, 0:T * NE].rearrange("p (e t) -> p e t", e=NE)[:, :, 0:1], 0.0))
            dve.wait_ge(S["rt_mm"], 2)
            et = cnt[:, :].rearrange("p (e t) -> p e t", e=NE)
            rstep(v.tensor_copy(et, bank[3][:, 0:T * NE].rearrange("p (t e) -> p e t", e=NE)))
            rstep(v.tensor_tensor_scan(upto[:, :], reset[:, :], cnt[:, :], 0.0, ALU.mult, ALU.add))
            ut = upto[:, :].rearrange("p (e t) -> p e t", e=NE)
            rstep(v.tensor_tensor(tmp.rearrange("p t e -> p (t e)").rearrange("p (e t) -> p e t", e=NE), ut[:, :, T - 1:T].to_broadcast([P, NE, T]),
                                  full_row[:, :].unsqueeze(1).to_broadcast([P, NE, T]), ALU.is_gt))
            rstep(v.tensor_reduce(rt_tiles[:, :], tmp.rearrange("p t e -> p (t e)").rearrange("p (e t) -> p e t", e=NE), AX_X, ALU.add))
            rstep(v.tensor_tensor_scan(rt_end[:, :], ones[:, 0:NE], rt_tiles[:, :], 0.0, ALU.mult, ALU.add))
            rstep(v.tensor_tensor(rt_start[:, :], rt_end[:, :], rt_tiles[:, :], ALU.subtract))
            te_ = rp[:, :, :].rearrange("p a n -> p (a n)")[:, 0:XPAD * NE].rearrange("p (s e) -> p s e", e=NE)
            rstep(v.tensor_tensor(te_, tile_row[:, :].unsqueeze(2).to_broadcast([P, XPAD, NE]), rt_end[:, :].unsqueeze(1).to_broadcast([P, XPAD, NE]), ALU.is_ge))
            ts_ = rp[:, :, :].rearrange("p a n -> p (a n)")[:, XPAD * NE:XPAD * (NE + 1)]
            rstep(v.tensor_reduce(ts_, te_, AX_X, ALU.add))
            rstep(v.tensor_scalar(tile_expert[:, :], ts_, NE - 1.0, float(U), ALU.min, ALU.mult))
            rstep(v.tensor_scalar(tile_bias[:, :], ts_, NE - 1.0, float(UC), ALU.min, ALU.mult))
            rstep(v.tensor_tensor(cnt[:, :], upto[:, :], cnt[:, :], ALU.subtract))
            rstep(v.scalar_tensor_tensor(out=et, in0=rt_start[:, :].unsqueeze(2).to_broadcast([P, NE, T]), scalar=float(P), in1=et, op0=ALU.mult, op1=ALU.add))
            rstep(v.tensor_tensor(lg2, bank[2][:, 0:T * NE].rearrange("p (t e) -> p t e", e=NE), cnt[:, :].rearrange("p (e t) -> p t e", e=NE), ALU.add))
            for k, oh in enumerate((oh1, oh2)):
                rstep(v.tensor_tensor(tmp, oh, lg2, ALU.mult))
                rstep(v.tensor_reduce(slot[:, :, k], tmp, AX_X, ALU.add))
            assert rcount[0] == R_ALL, rcount

            def angle_steps(i, par):
                pv = proj[:, bass.ds(i * (TB * NP1), TB * NP1)].rearrange("p (t n) -> p t n", t=TB)
                for t in range(TB):
                    a = v.tensor_tensor(ang[:, t * P:(t + 1) * P].rearrange("p (h n) -> p h n", h=NH),
                                        pv[:, t, C_ANG:C_ANG + NA].unsqueeze(1).to_broadcast([P, NH, NA]),
                                        tok(dt_all[:, bass.ds(i * (TB * NH) + t * NH, NH)], NA), ALU.mult)
                a.then_inc(S["ang_made"], 1)

            with dve.Fori(0, B) as i:
                dve.wait_ge(S["theta_mm"], i + 1)
                angle_steps(i, 0)
                dve.wait_ge(S["theta_mm"], i + 1 + 1)
                v.tensor_scalar(tk[:, :], bank[0][:, :], 1.0 / (2 * math.pi), ROUND, ALU.mult, ALU.add).then_inc(S["red1"], 1)
                dve.wait_ge(S["red1"], i + 1)
                v.tensor_scalar(tk[:, :], tk[:, :], ROUND, None, ALU.subtract).then_inc(S["red2"], 1)
                dve.wait_ge(S["red2"], i + 1)
                dve.wait_ge(S["sin_made"], i + 1)
                dve.wait_ge(S["abs_made"], i + 1)
                v.scalar_tensor_tensor(out=th[:, :], in0=tk[:, :], scalar=-TWO_PI_HI, in1=bank[0][:, :], op0=ALU.mult, op1=ALU.add).then_inc(S["red3"], 1)
                dve.wait_ge(S["red3"], 2 * i + 1)
                v.scalar_tensor_tensor(out=th[:, :], in0=tk[:, :], scalar=-TWO_PI_LO, in1=th[:, :], op0=ALU.mult, op1=ALU.add).then_inc(S["red3"], 1)
                dve.wait_ge(S["red3"], 2 * i + 2)
                v.tensor_scalar(th[:, :], th[:, :], math.pi, -math.pi, ALU.min, ALU.max).then_inc(S["red4"], 1)

            def rope(pt, ct, rb, rc, par, n):
                cv = cs[:, ct].rearrange("p (c n) -> p c n", c=2)
                v.scalar_tensor_tensor(out=bcn[:, 0:P], in0=proj[:, pt(C_B)], scalar=rb, in1=nw_b, op0=ALU.mult, op1=ALU.mult).then_inc(S["b_norm"], 1)
                v.scalar_tensor_tensor(out=bcn[:, P:], in0=proj[:, pt(C_C)], scalar=rc, in1=nw_c, op0=ALU.mult, op1=ALU.mult).then_inc(S["c_norm"], 1)
                dve.wait_ge(S["b_norm"], n + 1)
                dve.wait_ge(S["c_norm"], n + 1)
                k4 = kq[:, par, :].rearrange("p (q h n) -> p q h n", q=2, h=NH)
                b4 = kq_bias.rearrange("p (q h n) -> p q h n", q=2, h=NH)
                for q in range(2):
                    s = v.tensor_tensor(k4[:, q], bcn[:, q * P:(q + 1) * P].unsqueeze(1).to_broadcast([P, NH, P]), b4[:, q], ALU.add)
                    s.then_inc(S["kq_biased"], 1)
                dve.wait_ge(S["kq_biased"], 2 * n + 2)
                x1, x2 = k4[:, :, :, 0:NA], k4[:, :, :, NA:2 * NA]
                r = [rp[:, k, :].rearrange("p (q h n) -> p q h n", q=2, h=NH) for k in range(4)]
                c, s = (cv[:, k, :].rearrange("p (h n) -> p h n", h=NH).unsqueeze(1).to_broadcast([P, 2, NH, NA]) for k in range(2))
                v.tensor_tensor(r[0], x1, c, ALU.mult)
                v.tensor_tensor(r[1], x2, s, ALU.mult)
                v.tensor_tensor(r[2], x1, s, ALU.mult)
                v.tensor_tensor(r[3], x2, c, ALU.mult).then_inc(S["rotated"], 1)
                dve.wait_ge(S["rotated"], n + 1)
                v.tensor_tensor(x1, r[0], r[1], ALU.subtract).then_inc(S["kq_first"], 1)
                v.tensor_tensor(x2, r[2], r[3], ALU.add).then_inc(S["kq_ready"], 1)

            dve.wait_ge(S["cos_made"], B + 1)
            rope(lambda c: slice(c, c + P), slice(0, 2 * P), r_bc[:, 0, 0:1], r_bc[:, 1, 0:1], 0, 0)
            def recurrence(first, last, extra):
              with dve.Fori(first, last) as i:
                for j in range(TB):
                    par = j % 2
                    t, nxt = i * TB + j, i * TB + (j + 1)
                    hs = bass.ds(i * (TB * NH) + j * NH, NH)
                    dve.wait_ge(S["z_tanh"], nxt)
                    dve.wait_ge(S["x_copied"], nxt + 1)
                    v.scalar_tensor_tensor(out=sz[:, par, :], in0=zt[:, :], scalar=1.0, in1=bank[par][:, 0:DI], op0=ALU.add, op1=ALU.mult).then_inc(S["sz_made"], 1)
                    xr = heads(xs_raw[:, par, :])
                    v.tensor_tensor(heads(xg[:, par, :]), xr, tok(gg[:, hs], HD), ALU.mult).then_inc(S["xg_made"], 1)
                    v.tensor_tensor(heads(xw[:, par, :]), xr, tok(ge[:, hs], HD), ALU.mult).then_inc(S["xw_made"], 1)
                    dve.wait_ge(S["s_mm"], nxt)
                    dve.wait_ge(S["e_exp"], nxt + 1)
                    dve.wait_ge(S["intra_mm"], t + 1)
                    v.tensor_tensor(mm[:, :], bank[4][:, :], em[:, par, :], ALU.mult).then_inc(S["m_made"], 1)
                    dve.wait_ge(S["w_mm"], i * 3 + min(j, 3) + 1)
                    rope(lambda c: bass.ds(i * (TB * NP1) + ((j + 1) * NP1 + c), P), bass.ds((i * (TB * 2 * P) + (j + 1) * 2 * P), 2 * P),
                         r_bc[:, 0, bass.ds(nxt, 1)], r_bc[:, 1, bass.ds(nxt, 1)], 1 - par, nxt)
                    if j < 3:
                        dve.wait_ge(S["w_mm"], i * 3 + (j + 1) + 1)
                        if j == 0:
                            v.tensor_copy(st[:, 0, :], bank[6][:, 0:DI]).then_inc(S["st_made"], 1)
                        else:
                            dve.wait_ge(S["st_decayed"], i * 2 + j)
                            v.tensor_tensor(st[:, j % 2, :], std[:, :], bank[6][:, 0:DI], ALU.add).then_inc(S["st_made"], 1)
                    dve.wait_ge(S["intra_mm"], nxt + 1)
                    dve.wait_ge(S["xc_made"], nxt + 1)
                    if j == 0:
                        v.tensor_tensor(y2[:, :], bank[5][:, 0:DI], xc[:, par, :], ALU.add).then_inc(S["y_b"], 1)
                    else:
                        v.tensor_tensor(heads(y1[:, :]), heads(bank[5][:, DI:]), tok(expell[:, hs], HD), ALU.mult).then_inc(S["y_a"], 1)
                        v.tensor_tensor(y3[:, :], bank[5][:, 0:DI], xc[:, par, :], ALU.add).then_inc(S["y_c"], 1)
                        dve.wait_ge(S["y_a"], i * 3 + j)
                        dve.wait_ge(S["y_c"], i * 3 + j)
                        v.tensor_tensor(y2[:, :], y1[:, :], y3[:, :], ALU.add).then_inc(S["y_b"], 1)
                    dve.wait_ge(S["y_b"], nxt + 1)
                    dve.wait_ge(S["yt_mm"], t + 1)
                    v.tensor_tensor(yg[:, :], y2[:, :], sz[:, par, :], ALU.mult).then_inc(S["y_gated"], 1)
                    extra(i, j)

            def combine(i, j):
                i = i - BP1
                dve.wait_ge(gath[j % 2], i * 128 + (64 * (j // 2) + 64))
                for t in range(2):
                    at = bass.ds(i * (8 * P) + (2 * j + t) * P, P)
                    v.tensor_scalar(x_all[:, at], gb[j % 2][:, t, 0, :], gate[:, 0, bass.ds(i * 8 + (2 * j + t), 1)], None, ALU.mult).then_inc(S["combine1"], 1)
                for t in range(2):
                    at = bass.ds(i * (8 * P) + (2 * j + t) * P, P)
                    dve.wait_ge(S["combine1"], i * 8 + (2 * j + t + 1))
                    v.scalar_tensor_tensor(out=x_all[:, at], in0=gb[j % 2][:, t, 1, :], scalar=gate[:, 1, bass.ds(i * 8 + (2 * j + t), 1)], in1=x_all[:, at],
                                           op0=ALU.mult, op1=ALU.add).then_inc(S["combine2"], 1)

            recurrence(0, BP1, lambda i, j: None)

            dve.wait_ge(S["bd_in"], 32)
            dve.wait_ge(S["intra_mm"], BP1 * TB + 1)
            dve.wait_ge(S["sent"], BP1 * TB + 2)
            v.memset(bd, 0.0).then_inc(S["bd_made"], 1)
            dve.wait_ge(S["bd_made"], 5)
            v.tensor_copy(bd[0:33, :], bds[:, :]).then_inc(S["bd_made"], 1)
            dve.wait_ge(S["bd_made"], 6)
            v.tensor_tensor(bd[32:33, :], bds[32:33, :], bd[32:33, :], ALU.subtract).then_inc(S["bd_made"], 1)
            for n in range(2 * TB):
                dve.wait_ge(S["wx_hi"], n + 1)
                at = slice((n % TB) * 1024, (n % TB + 1) * 1024)
                v.tensor_tensor((wu_l if n < TB else wd_l)[:, at], stage[n % 2], (wu_h if n < TB else wd_h)[:, at], ALU.subtract).then_inc(S["wx_lo"], 1)

            def low_rows(par, n):
                dve.wait_ge(S["xg_hi"], n + 1)
                v.tensor_tensor(xgt[:, par, 1, :], bank[1][:, 0:P], xgt[:, par, 0, :], ALU.subtract).then_inc(S["xg_lo"], 1)

            def split_hidden(par, n, first=False):
                dve.wait_ge(S["gelu"], n + 2)
                if not first:
                    dve.wait_ge(S["down_mm"], n)
                v.tensor_copy(hh[:, par, 0, :], hf[:, par, :]).then_inc(S["h_hi"], 1)
                dve.wait_ge(S["h_hi"], n + 1)
                v.tensor_tensor(hh[:, par, 1, :], hf[:, par, :], hh[:, par, 0, :], ALU.subtract).then_inc(S["h_lo"], 1)

            def results(k, n, groups):
                dve.wait_ge(S["down_mm"], n + 2)
                v.tensor_copy(yb[:, k, :], bank[5 + k % 2][:, 0:P]).then_inc(S["y_copied"], 1)

            low_rows(0, 0)
            low_rows(1, 1)
            split_hidden(0, 0, True)
            with dve.Fori(0, XT // 8) as i:
                for k in range(8):
                    if k % 4 == 0:
                        dve.wait_ge(S[f"y_out{k // 4}"], i * 16 + 1)
                    low_rows(k % 2, i * 8 + (k + 2))
                    split_hidden((k + 1) % 2, i * 8 + (k + 1))
                    results(k, i * 8 + k, i)
            for g in range(2):
                dve.wait_ge(S[f"y_out{g}"], 16 * (XT // 8) + 1)
            recurrence(BP1, B, combine)
            for b in range(B):
                at = ao_view[:, b * TB:(b + 1) * TB, 0:P]
                dve.wait_ge(S["out_copied"], T + 1)
                dve.wait_ge(S["combine2"], T + 3)
                v.tensor_tensor(at, at, x_all[:, b * 512:(b + 1) * 512].rearrange("p (t n) -> p t n", t=TB), ALU.add).then_inc(S["moe_sum"], 1)

        @block.tensor
        def _(pe):
            te = nc.tensor
            for name in ("theta_mm", "intra_mm", "w_mm", "yt_mm"):
                pe.sem_inc(S[name], 1)
            pe.wait_ge(S["cross_made"], 3)
            pe.wait_ge(S["const_made"], 5)
            te.matmul(bank[0][:, 0:NH], wbt, cross[:, 0:NH], start=True, stop=True)
            te.matmul(bank[0][:, NH:2 * NH], wct, cross[:, NH:2 * NH], start=True, stop=True)
            te.matmul(bank[1][:, 0:NH], ones[:, :], cross[:, 2 * NH:], start=True, stop=True).then_inc(S["cross_mm"], 1)
            pe.wait_ge(S["w_lo"], 1)
            pe.wait_ge(S["cross_copied"], 2)

            def three(ps, at, cols):
                te.matmul(ps, xh[:, at], wh[:, cols], start=True, stop=False)
                te.matmul(ps, xh[:, at], wl[:, cols], start=False, stop=False)
                return te.matmul(ps, xl[:, at], wh[:, cols], start=False, stop=True)

            def turn(i, j):
                pe.wait_ge(S["xn_made"], i * TB + (j + 1))
                if j >= 2:
                    pe.wait_ge(S["xl_made"], i * TB + (j - 1) + 1)
                else:
                    pe.wait_ge(S["xl_made"], i * TB + 1)
                te.transpose(bank[j % 2][:, 0:P], xn[:, j, :], ident[:, :]).then_inc(S["xn_t"], 1)

            def project(i, j):
                pe.wait_ge(S["xl_made"], i * TB + (j + 1) + 1)
                pe.wait_ge(S["sq_done"], 2 * (i * TB + max(j - 1, 0)) + 1)
                three(bank[2 + j % 2][:, 0:NP1], bass.ds(i * 512 + j * P, P), slice(0, NP1)).then_inc(S["proj_mm"], 1)

            with pe.Fori(0, B) as i:
                turn(i, 0)
                for j in range(1, TB):
                    turn(i, j)
                    project(i, j - 1)
                project(i, TB - 1)

            pe.wait_ge(S["om_shift"], 5)
            te.matmul(bank[5][:, 0:TH], upper[:, :], adt[:, 0:TH], start=True, stop=True)
            te.matmul(bank[6][:, 0:TH], ones[:, :], adt[:, 0:TH], start=True, stop=True).then_inc(S["ell_mm"], 1)
            te.matmul(bank[4][:, 0:TH], shift[:, :], omega[:, 0:TH], start=True, stop=False)
            te.matmul(bank[4][:, 0:TH], wrap[:, :], omega[:, NH:TH + NH], start=False, stop=True).then_inc(S["ell_mm"], 1)
            pe.wait_ge(S["small_act"], 5)
            te.transpose(bank[7][:, 0:P], ell[:, 0:TH], ident[:, :]).then_inc(S["ellt_mm"], 1)

            pe.wait_ge(S["route"], R_CHOSEN)
            pe.wait_ge(S["const_made"], 5)
            te.matmul(bank[2][:, 0:T * NE], before[:, :], mm[:, 0:T * NE], start=True, stop=True).then_inc(S["rt_mm"], 1)
            te.matmul(bank[3][:, 0:T * NE], ones[:, :], mm[:, 0:T * NE], start=True, stop=True).then_inc(S["rt_mm"], 1)

            with pe.Fori(0, B) as i:
                pe.wait_ge(S["ang_made"], i + 1)
                pe.wait_ge(S["red4"], i + 1)
                te.matmul(bank[0][:, :], upper[:, :], ang[:, :], start=True, stop=False)
                for k in range(1, TB):
                    m = te.matmul(bank[0][:, k * P:], ones[:, :], ang[:, 0:(TB - k) * P], start=False, stop=(k == TB - 1))
                m.then_inc(S["theta_mm"], 1)

            def front(par, at, n):
                three(bank[par][:, :], at, slice(NP1, NP1 + NP2)).then_inc(S["zx_mm"], 1)
                pe.wait_ge(S["kq_ready"], n + 1)
                pe.wait_ge(S["kq_first"], n + 1)
                pe.wait_ge(S["qt_copied"], n)
                for q in range(2):
                    for h in range(NH):
                        m = te.transpose(bank[2 + q][:, h * P:(h + 1) * P], kq[:, par, (q * NH + h) * P:(q * NH + h + 1) * P], ident[:, :])
                m.then_inc(S["kq_tr"], 1)
                pe.wait_ge(S["kt_copied"], n + 1)
                pe.wait_ge(S["qt_copied"], n + 1)
                pe.wait_ge(S["m_made"], n + 1)
                for h in range(NH):
                    m = te.matmul(bank[4][:, h * P:(h + 1) * P], kqt[:, 0, h * P:(h + 1) * P], kqt[:, 1, h * P:(h + 1) * P], start=True, stop=True)
                m.then_inc(S["s_mm"], 1)

            pe.wait_ge(S["red4"], B + 1)
            pe.wait_ge(S["proj_out"], T)
            front(0, slice(0, P), 0)
            def recurrence(first, last):
              with pe.Fori(first, last) as i:
                for j in range(TB):
                    par = j % 2
                    t, nxt = i * TB + j, i * TB + (j + 1)
                    pe.wait_ge(S["y_b"], t + 1)
                    if j:
                        pe.wait_ge(S["st_made"], i * 3 + j + 1)
                        for h in range(NH):
                            c = slice(h * HD, (h + 1) * HD)
                            te.matmul(bank[5][:, DI + h * HD:DI + (h + 1) * HD], kqt[:, 1, h * P:(h + 1) * P], st[:, (j - 1) % 2, c], start=True, stop=True)
                    if j < 3:
                        pe.wait_ge(S["xw_made"], nxt + 1)
                        pe.wait_ge(S["st_made"], i * 3 + j + 1)
                        for h in range(NH):
                            c = slice(h * HD, (h + 1) * HD)
                            m = te.matmul(bank[6][:, c], kq[:, par, h * P:(h + 1) * P], xw[:, par, c], start=True, stop=True)
                        m.then_inc(S["w_mm"], 1)
                    pe.wait_ge(S["m_made"], nxt + 1)
                    pe.wait_ge(S["xg_made"], nxt + 1)
                    for h in range(NH):
                        c = slice(h * HD, (h + 1) * HD)
                        m = te.matmul(bank[5][:, c], mm[:, h * P:(h + 1) * P], xg[:, par, c], start=True, stop=True)
                    m.then_inc(S["intra_mm"], 1)
                    pe.wait_ge(S["x_copied"], t + 1)
                    pe.wait_ge(S["sz_made"], t + 1)
                    front(1 - par, bass.ds(i * 512 + (j + 1) * P, P), nxt)
                    pe.wait_ge(S["y_gated"], nxt)
                    pe.wait_ge(S["out_copied"], t + 1)
                    for c in range(2):
                        m = te.transpose(bank[7][:, c * P:(c + 1) * P], yg[:, c * P:(c + 1) * P], ident[:, :])
                    m.then_inc(S["yt_mm"], 1)
                    pe.wait_ge(S["yt_copied"], nxt)
                    pe.wait_ge(S["wo_half"], 1)
                    for c in range(2):
                        m = te.matmul(bank[7][:, DI:DI + P], ygt[:, c * P:(c + 1) * P], wo[:, c, :], start=(c == 0), stop=(c == 1))
                    m.then_inc(S["out_mm"], 1)

            recurrence(0, BP1)

            def turn_rows(k, n, load):
                if load is not None:
                    pe.wait_ge(S[f"xg_in{k // 4}"], load)
                if n is not None:
                    pe.wait_ge(S["xg_lo"], n)
                te.transpose(bank[1][:, 0:P], xgb[:, k, :], ident[:, :]).then_inc(S["x_t"], 1)

            def up(par, n, at, first=False):
                e = pe.value_load(tile_expert[0:1, at], min_val=0, max_val=(NE - 1) * U)
                pe.wait_ge(S["xg_lo"], n + 1)
                if not first:
                    pe.wait_ge(S["gelu"], n)
                for c in range(UC):
                    ps = bank[2 + par][:, c * P:(c + 1) * P]
                    w = bass.ds(e + c * P, P)
                    te.matmul(ps, wu_h[:, w], xgt[:, par, 0, :], start=True, stop=False)
                    te.matmul(ps, wu_h[:, w], xgt[:, par, 1, :], start=False, stop=False)
                    m = te.matmul(ps, wu_l[:, w], xgt[:, par, 0, :], start=False, stop=True)
                m.then_inc(S["up_mm"], 1)

            def down(par, n, at):
                e = pe.value_load(tile_expert[0:1, at], min_val=0, max_val=(NE - 1) * U)
                pe.wait_ge(S["h_lo"], n + 2)
                pe.wait_ge(S["y_copied"], n + 1)
                ps = bank[5 + par][:, 0:P]
                for c in range(UC):
                    w = bass.ds(e + c * P, P)
                    h, l = (hh[:, par, q, c * P:(c + 1) * P] for q in range(2))
                    te.matmul(ps, h, wd_h[:, w], start=(c == 0), stop=False)
                    te.matmul(ps, h, wd_l[:, w], start=False, stop=False)
                    te.matmul(ps, l, wd_h[:, w], start=False, stop=False)
                te.matmul(ps, sel[:, :], bd[:, bass.ds(pe.snap(e // UC), P)], start=False, stop=True).then_inc(S["down_mm"], 1)

            pe.wait_ge(S["wx_lo"], 2 * TB)
            pe.wait_ge(S["bd_made"], 7)
            turn_rows(0, None, 16)
            turn_rows(1, 1, None)
            up(0, 0, slice(0, 1), True)
            with pe.Fori(0, XT // 8) as i:
                for k in range(8):
                    ahead = (k + 2) % 8
                    turn_rows(ahead, i * 8 + (k + 2), {4: (i + 1) * 16, 0: (i + 2) * 16}.get(ahead))
                    up((k + 1) % 2, i * 8 + (k + 1), bass.ds(i * 8 + (k + 1), 1))
                    down(k % 2, i * 8 + k, bass.ds(i * 8 + k, 1))
            recurrence(BP1, B)


def kernel(L0_attn_u, L0_attn_W_in, L0_attn_W_out, L0_attn_dt_bias, L0_attn_B_bias, L0_attn_C_bias,
           L0_attn_B_norm_w, L0_attn_C_norm_w, L0_attn_D, L0_ffn_w_router, L0_ffn_w_up, L0_ffn_b_up,
           L0_ffn_w_down, L0_ffn_b_down):
    import numpy as np
    import concourse.bacc as bacc
    from concourse.bass_utils import run_bass_kernel_spmd

    w = np.asarray(L0_attn_W_in)
    z, xx, bg, cg, rest = w[:, :256], w[:, 256:512], w[:, 512:640], w[:, 640:768], w[:, 768:]
    bb, cb = np.asarray(L0_attn_B_bias), np.asarray(L0_attn_C_bias)
    bw, cw = np.asarray(L0_attn_B_norm_w), np.asarray(L0_attn_C_norm_w)
    arrays = {
        "x": np.asarray(L0_attn_u).reshape(B * L, DM),
        "w_in": np.concatenate([bg, cg, rest, np.asarray(L0_ffn_w_router).T, z, xx], axis=1),
        "cols": np.concatenate([bg.T, cg.T, bw[:, None], cw[:, None], bb.T, cb.T], axis=1),
        "rows": np.concatenate([bw, cw, bb.reshape(-1), cb.reshape(-1), np.asarray(L0_attn_dt_bias), np.asarray(L0_attn_D)]),
        "w_out": np.asarray(L0_attn_W_out),
        "w_up": np.asarray(L0_ffn_w_up).transpose(2, 0, 1).reshape(DM, NE * U),
        "b_up": np.asarray(L0_ffn_b_up).reshape(NE, UC, P).transpose(2, 0, 1).reshape(P, NE * UC),
        "w_dn": np.asarray(L0_ffn_w_down).reshape(NE, DM, UC, P).transpose(3, 0, 2, 1).reshape(P, NE * U),
        "b_dn": np.asarray(L0_ffn_b_down).reshape(-1),
    }
    arrays = {k: np.ascontiguousarray(a) for k, a in arrays.items()}
    nc = bacc.Bacc("TRN2", target_bir_lowering=False, num_devices=1)
    args = [nc.dram_tensor(k, a.shape, F32, kind="ExternalInput").ap() for k, a in arrays.items()]
    out = nc.dram_tensor("out", (B * L, DM), F32, kind="ExternalOutput").ap()
    build(nc, *args, out)
    r = run_bass_kernel_spmd(nc, [arrays], core_ids=[0])
    return r.results[0]["out"].reshape(B, L, DM)
```

```python
import math
from contextlib import ExitStack

import concourse.bass as bass
from concourse import mybir

ALU = mybir.AluOpType
ACT = mybir.ActivationFunctionType
AX_X = mybir.AxisListType.X
F32 = mybir.dt.float32
F16 = mybir.dt.float16
I32 = mybir.dt.int32

P = 128
B, L, DM = 8, 512, 128
T = B * L // P
TB = L // P
NH, HD = 4, 64
DI = NH * HD
NA = 32
NE = 8
U = 512
UC = U // P
RB = 2 * P
XB = 2 * B * L // RB + NE
XBPAD = XB + 4
XT, XPAD = XB * RB // P, XBPAD * RB // P
BP1 = 4
EPS = 1e-5
A_FLOOR = 1e-4
C_B, C_C, C_UB, C_UC, C_DT, C_A, C_TRAP, C_ANG, C_RT = 0, 128, 256, 260, 264, 268, 272, 276, 308
NP1 = C_RT + NE
NP2 = 2 * DI
TWO_PI_HI = 6.28125
TWO_PI_LO = 2 * math.pi - TWO_PI_HI
NEVER = -1e30
R_DIFF, R_CHOSEN, R_ALL = 12, 13, 35
ROUND = 1.5 * 2.0 ** 23


def build(nc, x, w_in, cols, rows, w_out, w_up, b_up, w_dn, b_dn, out):
    xv = x.rearrange("(b t p) d -> b p t d", t=TB, p=P)
    ov = out.rearrange("(b t p) d -> b p t d", t=TB, p=P)
    ell_dram = nc.dram_tensor("ell_rows", ((T + TB) * NH, P), F32, kind="Internal").ap()
    xg_dram = nc.dram_tensor("rows_by_expert", (XPAD * P, 2 * P), F16, kind="Internal").ap()
    yg_dram = nc.dram_tensor("results_by_expert", (XT * P, P), F32, kind="Internal").ap()

    with ExitStack() as ctx:
        def sb(name, shape, dt=F32):
            return ctx.enter_context(nc.sbuf_tensor(name, shape, dt))

        def sem(name):
            return ctx.enter_context(nc.semaphore(name))

        bank = [ctx.enter_context(nc.psum_tensor(f"bank{n}", [P, 512], F32)) for n in range(8)]

        ident = sb("ident", [P, P])
        upper = sb("upper", [P, P])
        ones = sb("ones", [P, P])
        shift = sb("shift", [P, P])
        wrap = sb("wrap", [P, P])
        zero4 = sb("zero4", [TB * NH, P])
        before = sb("before", [P, P])
        tile_row = sb("tile_row", [P, XBPAD])
        full_row = sb("full_row", [P, T])
        first_row = sb("first_row", [P, NE])
        rt_m1, rt_m2, rt_k = (sb(n, [P, T]) for n in ("rt_m1", "rt_m2", "rt_k"))
        rt_tiles, rt_end, rt_start = (sb(n, [P, NE]) for n in ("rt_tiles", "rt_end", "rt_start"))
        gate = sb("gate", [P, 2, T])
        slot = sb("slot", [P, T + 2, 2])
        tile_expert = sb("tile_expert", [P, XBPAD], I32)
        tile_bias = sb("tile_bias", [P, XBPAD], I32)
        em = sb("em", [P, 2, NH * P])
        wf = em[:, :, :].rearrange("p a n -> p (a n)")[:, 0:NP1 + NP2]
        wh = sb("wh", [P, NP1 + NP2], F16)
        wl = sb("wl", [P, NP1 + NP2], F16)
        colp = sb("colp", [P, 2 * P + 2 + 2 * NH])
        NROW = 2 * P + 2 * NH * P + NH + NH
        rowp = sb("rowp", [P, NROW])
        wo = sb("wo", [P, 2, P])
        wbt, wct = colp[:, 0:P], colp[:, P:2 * P]
        wn_b, wn_c = colp[:, 256:257], colp[:, 257:258]
        bb_t, cb_t = colp[:, 258:262], colp[:, 262:266]
        nw = rowp[:, 0:2 * P]
        kq_bias = rowp[:, 256:1280]
        dtb_r, d_r = rowp[:, 1280:1284], rowp[:, 1284:1288]
        bias8 = sb("bias8", [P, 2 * NH])
        cross = sb("cross", [P, 3 * NH])
        kappa = sb("kappa", [P, NH])
        x_all = sb("x_all", [P, T * P])
        xh = sb("xh", [P, (T + 1) * P], F16)
        xl = sb("xl", [P, (T + 1) * P], F16)
        proj = sb("proj", [P, (T + 1) * NP1 + 2 * P])
        cs = sb("cs", [P, (T + 1) * 2 * P])
        ao_view = cs[:, 0:T * 2 * P].rearrange("p (t c) -> p t c", c=2 * P)
        stats = sb("stats", [P, T * 6])
        mean, ve, rstd, nmr, ln_t = (sb(n, [P, T]) for n in ("mean", "ve", "rstd", "nmr", "ln_t"))
        ss = sb("ss", [P, 2, T + 2])
        bc0 = sb("bc0", [P, T])
        r_bc = sb("r_bc", [P, 2, T + 2])
        r_t = sb("r_t", [P, 2, T + 2])
        TH = T * NH
        dt_all, adt, beta, omega, gg = (sb(n, [P, TH + NH]) for n in ("dt_all", "adt", "beta", "omega", "gg"))
        ell, expell, ge, coef, cd, nell = (sb(n, [P, TH + NH]) for n in ("ell", "expell", "ge", "coef", "cd", "nell"))
        dece, u1, u2 = (sb(n, [P, TH]) for n in ("dece", "u1", "u2"))
        ellt = sb("ellt", [P, P])
        bu = sb("bu", [P, NE * UC])
        bds = sb("bds", [33, NE * P])
        sel = sb("sel", [P, P], F16)
        sx = sb("sx", [P, 2, 2, 2, P], F16)
        ident16 = sb("ident16", [P, P], F16)
        sidx = sb("sidx", [P, 2, 4], I32)
        junk = sb("junk", [P, 2, P])
        bcn = sb("bcn", [P, 2 * P])
        kq = sb("kq", [P, 2, 2 * NH * P])
        rp = sb("rp", [P, 4, 2 * NH * NA])
        kqt = sb("kqt", [P, 2, NH * P])
        el = sb("el", [P, TB, NH * P])
        ee = sb("ee", [P, 2, NH * P])
        ang, th, tk, ta = (kq[:, k // 2, (k % 2) * 512:(k % 2 + 1) * 512] for k in range(4))
        xn, bw = (ee[:, k, :].rearrange("p (t n) -> p t n", t=TB) for k in range(2))
        v8, e8, s8, q8 = (el[:, k, 0:T * 2 * NH].rearrange("p (t n) -> p t n", t=T) for k in range(4))
        p8 = el[:, 0, 256:512].rearrange("p (t n) -> p t n", t=T)
        mm = sb("mm", [P, NH * P])
        zt = sb("zt", [P, DI])
        xs_raw = sb("xs_raw", [P, 2, DI])
        sz = sb("sz", [P, 2, DI])
        xg = sb("xg", [P, 2, DI])
        xw = sb("xw", [P, 2, DI])
        xc = sb("xc", [P, 2, DI])
        st = sb("st", [P, 2, DI])
        std = sb("std", [P, DI])
        zeros = cs[:, 0:4 * P].bitcast(F16)
        xback = [a.rearrange("p (t d) -> p t d", t=TB) for a in (kq[:, 0, 0:512], kq[:, 0, 512:1024], kq[:, 1, 0:512], kq[:, 1, 512:1024],
                                                                 el[:, 0, :], el[:, 1, :], el[:, 2, :], el[:, 3, :])]
        x16, p16 = x_all[:, :].bitcast(F16), proj[:, :].bitcast(F16)
        NU = NE * U
        wu_h, wu_l = x16[:, 0:NU], x16[:, NU:2 * NU]
        wd = p16[:, 0:2 * NU].rearrange("p (m q n) -> p m q n", q=2, n=P)
        bd = p16[:, 2 * NU:2 * NU + NE * P]
        assert (2 * NU + NE * P) * 2 <= BP1 * TB * NP1 * 4 and 4 * NU <= T * P * 4
        xgb = rp[:, :, :].rearrange("p a n -> p (a n)").bitcast(F16).rearrange("p (b n) -> p b n", n=2 * P)
        xgt = sx[:, :, :, :, :].rearrange("p a q t n -> p a q (t n)")
        turned = bank[7][:, 0:RB].bitcast(F16)
        hf = sb("hf", [P, 2, 2 * RB])
        hh = sb("hh", [P, 2, 2, UC, RB], F16)
        yb = kq[:, 1, :].rearrange("p (b n) -> p b n", n=P)
        gb = [hf[:, q, :].rearrange("p (t k n) -> p t k n", t=2, k=2) for q in range(2)]
        hh32 = hh[:, :, :, :, :].rearrange("p a b c n -> p (a b c n)").bitcast(F32)
        stage = [hf[:, :, :].rearrange("p a n -> p (a n)"), hh32[:, 0:1024], hh32[:, 1024:2048], rp[:, :, :].rearrange("p a n -> p (a n)"), kq[:, 1, :]]
        NST = len(stage)
        y1, y2, y3, yg = (sb(n, [P, DI]) for n in ("y1", "y2", "y3", "yg"))
        ygt = sb("ygt", [P, DI])

        S = {n: sem(n) for n in (
            "x_in", "wf_in", "cols_in", "rows_in", "wo_in", "const_zero", "const_made", "pads",
            "cross_made", "kappa_in", "cross_mm", "cross_copied", "w_hi", "w_lo", "wo_half", "b8",
            "stats_done", "ln_chain", "ln_sqrt", "xn_made", "xn_t", "xh_made", "xl_made",
            "proj_mm", "proj_out", "sq_done", "bc_weighted", "bc0_done",
            "small", "small_act", "om_shift", "ell_mm", "ellt_mm", "ellt_sb", "ell_out", "pad_out",
            "r_sqrt", "ang_made", "theta_mm", "red1", "red2", "red3", "red4", "sin_made", "abs_made", "cos_made",
            "zx_mm", "z_tanh", "x_copied", "sz_made", "xg_made", "xw_made", "xc_made",
            "b_norm", "kq_biased", "rotated", "kq_first", "kq_ready",
            "kq_tr", "kt_copied", "qt_copied", "s_mm", "e_exp", "e_masked", "m_made",
            "inter_mm", "w_mm", "intra_mm", "st_decayed", "st_made", "y_a", "y_b", "y_c", "y_gated",
            "yt_mm", "yt_copied", "out_mm", "out_copied", "out_sum", "stored", "iotas", "route", "rt_mask", "rt_mm", "rt_exp", "xg_zeroed", "zeros", "staged", "xg_in0", "xg_in1",
            "wx_hi", "wx_lo", "bd_in", "bd_made", "bu_in", "x_t", "xg_copied", "up_mm", "gelu", "h_hi", "h_lo",
            "down_mm", "y_lo", "y_copied", "y_out0", "y_out1", "idx_made", "combine1", "combine2", "x_again", "moe_sum", "sent", "rows_made", "go", "rows_low", "ident_low")}
        scat = [sem(f"scat{n}") for n in range(2)]
        gath = [sem(f"gath{n}") for n in range(2)]
        w_raw = [sem(f"w_raw{n}") for n in range(NST)]
        el_in = [sem(f"el_in{n}") for n in range(TB)]

        block = ctx.enter_context(nc.Block())

        def tok(ap, n):
            return ap.unsqueeze(2).to_broadcast([P, NH, n])

        def heads(ap):
            return ap.rearrange("p (h n) -> p h n", h=NH)

        def by_chunk(ap):
            return ap.rearrange("p (m n) -> p m n", n=P)

        def piece(n, q):
            k = (n % TB) * 8
            return by_chunk((wu_h, wu_l)[q])[:, k:k + 8, :] if n < TB else wd[:, k:k + 8, q, :]

        up_banks = ((bank[2], bank[3]), (bank[5], bank[6]))

        @block.sync
        def _(sp):
            sp.dma_start(wf[:, 0:2 * P], w_in[:, 0:2 * P]).then_inc(S["wf_in"], 16)
            sp.dma_start(wf[:, C_DT:], w_in[:, 2 * P:]).then_inc(S["wf_in"], 16)
            for b in range(B):
                sp.dma_start(x_all[:, b * 512:(b + 1) * 512].rearrange("p (t d) -> p t d", t=TB), xv[b]).then_inc(S["x_in"], 16)
            sp.wait_ge(S["zeros"], 1)
            sp.dma_start(xg_dram.rearrange("(c p r) d -> p c (r d)", p=P, r=4), zeros.unsqueeze(1).to_broadcast([P, XPAD // 4, 8 * P])
                         ).then_inc(S["xg_zeroed"], 16)
            sp.wait_ge(S["pads"], 1)
            sp.dma_start(ell_dram[TH:TH + TB * NH, :], zero4[:, :]).then_inc(S["pad_out"], 16)
            sp.wait_ge(S["ellt_sb"], 1)
            sp.dma_start(ell_dram[0:TH, :], ellt[:, :]).then_inc(S["ell_out"], 16)
            sp.wait_ge(S["ell_out"], 16)
            sp.wait_ge(S["pad_out"], 16)
            ell_t = ell_dram.rearrange("(t h) p -> t (h p)", h=NH)
            for j in range(TB):
                sp.dma_start(el[:, j, :], ell_t[j, :].partition_broadcast(P)).then_inc(el_in[j], 16)
            def prefetch(first, last):
                with sp.Fori(first, last) as i:
                    for j in range(TB):
                        sp.wait_ge(S["e_masked"], i * TB + (j + 1))
                        sp.dma_start(el[:, j, :], ell_t[bass.ds(i * TB + (TB + j), 1), :].rearrange("o n -> (o n)").partition_broadcast(P)
                                     ).then_inc(el_in[j], 16)

            def load_piece(n):
                src = w_up if n < TB else w_dn
                sp.dma_start(stage[n % NST], src[:, (n % TB) * 1024:(n % TB + 1) * 1024]).then_inc(w_raw[n % NST], 16)

            for n in range(3):
                load_piece(n)
            prefetch(0, BP1)
            for n in range(3, 2 * TB):
                if n < NST:
                    sp.wait_ge(S["intra_mm"], BP1 * TB + 1)
                    sp.wait_ge(S["kq_ready"], BP1 * TB + 1)
                else:
                    sp.wait_ge(S["wx_lo"], n - NST + 1)
                load_piece(n)
            ygv = yg_dram.rearrange("(g t p) d -> g p t d", t=4, p=P)
            xgv = xg_dram.rearrange("(g t p) d -> g p t d", t=4, p=P)
            sp.wait_ge(S["sent"], BP1 * TB + 2)
            sp.wait_ge(S["wx_lo"], 2 * TB)
            for g in range(2):
                sp.dma_start(xgb[:, 4 * g:4 * g + 4, :], xgv[g]).then_inc(S[f"xg_in{g}"], 16)
            with sp.Fori(0, XT // 8) as i:
                for g in range(2):
                    sp.wait_ge(S["x_t"], i * 4 + (2 * g + 2))
                    sp.dma_start(xgb[:, 4 * g:4 * g + 4, :], xgv[bass.ds(i * 2 + (2 + g), 1)].rearrange("o p t d -> (o p) t d")).then_inc(S[f"xg_in{g}"], 16)
                for g in range(2):
                    sp.wait_ge(S["y_copied"], i * 4 + (2 * g + 2 + 1))
                    sp.dma_start(ygv[bass.ds(i * 2 + g, 1)].rearrange("o p t d -> (o p) t d"), yb[:, 4 * g:4 * g + 4, :]).then_inc(S[f"y_out{g}"], 16)
            prefetch(BP1, B)
            for b in range(B):
                if b == 0:
                    sp.wait_ge(S["out_copied"], T + 1)
                    sp.wait_ge(S["s_mm"], T + 1)
                    sp.wait_ge(S["e_masked"], T + 1)
                    for j in range(TB):
                        sp.wait_ge(el_in[j], 16 * (B + 1))
                sp.dma_start(xback[b], xv[b]).then_inc(S["x_again"], 16)
            with sp.Fori(0, B) as i:
                sp.wait_ge(S["out_sum"], i + 1)
                sp.dma_start(ov[bass.ds(i, 1)].rearrange("o p t d -> (o p) t d"),
                             ao_view[:, bass.ds(i * TB, TB), 0:P]).then_inc(S["stored"], 16)
            sp.wait_ge(S["stored"], 16 * B)

        @block.gpsimd
        def _(pool):
            pl = nc.gpsimd
            for name in ("xc_made", "y_out0", "y_out1"):
                pool.sem_inc(S[name], 1)
            for name in ("gelu", "y_copied", "rows_low", "y_a"):
                pool.sem_inc(S[name], 1)
            pool.sem_inc(S["down_mm"], 2)
            pool.sem_inc(S["combine2"], 3)
            pool.sem_inc(S["sent"], 2)
            pl.memset(ident[:, :], 0.0).then_inc(S["const_zero"], 1)
            pl.memset(upper[:, :], 1.0).then_inc(S["const_zero"], 1)
            pl.memset(shift[:, :], 0.0).then_inc(S["const_zero"], 1)
            pl.memset(wrap[:, :], 0.0).then_inc(S["const_zero"], 1)
            pl.memset(ones[:, :], 1.0).then_inc(S["const_zero"], 1)
            pool.wait_ge(S["const_zero"], 5)
            pl.affine_select(out=ident[:, :], in_=ident[:, :], compare_op=ALU.not_equal, fill=1.0, base=0,
                             pattern=[[-1, P]], channel_multiplier=1).then_inc(S["const_made"], 1)
            pl.affine_select(out=upper[:, :], in_=upper[:, :], compare_op=ALU.is_ge, fill=0.0, base=0,
                             pattern=[[1, P]], channel_multiplier=-1).then_inc(S["const_made"], 1)
            pl.affine_select(out=shift[:, :], in_=shift[:, :], compare_op=ALU.not_equal, fill=1.0, base=-1,
                             pattern=[[-1, P]], channel_multiplier=1).then_inc(S["const_made"], 1)
            pl.affine_select(out=wrap[:, :], in_=wrap[:, :], compare_op=ALU.not_equal, fill=1.0, base=-P * (P - 1),
                             pattern=[[P, P]], channel_multiplier=1).then_inc(S["const_made"], 1)
            pl.memset(zeros, 0.0).then_inc(S["zeros"], 1)
            pl.affine_select(out=before[:, :], in_=ones[:, :], compare_op=ALU.is_gt, fill=0.0, base=0,
                             pattern=[[1, P]], channel_multiplier=-1).then_inc(S["const_made"], 1)
            pl.iota(tile_row[:, :], pattern=[[1, XBPAD]], base=0, channel_multiplier=0, allow_small_or_imprecise_dtypes=True).then_inc(S["iotas"], 1)
            pl.iota(full_row[:, :], pattern=[[RB, T]], base=0, channel_multiplier=0, allow_small_or_imprecise_dtypes=True).then_inc(S["iotas"], 1)
            pl.iota(first_row[:, :], pattern=[[-1, NE]], base=NE, channel_multiplier=0, allow_small_or_imprecise_dtypes=True).then_inc(S["iotas"], 1)
            pool.wait_ge(S["const_made"], 5)
            pl.tensor_copy(ident16[:, :], ident[:, :]).then_inc(S["ident_low"], 1)
            pl.memset(sel[:, :], 0.0).then_inc(S["bd_made"], 1)
            pl.memset(bds[:, :], 0.0).then_inc(S["bd_made"], 1)
            pool.wait_ge(S["bd_made"], 2)
            for p in (0, 32):
                pl.memset(sel[p:p + 1, :], 1.0).then_inc(S["bd_made"], 1)
                pool.dma_start(bds[p:p + 1, :], b_dn.rearrange("(o n) -> o n", o=1)).then_inc(S["bd_in"], 16)
            pool.wait_ge(S["bd_made"], 4)
            pl.memset(zero4[:, :], 0.0).then_inc(S["pads"], 1)
            pl.memset(xh[:, T * P:], 0.0).then_inc(S["pads"], 1)
            pl.memset(xl[:, T * P:], 0.0).then_inc(S["pads"], 1)
            pl.memset(proj[:, T * NP1:], 0.0).then_inc(S["pads"], 1)
            pl.memset(cs[:, T * 2 * P:], 0.0).then_inc(S["pads"], 1)
            pl.memset(ss[:, :, T:], 0.0).then_inc(S["pads"], 1)
            pl.memset(slot[:, T:, :], 0.0).then_inc(S["pads"], 1)
            for a in (dt_all, omega, gg, expell, ge, coef, cd, nell):
                pl.memset(a[:, TH:], 0.0).then_inc(S["pads"], 1)
            pool.wait_ge(S["small"], 40)
            pool.wait_ge(el_in[0], 16)
            pl.affine_select(out=heads(ee[:, 0, :]), in_=heads(el[:, 0, :]), compare_op=ALU.is_gt,
                             fill=NEVER, base=0, pattern=[[0, NH], [1, P]], channel_multiplier=-1).then_inc(S["e_masked"], 1)

            def recurrence(first, last, moves):
                with pool.Fori(first, last) as i:
                    for j in range(TB):
                        n = i * TB + j
                        if j in (1, 2):
                            pool.wait_ge(S["st_made"], i * 3 + j + 1)
                            pl.tensor_tensor(heads(std[:, :]), heads(st[:, (j - 1) % 2, :]), tok(cd[:, bass.ds(i * (TB * NH) + j * NH, NH)], HD), ALU.mult
                                             ).then_inc(S["st_decayed"], 1)
                        pool.wait_ge(S["e_exp"], n + 1)
                        pool.wait_ge(el_in[(j + 1) % TB], (i + (1 if j < TB - 1 else 2)) * 16)
                        pool.wait_ge(S["x_copied"], i * TB + (j + 1) + 1)
                        pl.tensor_tensor(heads(xc[:, j % 2, :]), heads(xs_raw[:, j % 2, :]), tok(coef[:, bass.ds(i * (TB * NH) + j * NH, NH)], HD), ALU.mult
                                         ).then_inc(S["xc_made"], 1)
                        pl.affine_select(out=heads(ee[:, (j + 1) % 2, :]), in_=heads(el[:, (j + 1) % TB, :]), compare_op=ALU.is_gt,
                                         fill=NEVER, base=0, pattern=[[0, NH], [1, P]], channel_multiplier=-1).then_inc(S["e_masked"], 1)
                        moves(i, j)

            def send(i, j):
                def arrived(k):
                    pool.wait_ge(scat[k % 2], i * 128 + 64 * (k // 2 + 1))
                    pool.sem_inc(S["sent"], 1)

                if j:
                    arrived(j - 1)
                pool.wait_ge(S["staged"], 2 * (i * TB + (j + 1)))
                pl.tensor_tensor(sx[:, j % 2, :, 1, :], junk[:, :, :], sx[:, j % 2, :, 0, :], ALU.subtract).then_inc(S["rows_low"], 1)
                pool.wait_ge(S["rows_low"], i * TB + (j + 2))
                pool.sem_inc(S["go"], 1)
                for t in range(2):
                    for k in range(2):
                        pool.indirect_dma_start(xg_dram, bass.IndirectOffsetOnAxis(ap=sidx[:, j % 2, 2 * t + k:2 * t + k + 1], axis=0),
                                                sx[:, j % 2, t, :, :].rearrange("p q n -> p (q n)"), None).then_inc(scat[j % 2], 16)
                if j == TB - 1:
                    arrived(j)

            def fetch_results(par, n):
                pool.wait_ge(S["idx_made"], n + 1)
                pool.wait_ge(S["combine2"], 2 * n + 1)
                pool.sem_inc(S["go"], 1)
                for t in range(2):
                    for k in range(2):
                        pool.indirect_dma_start(gb[par][:, t, k, :], None, yg_dram,
                                                bass.IndirectOffsetOnAxis(ap=sidx[:, par, 2 * t + k:2 * t + k + 1], axis=0)).then_inc(gath[par], 16)

            def fetch(i, j):
                fetch_results((j + 1) % 2, (i - BP1) * TB + (j + 1))

            pool.wait_ge(S["xg_zeroed"], 16)
            recurrence(0, BP1, send)
            for g in range(2):
                pool.wait_ge(S[f"y_out{g}"], 16 * (XT // 8) + 1)
            pool.wait_ge(S["h_lo"], 2 * (XB + 2))
            fetch_results(0, 0)
            recurrence(BP1, B, fetch)
            pool.wait_ge(gath[0], 16 * 4 * (BP1 * TB // 2 + 1))
            pool.wait_ge(S["x_again"], 16 * B)
            for b in range(B):
                at = ao_view[:, b * TB:(b + 1) * TB, 0:P]
                pool.wait_ge(S["moe_sum"], b + 1)
                pl.tensor_tensor(at, at, xback[b], ALU.add).then_inc(S["out_sum"], 1)

        @block.scalar
        def _(act):
            sc = nc.scalar
            for name in ("sq_done", "cos_made", "sin_made", "abs_made", "e_exp", "out_copied", "x_copied"):
                act.sem_inc(S[name], 1)
            act.dma_start(colp[:, :], cols).then_inc(S["cols_in"], 16)
            act.dma_start(rowp[:, :], rows.partition_broadcast(P)).then_inc(S["rows_in"], 16)
            act.dma_start(wo[:, :, :], w_out.rearrange("(c p) d -> p c d", p=P)).then_inc(S["wo_in"], 16)
            act.dma_start(bu[:, :], b_up).then_inc(S["bu_in"], 16)
            act.wait_ge(S["cross_mm"], 1)
            sc.copy(wf[:, C_UB:C_DT], bank[0][:, 0:2 * NH]).then_inc(S["cross_copied"], 1)
            sc.copy(kappa[:, :], bank[1][:, 0:NH]).then_inc(S["cross_copied"], 1)
            act.wait_ge(S["ln_chain"], 6)
            sc.activation(ln_t[:, :], ve[:, :], ACT.Sqrt).then_inc(S["ln_sqrt"], 1)

            def high(i, j):
                act.wait_ge(S["xn_t"], i * TB + (j + 1))
                sc.copy(xh[:, bass.ds(i * 512 + j * P, P)], bank[j % 2][:, 0:P]).then_inc(S["xh_made"], 1)

            def project_out(i, j):
                act.wait_ge(S["proj_mm"], i * TB + (j + 1))
                ps = bank[2 + j % 2]
                sc.copy(proj[:, bass.ds(i * (TB * NP1) + j * NP1, NP1)], ps[:, 0:NP1]).then_inc(S["proj_out"], 1)
                act.wait_ge(S["sq_done"], 2 * (i * TB + j) + 1)
                for c in range(2):
                    sc.activation(junk[:, c, :], ps[:, c * P:(c + 1) * P], ACT.Square,
                                  accum_out=ss[:, c, bass.ds(i * TB + j, 1)]).then_inc(S["sq_done"], 1)

            with act.Fori(0, B) as i:
                high(i, 0)
                for j in range(1, TB):
                    high(i, j)
                    project_out(i, j - 1)
                project_out(i, TB - 1)

            act.wait_ge(S["small"], 2)
            sc.activation(r_t[:, :, :], ss[:, :, :], ACT.Sqrt).then_inc(S["small_act"], 1)
            act.wait_ge(S["small"], 4)
            sc.activation(e8[:, :, :], q8[:, :, :], ACT.Exp).then_inc(S["small_act"], 1)
            pr = proj[:, 0:T * NP1].rearrange("p (t n) -> p t n", t=T)
            trap = pr[:, :, C_TRAP:C_TRAP + NH]
            sc.activation(beta[:, 0:TH].rearrange("p (t h) -> p t h", h=NH), trap, ACT.Exp, scale=-1.0).then_inc(S["small_act"], 1)
            sc.activation(omega[:, 0:TH].rearrange("p (t h) -> p t h", h=NH), trap, ACT.Exp).then_inc(S["small_act"], 1)
            act.wait_ge(S["ell_mm"], 1)
            sc.copy(ell[:, 0:TH], bank[5][:, 0:TH]).then_inc(S["small_act"], 1)
            sc.activation(expell[:, 0:TH], bank[5][:, 0:TH], ACT.Exp).then_inc(S["small_act"], 1)
            sc.mul(nell[:, 0:TH], bank[5][:, 0:TH], -1.0).then_inc(S["small_act"], 1)
            sc.activation(cd[:, 0:TH], bank[6][:, 0:TH], ACT.Exp).then_inc(S["small_act"], 1)
            act.wait_ge(S["ellt_mm"], 1)
            sc.copy(ellt[:, :], bank[7][:, 0:P]).then_inc(S["ellt_sb"], 1)
            act.wait_ge(S["small"], 25)
            sc.activation(dece[:, :], dece[:, :], ACT.Exp).then_inc(S["small_act"], 1)

            act.wait_ge(S["route"], R_DIFF)
            sc.activation(rt_m2[:, :], rt_m2[:, :], ACT.Exp).then_inc(S["rt_exp"], 1)

            act.wait_ge(S["xg_zeroed"], 16)
            with act.Fori(0, B) as i:
                act.wait_ge(S["red4"], i + 1 + 1)
                cv = cs[:, bass.ds(i * (TB * 2 * P), TB * 2 * P)].rearrange("p (t c n) -> p t c n", t=TB, c=2)
                tv = th[:, :].rearrange("p (t n) -> p t n", t=TB)
                sc.activation(cv[:, :, 1, :], tv, ACT.Sin).then_inc(S["sin_made"], 1)
                act.wait_ge(S["cos_made"], i + 1)
                sc.activation(ta[:, :], th[:, :], ACT.Abs).then_inc(S["abs_made"], 1)
                act.wait_ge(S["abs_made"], i + 1 + 1)
                sc.activation(cv[:, :, 0, :], ta[:, :].rearrange("p (t n) -> p t n", t=TB), ACT.Sin, bias=math.pi / 2, scale=-1.0).then_inc(S["cos_made"], 1)

            def exps(par, col):
                for h in range(NH):
                    e = sc.activation(em[:, par, h * P:(h + 1) * P], ee[:, par, h * P:(h + 1) * P], ACT.Exp, bias=nell[:, col(h)])
                e.then_inc(S["e_exp"], 1)

            def norms(at, rb, rc):
                sc.activation(bcn[:, 0:P], proj[:, at(C_B)], ACT.Copy, scale=rb)
                sc.activation(bcn[:, P:], proj[:, at(C_C)], ACT.Copy, scale=rc).then_inc(S["b_norm"], 1)

            def zx_out(par, n):
                act.wait_ge(S["zx_mm"], n + 1)
                ps = bank[0]
                sc.activation(zt[:, :], ps[:, 0:DI], ACT.Tanh, scale=0.5).then_inc(S["z_tanh"], 1)
                sc.copy(xs_raw[:, par, :], ps[:, DI:2 * DI]).then_inc(S["x_copied"], 1)

            def kq_out(n):
                act.wait_ge(S["kq_tr"], n + 1)
                sc.copy(kqt[:, 0, :], bank[2][:, :]).then_inc(S["kt_copied"], 1)
                sc.copy(kqt[:, 1, :], bank[3][:, :]).then_inc(S["qt_copied"], 1)

            act.wait_ge(S["small"], 40)
            norms(lambda c: slice(c, c + P), r_bc[:, 0, 0:1], r_bc[:, 1, 0:1])
            act.wait_ge(S["e_masked"], 1)
            act.wait_ge(S["route"], R_ALL)
            exps(0, lambda h: slice(h, h + 1))
            zx_out(0, 0)
            kq_out(0)
            act.wait_ge(S["kq_biased"], 2)
            norms(lambda c: slice(NP1 + c, NP1 + c + P), r_bc[:, 0, 1:2], r_bc[:, 1, 1:2])
            def recurrence(first, last, moves):
              with act.Fori(first, last) as i:
                for j in range(TB):
                    t, nxt = i * TB + j, i * TB + (j + 1)
                    if j:
                        act.wait_ge(S["inter_mm"], i * 3 + j)
                        act.wait_ge(S["y_b"], t + 1)
                        for h in range(NH):
                            c = slice(h * HD, (h + 1) * HD)
                            a = sc.activation(y1[:, c], bank[1][:, c], ACT.Copy, scale=expell[:, bass.ds(i * (TB * NH) + (j * NH + h), 1)])
                        a.then_inc(S["y_a"], 1)
                    moves(i, j)
                    act.wait_ge(S["sz_made"], nxt + 1)
                    act.wait_ge(S["xg_made"], t + 1)
                    act.wait_ge(S["xw_made"], t + 1)
                    act.wait_ge(S["xc_made"], t + 1)
                    zx_out((j + 1) % 2, nxt)
                    act.wait_ge(S["e_masked"], i * TB + (j + 2))
                    act.wait_ge(S["m_made"], t + 1)
                    exps((j + 1) % 2, lambda h: bass.ds(i * (TB * NH) + ((j + 1) * NH + h), 1))
                    act.wait_ge(S["s_mm"], nxt)
                    kq_out(nxt)
                    act.wait_ge(S["kq_biased"], 2 * nxt + 2)
                    norms(lambda c: bass.ds(i * (TB * NP1) + ((j + 2) * NP1 + c), P), r_bc[:, 0, bass.ds(nxt + 1, 1)], r_bc[:, 1, bass.ds(nxt + 1, 1)])
                    act.wait_ge(S["yt_mm"], nxt + 1)
                    sc.copy(ygt[:, :], bank[7][:, 0:DI]).then_inc(S["yt_copied"], 1)
                    act.wait_ge(S["out_mm"], nxt)
                    sc.copy(cs[:, bass.ds(i * (TB * 2 * P) + j * 2 * P, P)], bank[7][:, DI:DI + P]).then_inc(S["out_copied"], 1)

            def stage_rows(i, j):
                act.wait_ge(S["sent"], i * TB + (j + 1))
                act.wait_ge(S["rows_low"], i * TB + (j + 1))
                for t in range(2):
                    n = i * 8 + (2 * j + t)
                    sc.activation(junk[:, t, :], x_all[:, bass.ds(n * P, P)], ACT.Identity,
                                  bias=nmr[:, bass.ds(n, 1)], scale=rstd[:, bass.ds(n, 1)]).then_inc(S["rows_made"], 1)
                act.wait_ge(S["rows_made"], i * 8 + (2 * j + 2))
                sc.copy(sx[:, j % 2, :, 0, :], junk[:, :, :]).then_inc(S["staged"], 1)
                sc.copy(sidx[:, j % 2, :], slot[:, :, :].rearrange("p t k -> p (t k)")[:, bass.ds(i * 16 + j * 4, 4)]).then_inc(S["staged"], 1)

            def places(par, n, at):
                act.wait_ge(S["combine2"], 2 * n + 1)
                sc.copy(sidx[:, par, :], slot[:, :, :].rearrange("p t k -> p (t k)")[:, at]).then_inc(S["idx_made"], 1)

            def stage_places(i, j):
                i = i - BP1
                act.wait_ge(gath[j % 2], i * 128 + (64 * (j // 2) + 64))
                for t in range(2):
                    n = i * 8 + (2 * j + t)
                    sc.activation(x_all[:, bass.ds(n * P, P)], gb[j % 2][:, t, 0, :], ACT.Copy, scale=gate[:, 0, bass.ds(n, 1)]).then_inc(S["combine1"], 1)
                places((j + 1) % 2, i * TB + (j + 1), bass.ds(i * 16 + (j + 1) * 4, 4))

            recurrence(0, BP1, stage_rows)

            act.wait_ge(S["sent"], BP1 * TB + 2)
            for n in range(2 * TB):
                act.wait_ge(w_raw[n % NST], 16 * (n // NST + 1))
                sc.copy(piece(n, 0), by_chunk(stage[n % NST])).then_inc(S["wx_hi"], 1)

            def copy_rows(par, n):
                act.wait_ge(S["x_t"], n + 1)
                sc.copy(xgt[:, par, :, :], turned.rearrange("p (q n) -> p q n", q=2)).then_inc(S["xg_copied"], 1)

            def gelus(par, n, b):
                for half in range(2):
                    act.wait_ge(S["up_mm"], 2 * n + (half + 1))
                    if not (isinstance(n, int) and n == 0):
                        act.wait_ge(S["h_lo"], 2 * n + (half - 1))
                    for c in range(UC // 2):
                        g = sc.activation(hf[:, half, c * RB:(c + 1) * RB], up_banks[par][half][:, c * RB:(c + 1) * RB], ACT.Gelu,
                                          bias=bu[:, 2 * half + c:][:, bass.ds(b, 1)])
                    g.then_inc(S["gelu"], 1)

            act.wait_ge(S["bu_in"], 16)
            def bias_at(n):
                return act.value_load(tile_bias[0:1, n], min_val=0, max_val=(NE - 1) * UC)

            copy_rows(0, 0)
            copy_rows(1, 1)
            gelus(0, 0, bias_at(slice(0, 1)))
            copy_rows(0, 2)
            gelus(1, 1, bias_at(slice(1, 2)))
            with act.Fori(0, XB // 8) as i:
                for k in range(8):
                    copy_rows((k + 1) % 2, i * 8 + (k + 3))
                    at = bias_at(bass.ds(i * 8 + (k + 2), 1))
                    act.wait_ge(S["down_mm"], i * 8 + (k + 3))
                    sc.copy(y1[:, :].rearrange("p (t n) -> p t n", t=2), bank[1][:, :].rearrange("p (t q n) -> p t q n", t=2, q=2)[:, :, 1, :]).then_inc(S["y_lo"], 1)
                    gelus(k % 2, i * 8 + (k + 2), at)
            places(0, 0, slice(0, 4))
            recurrence(BP1, B, stage_places)

        @block.vector
        def _(dve):
            v = nc.vector
            for name in ("bc0_done", "red4", "m_made", "y_b", "st_made", "sz_made", "xg_made", "xw_made", "xl_made"):
                dve.sem_inc(S[name], 1)
            dve.wait_ge(S["cols_in"], 16)
            v.tensor_scalar(cross[:, 0:NH], cb_t, wn_b, None, ALU.mult).then_inc(S["cross_made"], 1)
            v.tensor_scalar(cross[:, NH:2 * NH], bb_t, wn_c, None, ALU.mult).then_inc(S["cross_made"], 1)
            v.tensor_tensor(cross[:, 2 * NH:], bb_t, cb_t, ALU.mult).then_inc(S["cross_made"], 1)
            dve.wait_ge(S["wf_in"], 32)
            dve.wait_ge(S["cross_copied"], 1)
            v.tensor_copy(wh[:, :], wf[:, :]).then_inc(S["w_hi"], 1)
            dve.wait_ge(S["w_hi"], 1)
            v.tensor_tensor(wl[:, :], wf[:, :], wh[:, :], ALU.subtract).then_inc(S["w_lo"], 1)
            dve.wait_ge(S["rows_in"], 16)
            v.memset(bias8[:, NH:], 0.0).then_inc(S["b8"], 1)
            v.tensor_copy(bias8[:, 0:NH], dtb_r).then_inc(S["b8"], 1)
            dve.wait_ge(S["wo_in"], 16)
            v.tensor_scalar(wo[:, :, :], wo[:, :, :], 0.5, None, ALU.mult).then_inc(S["wo_half"], 1)

            dve.wait_ge(S["x_in"], 16 * B)
            with dve.Fori(0, B) as i:
                for j in range(TB):
                    v.bn_stats(stats[:, bass.ds(i * 24 + j * 6, 6)], x_all[:, bass.ds(i * 512 + j * P, P)]).then_inc(S["stats_done"], 1)
            dve.wait_ge(S["stats_done"], T)
            sv = stats[:, :].rearrange("p (t s) -> p t s", s=6)
            me, mo, ve2, vo2 = (sv[:, :, k] for k in (1, 4, 2, 5))
            v.tensor_tensor(mean[:, :], me, mo, ALU.add).then_inc(S["ln_chain"], 1)
            v.tensor_tensor(nmr[:, :], me, mo, ALU.subtract).then_inc(S["ln_chain"], 1)
            v.tensor_tensor(ve[:, :], ve2, vo2, ALU.add).then_inc(S["ln_chain"], 1)
            dve.wait_ge(S["ln_chain"], 3)
            v.scalar_tensor_tensor(out=ln_t[:, :], in0=nmr[:, :], scalar=0.25, in1=nmr[:, :], op0=ALU.mult, op1=ALU.mult).then_inc(S["ln_chain"], 1)
            dve.wait_ge(S["ln_chain"], 4)
            v.scalar_tensor_tensor(out=ve[:, :], in0=ve[:, :], scalar=1.0 / DM, in1=ln_t[:, :], op0=ALU.mult, op1=ALU.add).then_inc(S["ln_chain"], 1)
            dve.wait_ge(S["ln_chain"], 5)
            v.tensor_scalar(ve[:, :], ve[:, :], EPS, None, ALU.add).then_inc(S["ln_chain"], 1)
            dve.wait_ge(S["ln_sqrt"], 1)
            v.reciprocal(rstd[:, :], ln_t[:, :]).then_inc(S["ln_chain"], 1)
            dve.wait_ge(S["ln_chain"], 7)
            v.tensor_tensor(ln_t[:, :], rstd[:, :], rstd[:, :], ALU.mult).then_inc(S["ln_chain"], 1)
            dve.wait_ge(S["ln_chain"], 8)
            v.tensor_tensor(ln_t[:, :], ln_t[:, :], ve[:, :], ALU.mult).then_inc(S["ln_chain"], 1)
            dve.wait_ge(S["ln_chain"], 9)
            v.tensor_scalar(ln_t[:, :], ln_t[:, :], -0.5, 1.5, ALU.mult, ALU.add).then_inc(S["ln_chain"], 1)
            dve.wait_ge(S["ln_chain"], 10)
            v.tensor_tensor(rstd[:, :], rstd[:, :], ln_t[:, :], ALU.mult).then_inc(S["ln_chain"], 1)
            dve.wait_ge(S["ln_chain"], 11)
            v.scalar_tensor_tensor(out=nmr[:, :], in0=mean[:, :], scalar=-0.5, in1=rstd[:, :], op0=ALU.mult, op1=ALU.mult).then_inc(S["ln_chain"], 1)
            dve.wait_ge(S["ln_chain"], 12)

            def normalise(i, j):
                v.tensor_scalar(xn[:, j, :], x_all[:, bass.ds(i * 512 + j * P, P)], rstd[:, bass.ds(i * TB + j, 1)], nmr[:, bass.ds(i * TB + j, 1)],
                                ALU.mult, ALU.add).then_inc(S["xn_made"], 1)

            def low(i, j):
                dve.wait_ge(S["xh_made"], i * TB + (j + 1))
                at = bass.ds(i * 512 + j * P, P)
                v.tensor_tensor(xl[:, at], bank[j % 2][:, 0:P], xh[:, at], ALU.subtract).then_inc(S["xl_made"], 1)

            def weigh(i):
                dve.wait_ge(S["proj_out"], i * TB + TB)
                pv = proj[:, bass.ds(i * (TB * NP1), TB * NP1)].rearrange("p (t n) -> p t n", t=TB)
                v.tensor_tensor(pv[:, :, 0:2 * P], pv[:, :, 0:2 * P], nw.unsqueeze(1).to_broadcast([P, TB, 2 * P]), ALU.mult).then_inc(S["bc_weighted"], 1)
                dve.wait_ge(S["bc_weighted"], i + 1)
                dve.wait_ge(S["bc0_done"], i * TB + 1)
                for j in range(TB):
                    at = i * (TB * NP1) + j * NP1
                    v.scalar_tensor_tensor(out=bw[:, j, :], in0=proj[:, bass.ds(at + C_B, P)], scalar=1.0, in1=proj[:, bass.ds(at + C_C, P)],
                                           op0=ALU.mult, op1=ALU.mult, accum_out=bc0[:, bass.ds(i * TB + j, 1)]).then_inc(S["bc0_done"], 1)

            normalise(0, 0)
            normalise(0, 1)
            with dve.Fori(0, B - 1) as i:
                for j in range(TB):
                    low(i, j)
                    normalise(i + (j + 2) // TB, (j + 2) % TB)
                weigh(i)
            for j in range(TB):
                low(B - 1, j)
                if j < TB - 2:
                    normalise(B - 1, j + 2)
            weigh(B - 1)

            count = [0]

            def step(ins):
                ins.then_inc(S["small"], 1)
                count[0] += 1
                return count[0]

            def after(n):
                dve.wait_ge(S["small"], n)

            dve.wait_ge(S["pads"], 15)
            dve.wait_ge(S["b8"], 2)
            dve.wait_ge(S["sq_done"], 2 * T + 1)
            pr = proj[:, 0:T * NP1].rearrange("p (t n) -> p t n", t=T)
            n = step(v.tensor_scalar(ss[:, :, :], ss[:, :, :], 1.0 / P, EPS, ALU.mult, ALU.add))
            n = step(v.tensor_tensor(v8[:, :, :], pr[:, :, C_DT:C_DT + 2 * NH], bias8[:, :].unsqueeze(1).to_broadcast([P, T, 2 * NH]), ALU.add))
            after(2)
            n = step(v.scalar_tensor_tensor(out=q8[:, :, :], in0=v8[:, :, :], scalar=-1.0, in1=v8[:, :, :], op0=ALU.mult, op1=ALU.min))
            n = step(v.tensor_scalar(v8[:, :, :], v8[:, :, :], 0.0, None, ALU.max))
            dve.wait_ge(S["small_act"], 1)
            n = step(v.reciprocal(r_bc[:, :, :], r_t[:, :, :]))
            after(n)
            n = step(v.tensor_tensor(r_t[:, :, :], r_bc[:, :, :], r_bc[:, :, :], ALU.mult))
            after(n)
            n = step(v.tensor_tensor(r_t[:, :, :], r_t[:, :, :], ss[:, :, :], ALU.mult))
            after(n)
            n = step(v.tensor_scalar(r_t[:, :, :], r_t[:, :, :], -0.5, 1.5, ALU.mult, ALU.add))
            after(n)
            n = step(v.tensor_tensor(r_bc[:, :, :], r_bc[:, :, :], r_t[:, :, :], ALU.mult))
            dve.wait_ge(S["small_act"], 2)
            n = step(v.tensor_scalar(s8[:, :, :], e8[:, :, :], 2.0, None, ALU.add))
            after(n)
            n = step(v.reciprocal(s8[:, :, :], s8[:, :, :]))
            after(n)
            n = step(v.tensor_tensor(s8[:, :, :], s8[:, :, :], e8[:, :, :], ALU.mult))
            after(n)
            n = step(v.tensor_tensor(e8[:, :, :], s8[:, :, :], s8[:, :, :], ALU.mult))
            after(n)
            n = step(v.tensor_scalar(p8[:, :, :], e8[:, :, :], 1.0 / 15, None, ALU.mult))
            for k in (13, 11, 9, 7, 5, 3):
                after(n)
                n = step(v.scalar_tensor_tensor(out=p8[:, :, :], in0=p8[:, :, :], scalar=1.0 / k, in1=e8[:, :, :], op0=ALU.add, op1=ALU.mult))
            after(n)
            n = step(v.scalar_tensor_tensor(out=p8[:, :, :], in0=p8[:, :, :], scalar=1.0, in1=s8[:, :, :], op0=ALU.add, op1=ALU.mult))
            after(n)
            n = step(v.scalar_tensor_tensor(out=q8[:, :, :], in0=p8[:, :, :], scalar=2.0, in1=v8[:, :, :], op0=ALU.mult, op1=ALU.add))
            after(n)
            dtv = dt_all[:, 0:TH].rearrange("p (t h) -> p t h", h=NH)
            n = step(v.tensor_copy(dtv, q8[:, :, 0:NH]))
            n = step(v.tensor_scalar(q8[:, :, NH:], q8[:, :, NH:], A_FLOOR, -1.0, ALU.max, ALU.mult))
            after(24)
            v.tensor_tensor(adt[:, 0:TH].rearrange("p (t h) -> p t h", h=NH), q8[:, :, NH:], dtv, ALU.mult).then_inc(S["om_shift"], 1)
            dve.wait_ge(S["small_act"], 4)
            v.tensor_scalar(beta[:, 0:TH], beta[:, 0:TH], 1.0, None, ALU.add).then_inc(S["om_shift"], 1)
            v.tensor_scalar(omega[:, 0:TH], omega[:, 0:TH], 1.0, None, ALU.add).then_inc(S["om_shift"], 1)
            dve.wait_ge(S["om_shift"], 3)
            v.reciprocal(beta[:, 0:TH], beta[:, 0:TH]).then_inc(S["om_shift"], 1)
            v.reciprocal(omega[:, 0:TH], omega[:, 0:TH]).then_inc(S["om_shift"], 1)
            dve.wait_ge(S["small_act"], 8)
            n = step(v.tensor_tensor(dece[:, :], bank[6][:, 0:TH], ell[:, 0:TH], ALU.subtract))
            dve.wait_ge(S["ell_mm"], 2)
            n = step(v.tensor_tensor(gg[:, 0:TH], bank[4][:, 0:TH], beta[:, 0:TH], ALU.add))
            after(n)
            n = step(v.tensor_tensor(gg[:, 0:TH], gg[:, 0:TH], dt_all[:, 0:TH], ALU.mult))
            n = step(v.tensor_tensor(beta[:, 0:TH], beta[:, 0:TH], dt_all[:, 0:TH], ALU.mult))
            ub = pr[:, :, C_UB:C_UB + NH]
            uc = pr[:, :, C_UC:C_UC + NH]
            u1v, u2v = (a[:, :].rearrange("p (t h) -> p t h", h=NH) for a in (u1, u2))

            def per_tile(ap):
                return ap.unsqueeze(2).to_broadcast([P, T, NH])

            n = step(v.tensor_tensor(u1v, ub, per_tile(r_bc[:, 0, 0:T]), ALU.mult))
            n = step(v.tensor_tensor(u2v, uc, per_tile(r_bc[:, 1, 0:T]), ALU.mult))
            n = step(v.tensor_tensor(bc0[:, :], bc0[:, :], r_bc[:, 0, 0:T], ALU.mult))
            after(n)
            n = step(v.tensor_tensor(bc0[:, :], bc0[:, :], r_bc[:, 1, 0:T], ALU.mult))
            n = step(v.tensor_tensor(u1[:, :], u1[:, :], u2[:, :], ALU.add))
            after(n)
            n = step(v.tensor_tensor(u1v, u1v, per_tile(bc0[:, :]), ALU.add))
            dve.wait_ge(S["cross_copied"], 2)
            after(n)
            n = step(v.tensor_tensor(u1v, u1v, kappa[:, :].unsqueeze(1).to_broadcast([P, T, NH]), ALU.add))
            after(n)
            n = step(v.tensor_tensor(u1[:, :], u1[:, :], beta[:, 0:TH], ALU.mult))
            after(n)
            n = step(v.tensor_tensor(coef[:, 0:TH].rearrange("p (t h) -> p t h", h=NH), u1v, d_r.unsqueeze(1).to_broadcast([P, T, NH]), ALU.add))
            dve.wait_ge(S["small_act"], 9)
            n = step(v.tensor_tensor(ge[:, 0:TH], gg[:, 0:TH], dece[:, :], ALU.mult))
            after(n)
            n = step(v.memset(ta[:, 0:1], 0.0))
            n = step(v.memset(tk[:, 0:1], 0.0))
            assert n == 40

            lg = pr[:, :, C_RT:C_RT + NE]
            oh1, oh2, lg2, tmp = (em[:, k // 2, (k % 2) * 256:(k % 2 + 1) * 256].rearrange("p (t e) -> p t e", e=NE) for k in range(4))
            chosen = mm[:, 0:T * NE]
            cnt, upto, reset = y1, y2, y3
            rcount = [0]

            def rstep(ins):
                ins.then_inc(S["route"], 1)
                rcount[0] += 1
                dve.wait_ge(S["route"], rcount[0])

            def by_tile(ap):
                return ap.unsqueeze(2).to_broadcast([P, T, NE])

            def by_expert(ap):
                return ap.unsqueeze(1).to_broadcast([P, T, NE])

            def top(logits, m, oh):
                rstep(v.tensor_reduce(m, logits, AX_X, ALU.max))
                rstep(v.tensor_tensor(tmp, logits, by_tile(m), ALU.is_equal))
                rstep(v.tensor_tensor(tmp, tmp, by_expert(first_row[:, :]), ALU.mult))
                rstep(v.tensor_reduce(rt_k[:, :], tmp, AX_X, ALU.max))
                rstep(v.tensor_tensor(oh, by_tile(rt_k[:, :]), by_expert(first_row[:, :]), ALU.is_equal))

            dve.wait_ge(S["iotas"], 3)
            top(lg, rt_m1[:, :], oh1)
            rstep(v.scalar_tensor_tensor(out=lg2, in0=oh1, scalar=NEVER, in1=lg, op0=ALU.mult, op1=ALU.add))
            top(lg2, rt_m2[:, :], oh2)
            rstep(v.tensor_tensor(rt_m2[:, :], rt_m2[:, :], rt_m1[:, :], ALU.subtract))
            assert rcount[0] == R_DIFF
            rstep(v.tensor_tensor(chosen.rearrange("p (t e) -> p t e", e=NE), oh1, oh2, ALU.add))
            assert rcount[0] == R_CHOSEN
            dve.wait_ge(S["rt_exp"], 1)
            rstep(v.tensor_scalar(rt_m1[:, :], rt_m2[:, :], 1.0, None, ALU.add))
            rstep(v.reciprocal(gate[:, 0, :], rt_m1[:, :]))
            rstep(v.tensor_tensor(gate[:, 1, :], gate[:, 0, :], rt_m2[:, :], ALU.mult))
            rstep(v.memset(reset[:, :], 1.0))
            rstep(v.memset(reset[:, 0:T * NE].rearrange("p (e t) -> p e t", e=NE)[:, :, 0:1], 0.0))
            dve.wait_ge(S["rt_mm"], 2)
            et = cnt[:, :].rearrange("p (e t) -> p e t", e=NE)
            rstep(v.tensor_copy(et, bank[3][:, 0:T * NE].rearrange("p (t e) -> p e t", e=NE)))
            rstep(v.tensor_tensor_scan(upto[:, :], reset[:, :], cnt[:, :], 0.0, ALU.mult, ALU.add))
            ut = upto[:, :].rearrange("p (e t) -> p e t", e=NE)
            rstep(v.tensor_tensor(tmp.rearrange("p t e -> p (t e)").rearrange("p (e t) -> p e t", e=NE), ut[:, :, T - 1:T].to_broadcast([P, NE, T]),
                                  full_row[:, :].unsqueeze(1).to_broadcast([P, NE, T]), ALU.is_gt))
            rstep(v.tensor_reduce(rt_tiles[:, :], tmp.rearrange("p t e -> p (t e)").rearrange("p (e t) -> p e t", e=NE), AX_X, ALU.add))
            rstep(v.tensor_tensor_scan(rt_end[:, :], ones[:, 0:NE], rt_tiles[:, :], 0.0, ALU.mult, ALU.add))
            rstep(v.tensor_tensor(rt_start[:, :], rt_end[:, :], rt_tiles[:, :], ALU.subtract))
            te_ = rp[:, :, :].rearrange("p a n -> p (a n)")[:, 0:XBPAD * NE].rearrange("p (s e) -> p s e", e=NE)
            rstep(v.tensor_tensor(te_, tile_row[:, :].unsqueeze(2).to_broadcast([P, XBPAD, NE]), rt_end[:, :].unsqueeze(1).to_broadcast([P, XBPAD, NE]), ALU.is_ge))
            ts_ = rp[:, :, :].rearrange("p a n -> p (a n)")[:, XBPAD * NE:XBPAD * (NE + 1)]
            rstep(v.tensor_reduce(ts_, te_, AX_X, ALU.add))
            rstep(v.tensor_scalar(tile_expert[:, :], ts_, NE - 1.0, float(U), ALU.min, ALU.mult))
            rstep(v.tensor_scalar(tile_bias[:, :], ts_, NE - 1.0, float(UC), ALU.min, ALU.mult))
            rstep(v.tensor_tensor(cnt[:, :], upto[:, :], cnt[:, :], ALU.subtract))
            rstep(v.scalar_tensor_tensor(out=et, in0=rt_start[:, :].unsqueeze(2).to_broadcast([P, NE, T]), scalar=float(RB), in1=et, op0=ALU.mult, op1=ALU.add))
            rstep(v.tensor_tensor(lg2, bank[2][:, 0:T * NE].rearrange("p (t e) -> p t e", e=NE), cnt[:, :].rearrange("p (e t) -> p t e", e=NE), ALU.add))
            for k, oh in enumerate((oh1, oh2)):
                rstep(v.tensor_tensor(tmp, oh, lg2, ALU.mult))
                rstep(v.tensor_reduce(slot[:, 0:T, k], tmp, AX_X, ALU.add))
            assert rcount[0] == R_ALL, rcount

            def angle_steps(i, par):
                pv = proj[:, bass.ds(i * (TB * NP1), TB * NP1)].rearrange("p (t n) -> p t n", t=TB)
                for t in range(TB):
                    a = v.tensor_tensor(ang[:, t * P:(t + 1) * P].rearrange("p (h n) -> p h n", h=NH),
                                        pv[:, t, C_ANG:C_ANG + NA].unsqueeze(1).to_broadcast([P, NH, NA]),
                                        tok(dt_all[:, bass.ds(i * (TB * NH) + t * NH, NH)], NA), ALU.mult)
                a.then_inc(S["ang_made"], 1)

            with dve.Fori(0, B) as i:
                dve.wait_ge(S["theta_mm"], i + 1)
                angle_steps(i, 0)
                dve.wait_ge(S["theta_mm"], i + 1 + 1)
                v.tensor_scalar(tk[:, :], bank[0][:, :], 1.0 / (2 * math.pi), ROUND, ALU.mult, ALU.add).then_inc(S["red1"], 1)
                dve.wait_ge(S["red1"], i + 1)
                v.tensor_scalar(tk[:, :], tk[:, :], ROUND, None, ALU.subtract).then_inc(S["red2"], 1)
                dve.wait_ge(S["red2"], i + 1)
                dve.wait_ge(S["sin_made"], i + 1)
                dve.wait_ge(S["abs_made"], i + 1)
                v.scalar_tensor_tensor(out=th[:, :], in0=tk[:, :], scalar=-TWO_PI_HI, in1=bank[0][:, :], op0=ALU.mult, op1=ALU.add).then_inc(S["red3"], 1)
                dve.wait_ge(S["red3"], 2 * i + 1)
                v.scalar_tensor_tensor(out=th[:, :], in0=tk[:, :], scalar=-TWO_PI_LO, in1=th[:, :], op0=ALU.mult, op1=ALU.add).then_inc(S["red3"], 1)
                dve.wait_ge(S["red3"], 2 * i + 2)
                v.tensor_scalar(th[:, :], th[:, :], math.pi, -math.pi, ALU.min, ALU.max).then_inc(S["red4"], 1)

            def rope(ct, par, n):
                cv = cs[:, ct].rearrange("p (c n) -> p c n", c=2)
                dve.wait_ge(S["b_norm"], n + 1)
                k4 = kq[:, par, :].rearrange("p (q h n) -> p q h n", q=2, h=NH)
                b4 = kq_bias.rearrange("p (q h n) -> p q h n", q=2, h=NH)
                for q in range(2):
                    s = v.tensor_tensor(k4[:, q], bcn[:, q * P:(q + 1) * P].unsqueeze(1).to_broadcast([P, NH, P]), b4[:, q], ALU.add)
                    s.then_inc(S["kq_biased"], 1)
                dve.wait_ge(S["kq_biased"], 2 * n + 2)
                x1, x2 = k4[:, :, :, 0:NA], k4[:, :, :, NA:2 * NA]
                r = [rp[:, k, :].rearrange("p (q h n) -> p q h n", q=2, h=NH) for k in range(4)]
                c, s = (cv[:, k, :].rearrange("p (h n) -> p h n", h=NH).unsqueeze(1).to_broadcast([P, 2, NH, NA]) for k in range(2))
                v.tensor_tensor(r[0], x1, c, ALU.mult)
                v.tensor_tensor(r[1], x2, s, ALU.mult)
                v.tensor_tensor(r[2], x1, s, ALU.mult)
                v.tensor_tensor(r[3], x2, c, ALU.mult).then_inc(S["rotated"], 1)
                dve.wait_ge(S["rotated"], n + 1)
                v.tensor_tensor(x1, r[0], r[1], ALU.subtract).then_inc(S["kq_first"], 1)
                v.tensor_tensor(x2, r[2], r[3], ALU.add).then_inc(S["kq_ready"], 1)

            dve.wait_ge(S["cos_made"], B + 1)
            rope(slice(0, 2 * P), 0, 0)
            def recurrence(first, last, extra):
              with dve.Fori(first, last) as i:
                for j in range(TB):
                    par = j % 2
                    t, nxt = i * TB + j, i * TB + (j + 1)
                    hs = bass.ds(i * (TB * NH) + j * NH, NH)
                    dve.wait_ge(S["z_tanh"], nxt)
                    dve.wait_ge(S["x_copied"], nxt + 1)
                    v.scalar_tensor_tensor(out=sz[:, par, :], in0=zt[:, :], scalar=1.0, in1=bank[0][:, 0:DI], op0=ALU.add, op1=ALU.mult).then_inc(S["sz_made"], 1)
                    xr = heads(xs_raw[:, par, :])
                    v.tensor_tensor(heads(xg[:, par, :]), xr, tok(gg[:, hs], HD), ALU.mult).then_inc(S["xg_made"], 1)
                    v.tensor_tensor(heads(xw[:, par, :]), xr, tok(ge[:, hs], HD), ALU.mult).then_inc(S["xw_made"], 1)
                    dve.wait_ge(S["w_mm"], i * 3 + min(j, 3) + 1)
                    rope(bass.ds((i * (TB * 2 * P) + (j + 1) * 2 * P), 2 * P), 1 - par, nxt)
                    dve.wait_ge(S["s_mm"], nxt)
                    dve.wait_ge(S["e_exp"], nxt + 1)
                    dve.wait_ge(S["intra_mm"], t + 1)
                    v.tensor_tensor(mm[:, :], bank[4][:, :], em[:, par, :], ALU.mult).then_inc(S["m_made"], 1)
                    if j < 3:
                        dve.wait_ge(S["w_mm"], i * 3 + (j + 1) + 1)
                        if j == 0:
                            v.tensor_copy(st[:, 0, :], bank[6][:, 0:DI]).then_inc(S["st_made"], 1)
                        else:
                            dve.wait_ge(S["st_decayed"], i * 2 + j)
                            v.tensor_tensor(st[:, j % 2, :], std[:, :], bank[6][:, 0:DI], ALU.add).then_inc(S["st_made"], 1)
                    dve.wait_ge(S["intra_mm"], nxt + 1)
                    dve.wait_ge(S["xc_made"], nxt + 1)
                    if j == 0:
                        v.tensor_tensor(y2[:, :], bank[5][:, 0:DI], xc[:, par, :], ALU.add).then_inc(S["y_b"], 1)
                    else:
                        v.tensor_tensor(y3[:, :], bank[5][:, 0:DI], xc[:, par, :], ALU.add).then_inc(S["y_c"], 1)
                        dve.wait_ge(S["y_a"], i * 3 + j + 1)
                        dve.wait_ge(S["y_c"], i * 3 + j)
                        v.tensor_tensor(y2[:, :], y1[:, :], y3[:, :], ALU.add).then_inc(S["y_b"], 1)
                    dve.wait_ge(S["y_b"], nxt + 1)
                    dve.wait_ge(S["yt_mm"], t + 1)
                    v.tensor_tensor(yg[:, :], y2[:, :], sz[:, par, :], ALU.mult).then_inc(S["y_gated"], 1)
                    extra(i, j)

            def combine(i, j):
                i = i - BP1
                dve.wait_ge(gath[j % 2], i * 128 + (64 * (j // 2) + 64))
                for t in range(2):
                    at = bass.ds(i * (8 * P) + (2 * j + t) * P, P)
                    dve.wait_ge(S["combine1"], i * 8 + (2 * j + t + 1))
                    v.scalar_tensor_tensor(out=x_all[:, at], in0=gb[j % 2][:, t, 1, :], scalar=gate[:, 1, bass.ds(i * 8 + (2 * j + t), 1)], in1=x_all[:, at],
                                           op0=ALU.mult, op1=ALU.add).then_inc(S["combine2"], 1)

            recurrence(0, BP1, lambda i, j: None)

            dve.wait_ge(S["bd_in"], 32)
            dve.wait_ge(S["intra_mm"], BP1 * TB + 1)
            dve.wait_ge(S["sent"], BP1 * TB + 2)
            v.memset(bd, 0.0).then_inc(S["bd_made"], 1)
            dve.wait_ge(S["bd_made"], 5)
            v.tensor_copy(bd[0:33, :], bds[:, :]).then_inc(S["bd_made"], 1)
            dve.wait_ge(S["bd_made"], 6)
            v.tensor_tensor(bd[32:33, :], bds[32:33, :], bd[32:33, :], ALU.subtract).then_inc(S["bd_made"], 1)
            for n in range(2 * TB):
                dve.wait_ge(S["wx_hi"], n + 1)
                v.tensor_tensor(piece(n, 1), by_chunk(stage[n % NST]), piece(n, 0), ALU.subtract).then_inc(S["wx_lo"], 1)

            def split_hidden(par, n):
                if not isinstance(n, int):
                    dve.wait_ge(S["down_mm"], n + 1)
                for half in range(2):
                    f = hf[:, half, :].rearrange("p (c n) -> p c n", c=2)
                    h, l = (hh[:, par, q, 2 * half:2 * half + 2, :] for q in range(2))
                    dve.wait_ge(S["gelu"], 2 * n + (half + 2))
                    v.tensor_copy(h, f).then_inc(S["h_hi"], 1)
                    dve.wait_ge(S["h_hi"], 2 * n + (half + 1))
                    v.tensor_tensor(l, f, h, ALU.subtract).then_inc(S["h_lo"], 1)

            def results(k, n):
                dve.wait_ge(S["y_lo"], n + 1)
                v.tensor_tensor(yb[:, 2 * k:2 * k + 2, :], y1[:, :].rearrange("p (t n) -> p t n", t=2),
                                bank[1][:, :].rearrange("p (t q n) -> p t q n", t=2, q=2)[:, :, 0, :], ALU.add).then_inc(S["y_copied"], 1)

            split_hidden(0, 0)
            split_hidden(1, 1)
            with dve.Fori(0, XB // 8) as i:
                for k in range(8):
                    if k % 2 == 0:
                        dve.wait_ge(S[f"y_out{k // 2 % 2}"], i * 32 + (k // 4) * 16 + 1)
                    results(k % 4, i * 8 + k)
                    split_hidden(k % 2, i * 8 + (k + 2))
            for g in range(2):
                dve.wait_ge(S[f"y_out{g}"], 16 * (XT // 8) + 1)
            recurrence(BP1, B, combine)
            for b in range(B):
                at = ao_view[:, b * TB:(b + 1) * TB, 0:P]
                dve.wait_ge(S["out_copied"], T + 1)
                dve.wait_ge(S["combine2"], T + 3)
                v.tensor_tensor(at, at, x_all[:, b * 512:(b + 1) * 512].rearrange("p (t n) -> p t n", t=TB), ALU.add).then_inc(S["moe_sum"], 1)

        @block.tensor
        def _(pe):
            te = nc.tensor
            for name in ("theta_mm", "intra_mm", "w_mm", "yt_mm"):
                pe.sem_inc(S[name], 1)
            pe.wait_ge(S["cross_made"], 3)
            pe.wait_ge(S["const_made"], 5)
            te.matmul(bank[0][:, 0:NH], wbt, cross[:, 0:NH], start=True, stop=True)
            te.matmul(bank[0][:, NH:2 * NH], wct, cross[:, NH:2 * NH], start=True, stop=True)
            te.matmul(bank[1][:, 0:NH], ones[:, :], cross[:, 2 * NH:], start=True, stop=True).then_inc(S["cross_mm"], 1)
            pe.wait_ge(S["w_lo"], 1)
            pe.wait_ge(S["cross_copied"], 2)

            def three(ps, at, cols):
                te.matmul(ps, xh[:, at], wh[:, cols], start=True, stop=False)
                te.matmul(ps, xh[:, at], wl[:, cols], start=False, stop=False)
                return te.matmul(ps, xl[:, at], wh[:, cols], start=False, stop=True)

            def turn(i, j):
                pe.wait_ge(S["xn_made"], i * TB + (j + 1))
                if j >= 2:
                    pe.wait_ge(S["xl_made"], i * TB + (j - 1) + 1)
                else:
                    pe.wait_ge(S["xl_made"], i * TB + 1)
                te.transpose(bank[j % 2][:, 0:P], xn[:, j, :], ident[:, :]).then_inc(S["xn_t"], 1)

            def project(i, j):
                pe.wait_ge(S["xl_made"], i * TB + (j + 1) + 1)
                pe.wait_ge(S["sq_done"], 2 * (i * TB + max(j - 1, 0)) + 1)
                three(bank[2 + j % 2][:, 0:NP1], bass.ds(i * 512 + j * P, P), slice(0, NP1)).then_inc(S["proj_mm"], 1)

            with pe.Fori(0, B) as i:
                turn(i, 0)
                for j in range(1, TB):
                    turn(i, j)
                    project(i, j - 1)
                project(i, TB - 1)

            pe.wait_ge(S["om_shift"], 5)
            te.matmul(bank[5][:, 0:TH], upper[:, :], adt[:, 0:TH], start=True, stop=True)
            te.matmul(bank[6][:, 0:TH], ones[:, :], adt[:, 0:TH], start=True, stop=True).then_inc(S["ell_mm"], 1)
            te.matmul(bank[4][:, 0:TH], shift[:, :], omega[:, 0:TH], start=True, stop=False)
            te.matmul(bank[4][:, 0:TH], wrap[:, :], omega[:, NH:TH + NH], start=False, stop=True).then_inc(S["ell_mm"], 1)
            pe.wait_ge(S["small_act"], 5)
            te.transpose(bank[7][:, 0:P], ell[:, 0:TH], ident[:, :]).then_inc(S["ellt_mm"], 1)

            pe.wait_ge(S["route"], R_CHOSEN)
            pe.wait_ge(S["const_made"], 5)
            te.matmul(bank[2][:, 0:T * NE], before[:, :], mm[:, 0:T * NE], start=True, stop=True).then_inc(S["rt_mm"], 1)
            te.matmul(bank[3][:, 0:T * NE], ones[:, :], mm[:, 0:T * NE], start=True, stop=True).then_inc(S["rt_mm"], 1)

            with pe.Fori(0, B) as i:
                pe.wait_ge(S["ang_made"], i + 1)
                pe.wait_ge(S["red4"], i + 1)
                te.matmul(bank[0][:, :], upper[:, :], ang[:, :], start=True, stop=False)
                for k in range(1, TB):
                    m = te.matmul(bank[0][:, k * P:], ones[:, :], ang[:, 0:(TB - k) * P], start=False, stop=(k == TB - 1))
                m.then_inc(S["theta_mm"], 1)

            def zx(at):
                three(bank[0][:, :], at, slice(NP1, NP1 + NP2)).then_inc(S["zx_mm"], 1)

            def turn_kq(par, n):
                pe.wait_ge(S["kq_ready"], n + 1)
                pe.wait_ge(S["kq_first"], n + 1)
                pe.wait_ge(S["qt_copied"], n)
                for q in range(2):
                    for h in range(NH):
                        m = te.transpose(bank[2 + q][:, h * P:(h + 1) * P], kq[:, par, (q * NH + h) * P:(q * NH + h + 1) * P], ident[:, :])
                m.then_inc(S["kq_tr"], 1)

            def scores(n):
                pe.wait_ge(S["kt_copied"], n + 1)
                pe.wait_ge(S["qt_copied"], n + 1)
                pe.wait_ge(S["m_made"], n + 1)
                for h in range(NH):
                    m = te.matmul(bank[4][:, h * P:(h + 1) * P], kqt[:, 0, h * P:(h + 1) * P], kqt[:, 1, h * P:(h + 1) * P], start=True, stop=True)
                m.then_inc(S["s_mm"], 1)

            pe.wait_ge(S["red4"], B + 1)
            pe.wait_ge(S["proj_out"], T)
            zx(slice(0, P))
            turn_kq(0, 0)
            scores(0)
            def recurrence(first, last):
              with pe.Fori(first, last) as i:
                for j in range(TB):
                    par = j % 2
                    t, nxt = i * TB + j, i * TB + (j + 1)
                    pe.wait_ge(S["st_made"], i * 3 + j + 1)
                    if j:
                        pe.wait_ge(S["y_a"], i * 3 + j)
                        for h in range(NH):
                            c = slice(h * HD, (h + 1) * HD)
                            m = te.matmul(bank[1][:, c], kqt[:, 1, h * P:(h + 1) * P], st[:, (j - 1) % 2, c], start=True, stop=True)
                        m.then_inc(S["inter_mm"], 1)
                    if j < 3:
                        pe.wait_ge(S["xw_made"], nxt + 1)
                        for h in range(NH):
                            c = slice(h * HD, (h + 1) * HD)
                            m = te.matmul(bank[6][:, c], kq[:, par, h * P:(h + 1) * P], xw[:, par, c], start=True, stop=True)
                        m.then_inc(S["w_mm"], 1)
                    pe.wait_ge(S["x_copied"], nxt + 1)
                    pe.wait_ge(S["sz_made"], nxt + 1)
                    zx(bass.ds(i * 512 + (j + 1) * P, P))
                    pe.wait_ge(S["m_made"], nxt + 1)
                    pe.wait_ge(S["xg_made"], nxt + 1)
                    pe.wait_ge(S["y_b"], t + 1)
                    for h in range(NH):
                        c = slice(h * HD, (h + 1) * HD)
                        m = te.matmul(bank[5][:, c], mm[:, h * P:(h + 1) * P], xg[:, par, c], start=True, stop=True)
                    m.then_inc(S["intra_mm"], 1)
                    turn_kq(1 - par, nxt)
                    pe.wait_ge(S["y_gated"], nxt)
                    pe.wait_ge(S["out_copied"], t + 1)
                    for c in range(2):
                        m = te.transpose(bank[7][:, c * P:(c + 1) * P], yg[:, c * P:(c + 1) * P], ident[:, :])
                    m.then_inc(S["yt_mm"], 1)
                    scores(nxt)
                    pe.wait_ge(S["yt_copied"], nxt)
                    pe.wait_ge(S["wo_half"], 1)
                    for c in range(2):
                        m = te.matmul(bank[7][:, DI:DI + P], ygt[:, c * P:(c + 1) * P], wo[:, c, :], start=(c == 0), stop=(c == 1))
                    m.then_inc(S["out_mm"], 1)

            recurrence(0, BP1)

            def turn_rows(k, n, load):
                if load is not None:
                    pe.wait_ge(S[f"xg_in{k // 2}"], load)
                if n is not None:
                    pe.wait_ge(S["xg_copied"], n)
                for q in range(2):
                    for t in range(2):
                        at = (q * 2 + t) * P
                        m = te.transpose(turned[:, at:at + P], xgb[:, 2 * k + t, q * P:(q + 1) * P], ident16[:, :])
                m.then_inc(S["x_t"], 1)

            def up(par, n, e):
                pe.wait_ge(S["xg_copied"], n + 1)
                if not isinstance(n, int):
                    pe.wait_ge(S["gelu"], 2 * n - 1)
                for c in range(UC):
                    ps = up_banks[par][c // 2][:, (c % 2) * RB:(c % 2 + 1) * RB]
                    w_hi, w_lo = (w[:, c * P:][:, bass.ds(e, P)] for w in (wu_h, wu_l))
                    te.matmul(ps, w_hi, xgt[:, par, 0, :], start=True, stop=False)
                    te.matmul(ps, w_hi, xgt[:, par, 1, :], start=False, stop=False)
                    m = te.matmul(ps, w_lo, xgt[:, par, 0, :], start=False, stop=True)
                    if c % 2:
                        m.then_inc(S["up_mm"], 1)

            wd_flat = wd.rearrange("p m q n -> p (m q n)")

            def down(par, n, e):
                pe.wait_ge(S["y_copied"], n + 1)
                pe.wait_ge(S["h_lo"], 2 * n + 2)
                e2, e4 = pe.snap(e * 2), pe.snap(e // UC)
                for t in range(2):
                    for c in range(UC):
                        w = wd_flat[:, c * 2 * P:]
                        h, l = (hh[:, par, q, c, t * P:(t + 1) * P] for q in range(2))
                        te.matmul(bank[1][:, t * RB:(t + 1) * RB], h, w[:, bass.ds(e2, 2 * P)], start=(c == 0), stop=False)
                        te.matmul(bank[1][:, t * RB:t * RB + P], l, w[:, bass.ds(e2, P)], start=False, stop=False)
                    m = te.matmul(bank[1][:, t * RB:t * RB + P], sel[:, :], bd[:, bass.ds(e4, P)], start=False, stop=True)
                m.then_inc(S["down_mm"], 1)

            def expert(n):
                return pe.value_load(tile_expert[0:1, n], min_val=0, max_val=(NE - 1) * U)

            pe.wait_ge(S["wx_lo"], 2 * TB)
            pe.wait_ge(S["bd_made"], 7)
            pe.wait_ge(S["ident_low"], 1)
            turn_rows(0, None, 16)
            turn_rows(1, 1, None)
            up(0, 0, expert(slice(0, 1)))
            turn_rows(2, 2, 16)
            up(1, 1, expert(slice(1, 2)))
            with pe.Fori(0, XB // 8) as i:
                es = [expert(bass.ds(i * 8 + k, 1)) for k in range(2)]
                for k in range(8):
                    ahead = k + 3
                    es.append(expert(bass.ds(i * 8 + (k + 2), 1)))
                    turn_rows(ahead % 4, i * 8 + ahead, i * 32 + (ahead // 4 + 1) * 16 if ahead % 2 == 0 else None)
                    down(k % 2, i * 8 + k, es[k])
                    up(k % 2, i * 8 + (k + 2), es[k + 2])
            recurrence(BP1, B)


def kernel(L0_attn_u, L0_attn_W_in, L0_attn_W_out, L0_attn_dt_bias, L0_attn_B_bias, L0_attn_C_bias,
           L0_attn_B_norm_w, L0_attn_C_norm_w, L0_attn_D, L0_ffn_w_router, L0_ffn_w_up, L0_ffn_b_up,
           L0_ffn_w_down, L0_ffn_b_down):
    import numpy as np
    import concourse.bacc as bacc
    from concourse.bass_utils import run_bass_kernel_spmd

    w = np.asarray(L0_attn_W_in)
    z, xx, bg, cg, rest = w[:, :256], w[:, 256:512], w[:, 512:640], w[:, 640:768], w[:, 768:]
    bb, cb = np.asarray(L0_attn_B_bias), np.asarray(L0_attn_C_bias)
    bw, cw = np.asarray(L0_attn_B_norm_w), np.asarray(L0_attn_C_norm_w)
    arrays = {
        "x": np.asarray(L0_attn_u).reshape(B * L, DM),
        "w_in": np.concatenate([bg, cg, rest, np.asarray(L0_ffn_w_router).T, z, xx], axis=1),
        "cols": np.concatenate([bg.T, cg.T, bw[:, None], cw[:, None], bb.T, cb.T], axis=1),
        "rows": np.concatenate([bw, cw, bb.reshape(-1), cb.reshape(-1), np.asarray(L0_attn_dt_bias), np.asarray(L0_attn_D)]),
        "w_out": np.asarray(L0_attn_W_out),
        "w_up": np.asarray(L0_ffn_w_up).transpose(2, 0, 1).reshape(DM, NE * U),
        "b_up": np.asarray(L0_ffn_b_up).reshape(NE, UC, P).transpose(2, 0, 1).reshape(P, NE * UC),
        "w_dn": np.asarray(L0_ffn_w_down).reshape(NE, DM, UC, P).transpose(3, 0, 2, 1).reshape(P, NE * U),
        "b_dn": np.asarray(L0_ffn_b_down).reshape(-1),
    }
    arrays = {k: np.ascontiguousarray(a) for k, a in arrays.items()}
    nc = bacc.Bacc("TRN2", target_bir_lowering=False, num_devices=1)
    args = [nc.dram_tensor(k, a.shape, F32, kind="ExternalInput").ap() for k, a in arrays.items()]
    out = nc.dram_tensor("out", (B * L, DM), F32, kind="ExternalOutput").ap()
    build(nc, *args, out)
    r = run_bass_kernel_spmd(nc, [arrays], core_ids=[0])
    return r.results[0]["out"].reshape(B, L, DM)
```

```python
import math
from contextlib import ExitStack

import concourse.bass as bass
from concourse import mybir

ALU = mybir.AluOpType
ACT = mybir.ActivationFunctionType
AX_X = mybir.AxisListType.X
F32 = mybir.dt.float32
F16 = mybir.dt.float16
I32 = mybir.dt.int32

P = 128
B, L, DM = 8, 512, 128
T = B * L // P
TB = L // P
NH, HD = 4, 64
DI = NH * HD
NA = 32
NE = 8
U = 512
UC = U // P
RB = 2 * P
XB = 2 * B * L // RB + NE
XBPAD = XB + 4
XT, XPAD = XB * RB // P, XBPAD * RB // P
BP1 = 4
EPS = 1e-5
A_FLOOR = 1e-4
C_B, C_C, C_UB, C_UC, C_DT, C_A, C_TRAP, C_ANG, C_RT = 0, 128, 256, 260, 264, 268, 272, 276, 308
NP1 = C_RT + NE
NP2 = 2 * DI
TWO_PI_HI = 6.28125
TWO_PI_LO = 2 * math.pi - TWO_PI_HI
NEVER = -1e30
R_DIFF, R_CHOSEN, R_ALL = 12, 13, 35
ROUND = 1.5 * 2.0 ** 23


def build(nc, x, w_in, cols, rows, w_out, w_up, b_up, w_dn, b_dn, out):
    xv = x.rearrange("(b t p) d -> b p t d", t=TB, p=P)
    ov = out.rearrange("(b t p) d -> b p t d", t=TB, p=P)
    ell_dram = nc.dram_tensor("ell_rows", ((T + TB) * NH, P), F32, kind="Internal").ap()
    xg_dram = nc.dram_tensor("rows_by_expert", (XPAD * P, 2 * P), F16, kind="Internal").ap()
    yg_dram = nc.dram_tensor("results_by_expert", (XT * P, P), F32, kind="Internal").ap()

    with ExitStack() as ctx:
        def sb(name, shape, dt=F32):
            return ctx.enter_context(nc.sbuf_tensor(name, shape, dt))

        def sem(name):
            return ctx.enter_context(nc.semaphore(name))

        bank = [ctx.enter_context(nc.psum_tensor(f"bank{n}", [P, 512], F32)) for n in range(8)]

        ident = sb("ident", [P, P])
        upper = sb("upper", [P, P])
        ones = sb("ones", [P, P])
        shift = sb("shift", [P, P])
        wrap = sb("wrap", [P, P])
        zero4 = sb("zero4", [TB * NH, P])
        before = sb("before", [P, P])
        tile_row = sb("tile_row", [P, XBPAD])
        full_row = sb("full_row", [P, T])
        first_row = sb("first_row", [P, NE])
        rt_m1, rt_m2, rt_k = (sb(n, [P, T]) for n in ("rt_m1", "rt_m2", "rt_k"))
        rt_tiles, rt_end, rt_start = (sb(n, [P, NE]) for n in ("rt_tiles", "rt_end", "rt_start"))
        gate = sb("gate", [P, 2, T])
        slot = sb("slot", [P, T + 2, 2])
        tile_expert = sb("tile_expert", [P, XBPAD], I32)
        tile_bias = sb("tile_bias", [P, XBPAD], I32)
        em = sb("em", [P, 2, NH * P])
        wf = em[:, :, :].rearrange("p a n -> p (a n)")[:, 0:NP1 + NP2]
        wh = sb("wh", [P, NP1 + NP2], F16)
        wl = sb("wl", [P, NP1 + NP2], F16)
        colp = sb("colp", [P, 2 * P + 2 + 2 * NH])
        NROW = 2 * P + 2 * NH * P + NH + NH
        rowp = sb("rowp", [P, NROW])
        wo = sb("wo", [P, 2, P])
        wbt, wct = colp[:, 0:P], colp[:, P:2 * P]
        wn_b, wn_c = colp[:, 256:257], colp[:, 257:258]
        bb_t, cb_t = colp[:, 258:262], colp[:, 262:266]
        nw = rowp[:, 0:2 * P]
        kq_bias = rowp[:, 256:1280]
        dtb_r, d_r = rowp[:, 1280:1284], rowp[:, 1284:1288]
        bias8 = sb("bias8", [P, 2 * NH])
        cross = sb("cross", [P, 3 * NH])
        kappa = sb("kappa", [P, NH])
        x_all = sb("x_all", [P, T * P])
        xh = sb("xh", [P, (T + 1) * P], F16)
        xl = sb("xl", [P, (T + 1) * P], F16)
        proj = sb("proj", [P, (T + 1) * NP1 + 2 * P])
        cs = sb("cs", [P, (T + 1) * 2 * P])
        ao_view = cs[:, 0:T * 2 * P].rearrange("p (t c) -> p t c", c=2 * P)
        stats = sb("stats", [P, T * 6])
        mean, ve, rstd, nmr, ln_t = (sb(n, [P, T]) for n in ("mean", "ve", "rstd", "nmr", "ln_t"))
        ss = sb("ss", [P, 2, T + 2])
        bc0 = sb("bc0", [P, T])
        r_bc = sb("r_bc", [P, 2, T + 2])
        r_t = sb("r_t", [P, 2, T + 2])
        TH = T * NH
        dt_all, adt, beta, omega, gg = (sb(n, [P, TH + NH]) for n in ("dt_all", "adt", "beta", "omega", "gg"))
        ell, expell, ge, coef, cd, nell = (sb(n, [P, TH + NH]) for n in ("ell", "expell", "ge", "coef", "cd", "nell"))
        dece, u1, u2 = (sb(n, [P, TH]) for n in ("dece", "u1", "u2"))
        ellt = sb("ellt", [P, P])
        bu = sb("bu", [P, NE * UC])
        bds = sb("bds", [33, NE * P])
        sel = sb("sel", [P, P], F16)
        sx = sb("sx", [P, 2, 2, 2, P], F16)
        ident16 = sb("ident16", [P, P], F16)
        sidx = sb("sidx", [P, 2, 4], I32)
        junk = sb("junk", [P, 2, P])
        bcn = sb("bcn", [P, 2 * P])
        kq = sb("kq", [P, 2, 2 * NH * P])
        rp = sb("rp", [P, 4, 2 * NH * NA])
        kqt = sb("kqt", [P, 2, NH * P])
        el = sb("el", [P, TB, NH * P])
        ee = sb("ee", [P, 2, NH * P])
        ang, th = (tuple(kq[:, k, q * 512:(q + 1) * 512] for q in range(2)) for k in range(2))
        xn, bw = (ee[:, k, :].rearrange("p (t n) -> p t n", t=TB) for k in range(2))
        v8, e8, s8, q8 = (el[:, k, 0:T * 2 * NH].rearrange("p (t n) -> p t n", t=T) for k in range(4))
        p8 = el[:, 0, 256:512].rearrange("p (t n) -> p t n", t=T)
        mm = sb("mm", [P, NH * P])
        zt = sb("zt", [P, DI])
        xs_raw = sb("xs_raw", [P, 2, DI])
        sz = sb("sz", [P, 2, DI])
        xg = sb("xg", [P, 2, DI])
        xw = sb("xw", [P, 2, DI])
        xc = sb("xc", [P, 2, DI])
        st = sb("st", [P, 2, DI])
        std = sb("std", [P, DI])
        tk0, tk1, ta = (a[:, :, :].rearrange("p a n -> p (a n)") for a in (xg, sz, xw))
        tk = (tk0, tk1)
        zeros = cs[:, 0:4 * P].bitcast(F16)
        x16, p16 = x_all[:, :].bitcast(F16), proj[:, :].bitcast(F16)
        NU = NE * U
        wu_h, wu_l = x16[:, 0:NU], x16[:, NU:2 * NU]
        wd = p16[:, 0:2 * NU].rearrange("p (m q n) -> p m q n", q=2, n=P)
        bd = p16[:, 2 * NU:2 * NU + NE * P]
        x_in2 = proj[:, 0:T * P]
        assert T * P <= BP1 * TB * NP1
        assert (2 * NU + NE * P) * 2 <= BP1 * TB * NP1 * 4 and 4 * NU <= T * P * 4
        xgb = rp[:, :, :].rearrange("p a n -> p (a n)").bitcast(F16).rearrange("p (b n) -> p b n", n=2 * P)
        xgt = sx[:, :, :, :, :].rearrange("p a q t n -> p a q (t n)")
        turned = bank[7][:, 0:RB].bitcast(F16)
        hf = sb("hf", [P, 2, 2 * RB])
        hh = sb("hh", [P, 2, 2, UC, RB], F16)
        yb = kq[:, 1, :].rearrange("p (b n) -> p b n", n=P)
        gb = [hf[:, q, :].rearrange("p (t k n) -> p t k n", t=2, k=2) for q in range(2)]
        hh32 = hh[:, :, :, :, :].rearrange("p a b c n -> p (a b c n)").bitcast(F32)
        stage = [hf[:, :, :].rearrange("p a n -> p (a n)"), hh32[:, 0:1024], hh32[:, 1024:2048], rp[:, :, :].rearrange("p a n -> p (a n)"), kq[:, 1, :]]
        NST = len(stage)
        y1, y2, y3, yg = (sb(n, [P, DI]) for n in ("y1", "y2", "y3", "yg"))
        ygt = sb("ygt", [P, DI])

        S = {n: sem(n) for n in (
            "wf_in", "cols_in", "rows_in", "wo_in", "const_zero", "const_made", "pads",
            "cross_made", "kappa_in", "cross_mm", "cross_copied", "w_hi", "w_lo", "wo_half", "b8",
            "stats_done", "ln_chain", "ln_sqrt", "xn_made", "xn_t", "xh_made", "xl_made",
            "proj_mm", "proj_out", "sq_done", "bc_weighted", "bw_made", "bc0_done",
            "small", "small_act", "om_shift", "ell_mm", "ellt_mm", "ellt_sb", "ell_out", "pad_out",
            "r_sqrt", "ang_made", "theta_mm", "red1", "red2", "red3", "red4", "red5", "sin_made", "abs_made", "cos_made",
            "zx_mm", "z_tanh", "x_copied", "sz_made", "xg_made", "xw_made", "xc_made",
            "b_norm", "kq_biased", "rotated", "kq_first", "kq_ready",
            "kq_tr", "kt_copied", "qt_copied", "s_mm", "e_exp", "e_masked", "m_made",
            "inter_mm", "w_mm", "intra_mm", "st_decayed", "st_made", "y_a", "y_b", "y_c", "y_gated",
            "yt_mm", "yt_copied", "out_mm", "out_copied", "out_sum", "stored", "iotas", "route", "rt_mm", "rt_exp", "xg_zeroed", "zeros", "staged", "xg_in0", "xg_in1",
            "wx_hi", "wx_lo", "bd_in", "bd_made", "bu_in", "x_t", "xg_copied", "up_mm", "gelu", "h_hi", "h_lo",
            "down_mm", "y_lo", "y_copied", "y_out0", "y_out1", "idx_made", "combine1", "combine2", "x_again", "x_added", "rows_made", "go", "primed", "rows_low", "ident_low")}
        scat = [sem(f"scat{n}") for n in range(2)]
        gath = [sem(f"gath{n}") for n in range(2)]
        x_in = [sem(f"x_in{n}") for n in range(B)]
        w_raw = [sem(f"w_raw{n}") for n in range(NST)]
        el_in = [sem(f"el_in{n}") for n in range(TB)]

        block = ctx.enter_context(nc.Block())

        def tok(ap, n):
            return ap.unsqueeze(2).to_broadcast([P, NH, n])

        def heads(ap):
            return ap.rearrange("p (h n) -> p h n", h=NH)

        def by_chunk(ap):
            return ap.rearrange("p (m n) -> p m n", n=P)

        def piece(n, q):
            k = (n % TB) * 8
            return by_chunk((wu_h, wu_l)[q])[:, k:k + 8, :] if n < TB else wd[:, k:k + 8, q, :]

        turn_banks = (bank[0], bank[1], bank[4], bank[5])
        up_banks = ((bank[2], bank[3]), (bank[5], bank[6]))

        @block.sync
        def _(sp):
            sp.dma_start(wf[:, 0:2 * P], w_in[:, 0:2 * P]).then_inc(S["wf_in"], 16)
            sp.dma_start(wf[:, C_DT:], w_in[:, 2 * P:]).then_inc(S["wf_in"], 16)
            for b in range(B):
                sp.dma_start(x_all[:, b * 512:(b + 1) * 512].rearrange("p (t d) -> p t d", t=TB), xv[b]).then_inc(x_in[b], 16)
            sp.wait_ge(S["zeros"], 1)
            sp.dma_start(xg_dram.rearrange("(c p r) d -> p c (r d)", p=P, r=4), zeros.unsqueeze(1).to_broadcast([P, XPAD // 4, 8 * P])
                         ).then_inc(S["xg_zeroed"], 16)
            sp.wait_ge(S["pads"], 1)
            sp.dma_start(ell_dram[TH:TH + TB * NH, :], zero4[:, :]).then_inc(S["pad_out"], 16)
            sp.wait_ge(S["ellt_sb"], 1)
            sp.dma_start(ell_dram[0:TH, :], ellt[:, :]).then_inc(S["ell_out"], 16)
            sp.wait_ge(S["ell_out"], 16)
            sp.wait_ge(S["pad_out"], 16)
            ell_t = ell_dram.rearrange("(t h) p -> t (h p)", h=NH)
            for j in range(TB):
                sp.dma_start(el[:, j, :], ell_t[j, :].partition_broadcast(P)).then_inc(el_in[j], 16)
            def prefetch(first, last):
                with sp.Fori(first, last) as i:
                    for j in range(TB):
                        sp.wait_ge(S["e_masked"], i * TB + (j + 1))
                        sp.dma_start(el[:, j, :], ell_t[bass.ds(i * TB + (TB + j), 1), :].rearrange("o n -> (o n)").partition_broadcast(P)
                                     ).then_inc(el_in[j], 16)

            def load_piece(n):
                src = w_up if n < TB else w_dn
                sp.dma_start(stage[n % NST], src[:, (n % TB) * 1024:(n % TB + 1) * 1024]).then_inc(w_raw[n % NST], 16)

            for n in range(3):
                load_piece(n)
            prefetch(0, BP1)
            for n in range(3, 2 * TB):
                if n < NST:
                    sp.wait_ge(S["intra_mm"], BP1 * TB + 1)
                    sp.wait_ge(S["kq_ready"], BP1 * TB + 1)
                else:
                    sp.wait_ge(S["wx_lo"], n - NST + 1)
                load_piece(n)
            ygv = yg_dram.rearrange("(g t p) d -> g p t d", t=4, p=P)
            xgv = xg_dram.rearrange("(g t p) d -> g p t d", t=4, p=P)
            for k in range(2):
                sp.wait_ge(scat[k], 16 * T + 16)
            sp.wait_ge(S["wx_lo"], 4)
            for g in range(2):
                sp.dma_start(xgb[:, 4 * g:4 * g + 4, :], xgv[g]).then_inc(S[f"xg_in{g}"], 16)

            def load_rows(i, g):
                at = 2 * i + (2 + g)
                src = xgv[at] if isinstance(i, int) else xgv[bass.ds(at, 1)].rearrange("o p t d -> (o p) t d")
                sp.wait_ge(S["x_t"], i * 4 + (2 * g + 2))
                sp.dma_start(xgb[:, 4 * g:4 * g + 4, :], src).then_inc(S[f"xg_in{g}"], 16)

            def store_results(i, g):
                at = 2 * i + g
                dst = ygv[at] if isinstance(i, int) else ygv[bass.ds(at, 1)].rearrange("o p t d -> (o p) t d")
                sp.wait_ge(S["y_copied"], i * 4 + (2 * g + 2 + 1))
                sp.dma_start(dst, yb[:, 4 * g:4 * g + 4, :]).then_inc(S[f"y_out{g}"], 16)

            for g in range(2):
                load_rows(0, g)
            with sp.Fori(1, XB // 4) as i:
                for g in range(2):
                    load_rows(i, g)
                    store_results(i - 1, g)
            for g in range(2):
                store_results(XB // 4 - 1, g)
            sp.wait_ge(S["down_mm"], XB + 2)
            for b in range(B):
                sp.dma_start(x_in2[:, b * 512:(b + 1) * 512].rearrange("p (t d) -> p t d", t=TB), xv[b]).then_inc(S["x_again"], 16)
            prefetch(BP1, B)
            with sp.Fori(0, B) as i:
                sp.wait_ge(S["out_sum"], i + 1)
                sp.dma_start(ov[bass.ds(i, 1)].rearrange("o p t d -> (o p) t d"),
                             ao_view[:, bass.ds(i * TB, TB), 0:P]).then_inc(S["stored"], 16)
            sp.wait_ge(S["stored"], 16 * B)

        @block.gpsimd
        def _(pool):
            pl = nc.gpsimd
            for name in ("xc_made", "y_out0", "y_out1"):
                pool.sem_inc(S[name], 1)
            for name in ("gelu", "y_copied", "rows_low", "y_a"):
                pool.sem_inc(S[name], 1)
            pool.sem_inc(S["down_mm"], 2)
            pool.sem_inc(S["combine2"], 3)
            pl.memset(ident[:, :], 0.0).then_inc(S["const_zero"], 1)
            pl.memset(upper[:, :], 1.0).then_inc(S["const_zero"], 1)
            pl.memset(shift[:, :], 0.0).then_inc(S["const_zero"], 1)
            pl.memset(wrap[:, :], 0.0).then_inc(S["const_zero"], 1)
            pl.memset(ones[:, :], 1.0).then_inc(S["const_zero"], 1)
            pool.wait_ge(S["const_zero"], 5)
            pl.affine_select(out=ident[:, :], in_=ident[:, :], compare_op=ALU.not_equal, fill=1.0, base=0,
                             pattern=[[-1, P]], channel_multiplier=1).then_inc(S["const_made"], 1)
            pl.affine_select(out=upper[:, :], in_=upper[:, :], compare_op=ALU.is_ge, fill=0.0, base=0,
                             pattern=[[1, P]], channel_multiplier=-1).then_inc(S["const_made"], 1)
            pl.affine_select(out=shift[:, :], in_=shift[:, :], compare_op=ALU.not_equal, fill=1.0, base=-1,
                             pattern=[[-1, P]], channel_multiplier=1).then_inc(S["const_made"], 1)
            pl.affine_select(out=wrap[:, :], in_=wrap[:, :], compare_op=ALU.not_equal, fill=1.0, base=-P * (P - 1),
                             pattern=[[P, P]], channel_multiplier=1).then_inc(S["const_made"], 1)
            pl.memset(zeros, 0.0).then_inc(S["zeros"], 1)
            pl.affine_select(out=before[:, :], in_=ones[:, :], compare_op=ALU.is_gt, fill=0.0, base=0,
                             pattern=[[1, P]], channel_multiplier=-1).then_inc(S["const_made"], 1)
            pl.iota(tile_row[:, :], pattern=[[1, XBPAD]], base=0, channel_multiplier=0, allow_small_or_imprecise_dtypes=True).then_inc(S["iotas"], 1)
            pl.iota(full_row[:, :], pattern=[[RB, T]], base=0, channel_multiplier=0, allow_small_or_imprecise_dtypes=True).then_inc(S["iotas"], 1)
            pl.iota(first_row[:, :], pattern=[[-1, NE]], base=NE, channel_multiplier=0, allow_small_or_imprecise_dtypes=True).then_inc(S["iotas"], 1)
            pool.wait_ge(S["const_made"], 5)
            pl.tensor_copy(ident16[:, :], ident[:, :]).then_inc(S["ident_low"], 1)
            pl.memset(sel[:, :], 0.0).then_inc(S["bd_made"], 1)
            pl.memset(bds[:, :], 0.0).then_inc(S["bd_made"], 1)
            pool.wait_ge(S["bd_made"], 2)
            for p in (0, 32):
                pl.memset(sel[p:p + 1, :], 1.0).then_inc(S["bd_made"], 1)
                pool.dma_start(bds[p:p + 1, :], b_dn.rearrange("(o n) -> o n", o=1)).then_inc(S["bd_in"], 16)
            pool.wait_ge(S["bd_made"], 4)
            pl.memset(zero4[:, :], 0.0).then_inc(S["pads"], 1)
            pl.memset(xh[:, T * P:], 0.0).then_inc(S["pads"], 1)
            pl.memset(xl[:, T * P:], 0.0).then_inc(S["pads"], 1)
            pl.memset(proj[:, T * NP1:], 0.0).then_inc(S["pads"], 1)
            pl.memset(cs[:, T * 2 * P:], 0.0).then_inc(S["pads"], 1)
            pl.memset(ss[:, :, T:], 0.0).then_inc(S["pads"], 1)
            pl.memset(slot[:, T:, :], 0.0).then_inc(S["pads"], 1)
            for a in (dt_all, omega, gg, expell, ge, coef, cd, nell):
                pl.memset(a[:, TH:], 0.0).then_inc(S["pads"], 1)
            pool.wait_ge(S["rows_in"], 16)
            with pool.Fori(0, B) as i:
                pv = proj[:, bass.ds(i * (TB * NP1), TB * NP1)].rearrange("p (t n) -> p t n", t=TB)
                pool.wait_ge(S["proj_out"], i * TB + TB)
                pl.tensor_tensor(pv[:, :, 0:2 * P], pv[:, :, 0:2 * P], nw.unsqueeze(1).to_broadcast([P, TB, 2 * P]), ALU.mult).then_inc(S["bc_weighted"], 1)
                pool.wait_ge(S["bc_weighted"], i + 1)
                pool.wait_ge(S["bc0_done"], i + 1)
                pl.tensor_tensor(bw[:, :, :], pv[:, :, C_B:C_B + P], pv[:, :, C_C:C_C + P], ALU.mult).then_inc(S["bw_made"], 1)

            pool.wait_ge(S["small"], 24)
            with pool.Fori(0, B // 2) as i:
                for par in range(2):
                    n = i * 2 + par
                    pool.wait_ge(S["theta_mm"], n + 1)
                    pv = proj[:, bass.ds(n * (TB * NP1), TB * NP1)].rearrange("p (t n) -> p t n", t=TB)
                    for t in range(TB):
                        a = pl.tensor_tensor(ang[par][:, t * P:(t + 1) * P].rearrange("p (h n) -> p h n", h=NH),
                                             pv[:, t, C_ANG:C_ANG + NA].unsqueeze(1).to_broadcast([P, NH, NA]),
                                             tok(dt_all[:, bass.ds(n * (TB * NH) + t * NH, NH)], NA), ALU.mult)
                    a.then_inc(S["ang_made"], 1)

            pool.wait_ge(el_in[0], 16)
            pl.affine_select(out=heads(ee[:, 0, :]), in_=heads(el[:, 0, :]), compare_op=ALU.is_gt,
                             fill=NEVER, base=0, pattern=[[0, NH], [1, P]], channel_multiplier=-1).then_inc(S["e_masked"], 1)

            def recurrence(first, last, moves):
                with pool.Fori(first, last) as i:
                    for j in range(TB):
                        n = i * TB + j
                        if j in (1, 2):
                            pool.wait_ge(S["st_made"], i * 3 + j + 1)
                            pl.tensor_tensor(heads(std[:, :]), heads(st[:, (j - 1) % 2, :]), tok(cd[:, bass.ds(i * (TB * NH) + j * NH, NH)], HD), ALU.mult
                                             ).then_inc(S["st_decayed"], 1)
                        pool.wait_ge(S["e_exp"], n + 1)
                        pool.wait_ge(el_in[(j + 1) % TB], (i + (1 if j < TB - 1 else 2)) * 16)
                        pool.wait_ge(S["x_copied"], i * TB + (j + 1) + 1)
                        pl.tensor_tensor(heads(xc[:, j % 2, :]), heads(xs_raw[:, j % 2, :]), tok(coef[:, bass.ds(i * (TB * NH) + j * NH, NH)], HD), ALU.mult
                                         ).then_inc(S["xc_made"], 1)
                        pl.affine_select(out=heads(ee[:, (j + 1) % 2, :]), in_=heads(el[:, (j + 1) % TB, :]), compare_op=ALU.is_gt,
                                         fill=NEVER, base=0, pattern=[[0, NH], [1, P]], channel_multiplier=-1).then_inc(S["e_masked"], 1)
                        moves(i, j)
                        if first == BP1 and j >= 2:
                            add_input(i, j)

            def send(i, j):
                pool.wait_ge(S["staged"], 2 * (i * TB + (j + 1)))
                pl.tensor_tensor(sx[:, j % 2, :, 1, :], junk[:, :, :], sx[:, j % 2, :, 0, :], ALU.subtract).then_inc(S["rows_low"], 1)
                pool.wait_ge(S["rows_low"], i * TB + (j + 2))
                pool.sem_inc(S["go"], 1)
                for t in range(2):
                    for k in range(2):
                        pool.indirect_dma_start(xg_dram, bass.IndirectOffsetOnAxis(ap=sidx[:, j % 2, 2 * t + k:2 * t + k + 1], axis=0),
                                                sx[:, j % 2, t, :, :].rearrange("p q n -> p (q n)"), None).then_inc(scat[j % 2], 16)

            def fetch_results(par, n):
                pool.wait_ge(S["idx_made"], n + 1)
                pool.wait_ge(S["combine2"], 2 * n + 1)
                pool.sem_inc(S["go"], 1)
                for t in range(2):
                    for k in range(2):
                        pool.indirect_dma_start(gb[par][:, t, k, :], None, yg_dram,
                                                bass.IndirectOffsetOnAxis(ap=sidx[:, par, 2 * t + k:2 * t + k + 1], axis=0)).then_inc(gath[par], 16)

            def fetch(i, j):
                fetch_results((j + 1) % 2, (i - BP1) * TB + (j + 1))

            def add_input(i, j):
                n = (i - BP1) * TB + 2 * (j - 2)
                pool.wait_ge(S["x_again"], 16 * B)
                at = cs[:, bass.ds(n * (2 * P), 4 * P)].rearrange("p (t c) -> p t c", t=2)[:, :, 0:P]
                pl.tensor_tensor(at, at, x_in2[:, bass.ds(n * P, 2 * P)].rearrange("p (t c) -> p t c", t=2), ALU.add).then_inc(S["x_added"], 1)

            pl.memset(sx[:, :, :, :, :], 0.0).then_inc(S["primed"], 1)
            pl.iota(sidx[:, :, 0:1], pattern=[[-P, 2], [1, 1]], base=(XPAD - 1) * P, channel_multiplier=1).then_inc(S["primed"], 1)
            pool.wait_ge(S["primed"], 2)
            pool.wait_ge(S["xg_zeroed"], 16)
            for k in range(2):
                pool.indirect_dma_start(xg_dram, bass.IndirectOffsetOnAxis(ap=sidx[:, k, 0:1], axis=0),
                                        sx[:, k, 0, :, :].rearrange("p q n -> p (q n)"), None).then_inc(scat[k], 16)
            recurrence(0, BP1, send)
            pool.wait_ge(S["bd_in"], 32)
            pool.wait_ge(S["intra_mm"], BP1 * TB + 1)
            for k in range(2):
                pool.wait_ge(scat[k], 16 * T + 16)
            pl.memset(bd, 0.0).then_inc(S["bd_made"], 1)
            pool.wait_ge(S["bd_made"], 5)
            pl.tensor_copy(bd[0:33, :], bds[:, :]).then_inc(S["bd_made"], 1)
            pool.wait_ge(S["bd_made"], 6)
            pl.tensor_tensor(bd[32:33, :], bds[32:33, :], bd[32:33, :], ALU.subtract).then_inc(S["bd_made"], 1)
            for g in range(2):
                pool.wait_ge(S[f"y_out{g}"], 16 * (XT // 8) + 1)
            pool.wait_ge(S["h_lo"], 2 * (XB + 2))
            fetch_results(0, 0)
            recurrence(BP1, B, fetch)
            pool.wait_ge(gath[0], 16 * 4 * (BP1 * TB // 2 + 1))
            pool.wait_ge(S["x_again"], 16 * B)
            pool.wait_ge(S["out_copied"], T + 1)
            for b in range(BP1, B):
                at = ao_view[:, b * TB:(b + 1) * TB, 0:P]
                pl.tensor_tensor(at, at, x_in2[:, b * 512:(b + 1) * 512].rearrange("p (t d) -> p t d", t=TB), ALU.add).then_inc(S["x_added"], 1)

        @block.scalar
        def _(act):
            sc = nc.scalar
            for name in ("sq_done", "cos_made", "e_exp", "out_copied", "x_copied"):
                act.sem_inc(S[name], 1)
            act.sem_inc(S["sin_made"], 2)
            act.sem_inc(S["abs_made"], 2)
            act.dma_start(colp[:, :], cols).then_inc(S["cols_in"], 16)
            act.dma_start(rowp[:, :], rows.partition_broadcast(P)).then_inc(S["rows_in"], 16)
            act.dma_start(wo[:, :, :], w_out.rearrange("(c p) d -> p c d", p=P)).then_inc(S["wo_in"], 16)
            act.dma_start(bu[:, :], b_up).then_inc(S["bu_in"], 16)
            act.wait_ge(S["cross_mm"], 1)
            sc.copy(wf[:, C_UB:C_DT], bank[0][:, 0:2 * NH]).then_inc(S["cross_copied"], 1)
            sc.copy(kappa[:, :], bank[1][:, 0:NH]).then_inc(S["cross_copied"], 1)
            act.wait_ge(S["ln_chain"], 6)
            sc.activation(ln_t[:, :], ve[:, :], ACT.Sqrt).then_inc(S["ln_sqrt"], 1)

            def project_out(i, j):
                act.wait_ge(S["proj_mm"], i * TB + (j + 1))
                ps = bank[2 + j % 2]
                sc.copy(proj[:, bass.ds(i * (TB * NP1) + j * NP1, NP1)], ps[:, 0:NP1]).then_inc(S["proj_out"], 1)
                act.wait_ge(S["sq_done"], 2 * (i * TB + j) + 1)
                for c in range(2):
                    sc.activation(junk[:, c, :], ps[:, c * P:(c + 1) * P], ACT.Square,
                                  accum_out=ss[:, c, bass.ds(i * TB + j, 1)]).then_inc(S["sq_done"], 1)

            with act.Fori(0, B) as i:
                for j in range(TB):
                    project_out(i, j)

            act.wait_ge(S["small"], 2)
            sc.activation(r_t[:, :, :], ss[:, :, :], ACT.Sqrt).then_inc(S["small_act"], 1)
            act.wait_ge(S["small"], 4)
            sc.activation(e8[:, :, :], q8[:, :, :], ACT.Exp).then_inc(S["small_act"], 1)
            pr = proj[:, 0:T * NP1].rearrange("p (t n) -> p t n", t=T)
            trap = pr[:, :, C_TRAP:C_TRAP + NH]
            sc.activation(beta[:, 0:TH].rearrange("p (t h) -> p t h", h=NH), trap, ACT.Exp, scale=-1.0).then_inc(S["small_act"], 1)
            sc.activation(omega[:, 0:TH].rearrange("p (t h) -> p t h", h=NH), trap, ACT.Exp).then_inc(S["small_act"], 1)
            act.wait_ge(S["ell_mm"], 1)
            sc.copy(ell[:, 0:TH], bank[5][:, 0:TH]).then_inc(S["small_act"], 1)
            sc.activation(expell[:, 0:TH], bank[5][:, 0:TH], ACT.Exp).then_inc(S["small_act"], 1)
            sc.mul(nell[:, 0:TH], bank[5][:, 0:TH], -1.0).then_inc(S["small_act"], 1)
            sc.activation(cd[:, 0:TH], bank[6][:, 0:TH], ACT.Exp).then_inc(S["small_act"], 1)
            act.wait_ge(S["ellt_mm"], 1)
            sc.copy(ellt[:, :], bank[7][:, 0:P]).then_inc(S["ellt_sb"], 1)
            act.wait_ge(S["small"], 25)
            sc.activation(dece[:, :], dece[:, :], ACT.Exp).then_inc(S["small_act"], 1)

            act.wait_ge(S["route"], R_DIFF)
            sc.activation(rt_m2[:, :], rt_m2[:, :], ACT.Exp).then_inc(S["rt_exp"], 1)

            act.wait_ge(S["xg_zeroed"], 16)
            def turns(par, n):
                act.wait_ge(S["theta_mm"], n + 3)
                act.wait_ge(S["red4"], n + 1)
                sc.activation(tk[par], bank[par][:, :], ACT.Identity, bias=ROUND, scale=1.0 / (2 * math.pi)).then_inc(S["red1"], 1)

            def sine_cosine(par, n):
                act.wait_ge(S["red5"], n + 1)
                cv = cs[:, bass.ds(n * (TB * 2 * P), TB * 2 * P)].rearrange("p (t c n) -> p t c n", t=TB, c=2)
                sc.activation(cv[:, :, 1, :], th[par].rearrange("p (t n) -> p t n", t=TB), ACT.Sin).then_inc(S["sin_made"], 1)
                act.wait_ge(S["cos_made"], n + 1)
                sc.activation(ta[:, :], th[par], ACT.Abs).then_inc(S["abs_made"], 1)
                act.wait_ge(S["abs_made"], n + 3)
                sc.activation(cv[:, :, 0, :], ta[:, :].rearrange("p (t n) -> p t n", t=TB), ACT.Sin, bias=math.pi / 2, scale=-1.0).then_inc(S["cos_made"], 1)

            turns(0, 0)
            turns(1, 1)
            with act.Fori(0, B // 2 - 1) as i:
                for par in range(2):
                    sine_cosine(par, i * 2 + par)
                    turns(par, i * 2 + (par + 2))
            for par in range(2):
                sine_cosine(par, B - 2 + par)

            def exps(par, col):
                for h in range(NH):
                    e = sc.activation(em[:, par, h * P:(h + 1) * P], ee[:, par, h * P:(h + 1) * P], ACT.Exp, bias=nell[:, col(h)])
                e.then_inc(S["e_exp"], 1)

            def norms(at, rb, rc):
                sc.activation(bcn[:, 0:P], proj[:, at(C_B)], ACT.Copy, scale=rb)
                sc.activation(bcn[:, P:], proj[:, at(C_C)], ACT.Copy, scale=rc).then_inc(S["b_norm"], 1)

            def zx_out(par, n):
                act.wait_ge(S["zx_mm"], n + 1)
                ps = bank[0]
                sc.activation(zt[:, :], ps[:, 0:DI], ACT.Tanh, scale=0.5).then_inc(S["z_tanh"], 1)
                sc.copy(xs_raw[:, par, :], ps[:, DI:2 * DI]).then_inc(S["x_copied"], 1)

            def kq_out(n):
                act.wait_ge(S["kq_tr"], n + 1)
                sc.copy(kqt[:, 0, :], bank[2][:, :]).then_inc(S["kt_copied"], 1)
                sc.copy(kqt[:, 1, :], bank[3][:, :]).then_inc(S["qt_copied"], 1)

            act.wait_ge(S["small"], 40)
            norms(lambda c: slice(c, c + P), r_bc[:, 0, 0:1], r_bc[:, 1, 0:1])
            act.wait_ge(S["e_masked"], 1)
            act.wait_ge(S["route"], R_ALL)
            exps(0, lambda h: slice(h, h + 1))
            zx_out(0, 0)
            kq_out(0)
            act.wait_ge(S["kq_biased"], 2)
            norms(lambda c: slice(NP1 + c, NP1 + c + P), r_bc[:, 0, 1:2], r_bc[:, 1, 1:2])
            def recurrence(first, last, moves):
              with act.Fori(first, last) as i:
                for j in range(TB):
                    t, nxt = i * TB + j, i * TB + (j + 1)
                    if j:
                        act.wait_ge(S["inter_mm"], i * 3 + j)
                        act.wait_ge(S["y_b"], t + 1)
                        for h in range(NH):
                            c = slice(h * HD, (h + 1) * HD)
                            a = sc.activation(y1[:, c], bank[1][:, c], ACT.Copy, scale=expell[:, bass.ds(i * (TB * NH) + (j * NH + h), 1)])
                        a.then_inc(S["y_a"], 1)
                    moves(i, j)
                    act.wait_ge(S["sz_made"], nxt + 1)
                    act.wait_ge(S["xg_made"], t + 1)
                    act.wait_ge(S["xw_made"], t + 1)
                    act.wait_ge(S["xc_made"], t + 1)
                    zx_out((j + 1) % 2, nxt)
                    act.wait_ge(S["kq_biased"], 2 * nxt + 2)
                    norms(lambda c: bass.ds(i * (TB * NP1) + ((j + 2) * NP1 + c), P), r_bc[:, 0, bass.ds(nxt + 1, 1)], r_bc[:, 1, bass.ds(nxt + 1, 1)])
                    act.wait_ge(S["s_mm"], nxt)
                    kq_out(nxt)
                    act.wait_ge(S["yt_mm"], nxt + 1)
                    sc.copy(ygt[:, :], bank[7][:, 0:DI]).then_inc(S["yt_copied"], 1)
                    act.wait_ge(S["e_masked"], i * TB + (j + 2))
                    act.wait_ge(S["m_made"], t + 1)
                    exps((j + 1) % 2, lambda h: bass.ds(i * (TB * NH) + ((j + 1) * NH + h), 1))
                    act.wait_ge(S["out_mm"], nxt)
                    sc.copy(cs[:, bass.ds(i * (TB * 2 * P) + j * 2 * P, P)], bank[7][:, DI:DI + P]).then_inc(S["out_copied"], 1)

            def stage_rows(i, j):
                act.wait_ge(scat[j % 2], i * 128 + (64 * (j // 2) + 16))
                act.wait_ge(S["rows_low"], i * TB + (j + 1))
                for t in range(2):
                    n = i * 8 + (2 * j + t)
                    sc.activation(junk[:, t, :], x_all[:, bass.ds(n * P, P)], ACT.Identity,
                                  bias=nmr[:, bass.ds(n, 1)], scale=rstd[:, bass.ds(n, 1)]).then_inc(S["rows_made"], 1)
                act.wait_ge(S["rows_made"], i * 8 + (2 * j + 2))
                sc.copy(sx[:, j % 2, :, 0, :], junk[:, :, :]).then_inc(S["staged"], 1)
                sc.copy(sidx[:, j % 2, :], slot[:, :, :].rearrange("p t k -> p (t k)")[:, bass.ds(i * 16 + j * 4, 4)]).then_inc(S["staged"], 1)

            def places(par, n, at):
                act.wait_ge(S["combine2"], 2 * n + 1)
                sc.copy(sidx[:, par, :], slot[:, :, :].rearrange("p t k -> p (t k)")[:, at]).then_inc(S["idx_made"], 1)

            def stage_places(i, j):
                i = i - BP1
                act.wait_ge(gath[j % 2], i * 128 + (64 * (j // 2) + 64))
                for t in range(2):
                    n = i * 8 + (2 * j + t)
                    sc.activation(x_all[:, bass.ds(n * P, P)], gb[j % 2][:, t, 0, :], ACT.Copy, scale=gate[:, 0, bass.ds(n, 1)]).then_inc(S["combine1"], 1)
                places((j + 1) % 2, i * TB + (j + 1), bass.ds(i * 16 + (j + 1) * 4, 4))

            recurrence(0, BP1, stage_rows)

            for k in range(2):
                act.wait_ge(scat[k], 16 * T + 16)
            for n in range(2 * TB):
                act.wait_ge(w_raw[n % NST], 16 * (n // NST + 1))
                sc.copy(piece(n, 0), by_chunk(stage[n % NST])).then_inc(S["wx_hi"], 1)

            def copy_rows(par, n):
                act.wait_ge(S["x_t"], n + 1)
                sc.copy(xgt[:, par, :, :], turned.rearrange("p (q n) -> p q n", q=2)).then_inc(S["xg_copied"], 1)

            def gelus(par, n, b):
                for half in range(2):
                    act.wait_ge(S["up_mm"], 2 * n + (half + 1))
                    if not (isinstance(n, int) and n == 0):
                        act.wait_ge(S["h_lo"], 2 * n + (half - 1))
                    for c in range(UC // 2):
                        g = sc.activation(hf[:, half, c * RB:(c + 1) * RB], up_banks[par][half][:, c * RB:(c + 1) * RB], ACT.Gelu,
                                          bias=bu[:, 2 * half + c:][:, bass.ds(b, 1)])
                    g.then_inc(S["gelu"], 1)

            act.wait_ge(S["bu_in"], 16)
            act.wait_ge(S["wx_lo"], 2 * TB)
            def bias_at(n):
                return act.value_load(tile_bias[0:1, n], min_val=0, max_val=(NE - 1) * UC)

            copy_rows(0, 0)
            copy_rows(1, 1)
            gelus(0, 0, bias_at(slice(0, 1)))
            copy_rows(0, 2)
            gelus(1, 1, bias_at(slice(1, 2)))
            with act.Fori(0, XB // 8) as i:
                for k in range(8):
                    copy_rows((k + 1) % 2, i * 8 + (k + 3))
                    at = bias_at(bass.ds(i * 8 + (k + 2), 1))
                    act.wait_ge(S["down_mm"], i * 8 + (k + 3))
                    sc.copy(y1[:, :].rearrange("p (t n) -> p t n", t=2), bank[1][:, :].rearrange("p (t q n) -> p t q n", t=2, q=2)[:, :, 1, :]).then_inc(S["y_lo"], 1)
                    gelus(k % 2, i * 8 + (k + 2), at)
            places(0, 0, slice(0, 4))
            recurrence(BP1, B, stage_places)

        @block.vector
        def _(dve):
            v = nc.vector
            for name in ("bc0_done", "m_made", "y_b", "st_made", "sz_made", "xg_made", "xw_made"):
                dve.sem_inc(S[name], 1)
            dve.sem_inc(S["red3"], 2)
            dve.sem_inc(S["red4"], 2)
            dve.sem_inc(S["xl_made"], TB)
            dve.wait_ge(S["cols_in"], 16)
            v.tensor_scalar(cross[:, 0:NH], cb_t, wn_b, None, ALU.mult).then_inc(S["cross_made"], 1)
            v.tensor_scalar(cross[:, NH:2 * NH], bb_t, wn_c, None, ALU.mult).then_inc(S["cross_made"], 1)
            v.tensor_tensor(cross[:, 2 * NH:], bb_t, cb_t, ALU.mult).then_inc(S["cross_made"], 1)
            dve.wait_ge(S["wf_in"], 32)
            dve.wait_ge(S["cross_copied"], 1)
            v.tensor_copy(wh[:, :], wf[:, :]).then_inc(S["w_hi"], 1)
            dve.wait_ge(S["w_hi"], 1)
            v.tensor_tensor(wl[:, :], wf[:, :], wh[:, :], ALU.subtract).then_inc(S["w_lo"], 1)
            dve.wait_ge(S["rows_in"], 16)
            v.memset(bias8[:, NH:], 0.0).then_inc(S["b8"], 1)
            v.tensor_copy(bias8[:, 0:NH], dtb_r).then_inc(S["b8"], 1)
            dve.wait_ge(S["wo_in"], 16)
            v.tensor_scalar(wo[:, :, :], wo[:, :, :], 0.5, None, ALU.mult).then_inc(S["wo_half"], 1)

            for t in range(T):
                if t % TB == 0:
                    dve.wait_ge(x_in[t // TB], 16)
                v.bn_stats(stats[:, t * 6:(t + 1) * 6], x_all[:, t * P:(t + 1) * P]).then_inc(S["stats_done"], 1)
            dve.wait_ge(S["stats_done"], T)
            sv = stats[:, :].rearrange("p (t s) -> p t s", s=6)
            me, mo, ve2, vo2 = (sv[:, :, k] for k in (1, 4, 2, 5))
            v.tensor_tensor(mean[:, :], me, mo, ALU.add).then_inc(S["ln_chain"], 1)
            v.tensor_tensor(nmr[:, :], me, mo, ALU.subtract).then_inc(S["ln_chain"], 1)
            v.tensor_tensor(ve[:, :], ve2, vo2, ALU.add).then_inc(S["ln_chain"], 1)
            dve.wait_ge(S["ln_chain"], 3)
            v.scalar_tensor_tensor(out=ln_t[:, :], in0=nmr[:, :], scalar=0.25, in1=nmr[:, :], op0=ALU.mult, op1=ALU.mult).then_inc(S["ln_chain"], 1)
            dve.wait_ge(S["ln_chain"], 4)
            v.scalar_tensor_tensor(out=ve[:, :], in0=ve[:, :], scalar=1.0 / DM, in1=ln_t[:, :], op0=ALU.mult, op1=ALU.add).then_inc(S["ln_chain"], 1)
            dve.wait_ge(S["ln_chain"], 5)
            v.tensor_scalar(ve[:, :], ve[:, :], EPS, None, ALU.add).then_inc(S["ln_chain"], 1)
            dve.wait_ge(S["ln_sqrt"], 1)
            v.reciprocal(rstd[:, :], ln_t[:, :]).then_inc(S["ln_chain"], 1)
            dve.wait_ge(S["ln_chain"], 7)
            v.tensor_tensor(ln_t[:, :], rstd[:, :], rstd[:, :], ALU.mult).then_inc(S["ln_chain"], 1)
            dve.wait_ge(S["ln_chain"], 8)
            v.tensor_tensor(ln_t[:, :], ln_t[:, :], ve[:, :], ALU.mult).then_inc(S["ln_chain"], 1)
            dve.wait_ge(S["ln_chain"], 9)
            v.tensor_scalar(ln_t[:, :], ln_t[:, :], -0.5, 1.5, ALU.mult, ALU.add).then_inc(S["ln_chain"], 1)
            dve.wait_ge(S["ln_chain"], 10)
            v.tensor_tensor(rstd[:, :], rstd[:, :], ln_t[:, :], ALU.mult).then_inc(S["ln_chain"], 1)
            dve.wait_ge(S["ln_chain"], 11)
            v.scalar_tensor_tensor(out=nmr[:, :], in0=mean[:, :], scalar=-0.5, in1=rstd[:, :], op0=ALU.mult, op1=ALU.mult).then_inc(S["ln_chain"], 1)
            dve.wait_ge(S["ln_chain"], 12)

            def normalise(i, j):
                v.tensor_scalar(xn[:, j, :], x_all[:, bass.ds(i * 512 + j * P, P)], rstd[:, bass.ds(i * TB + j, 1)], nmr[:, bass.ds(i * TB + j, 1)],
                                ALU.mult, ALU.add).then_inc(S["xn_made"], 1)

            def high(i, j):
                dve.wait_ge(S["xn_t"], i * TB + (j + 1))
                v.tensor_copy(xh[:, bass.ds(i * 512 + j * P, P)], turn_banks[j][:, 0:P]).then_inc(S["xh_made"], 1)

            def low(i, j):
                dve.wait_ge(S["xh_made"], i * TB + (j + 1))
                at = bass.ds(i * 512 + j * P, P)
                v.tensor_tensor(xl[:, at], turn_banks[j][:, 0:P], xh[:, at], ALU.subtract).then_inc(S["xl_made"], 1)

            def products(i):
                dve.wait_ge(S["bw_made"], i + 1)
                v.tensor_reduce(bc0[:, bass.ds(i * TB, TB)], bw[:, :, :], AX_X, ALU.add).then_inc(S["bc0_done"], 1)

            def sequence(i):
                for j in range(TB):
                    high(i, j)
                    if not isinstance(i, int) or i == 0 or j < TB - 2:
                        normalise(i + (j + 2) // TB, (j + 2) % TB)
                    low(i, j)
                if not (isinstance(i, int) and i == 0):
                    products(i - 1)

            normalise(0, 0)
            normalise(0, 1)
            sequence(0)
            with dve.Fori(1, B - 1) as i:
                sequence(i)
            sequence(B - 1)
            products(B - 1)

            count = [0]

            def step(ins):
                ins.then_inc(S["small"], 1)
                count[0] += 1
                return count[0]

            def after(n):
                dve.wait_ge(S["small"], n)

            dve.wait_ge(S["pads"], 15)
            dve.wait_ge(S["b8"], 2)
            dve.wait_ge(S["sq_done"], 2 * T + 1)
            pr = proj[:, 0:T * NP1].rearrange("p (t n) -> p t n", t=T)
            n = step(v.tensor_scalar(ss[:, :, :], ss[:, :, :], 1.0 / P, EPS, ALU.mult, ALU.add))
            n = step(v.tensor_tensor(v8[:, :, :], pr[:, :, C_DT:C_DT + 2 * NH], bias8[:, :].unsqueeze(1).to_broadcast([P, T, 2 * NH]), ALU.add))
            after(2)
            n = step(v.scalar_tensor_tensor(out=q8[:, :, :], in0=v8[:, :, :], scalar=-1.0, in1=v8[:, :, :], op0=ALU.mult, op1=ALU.min))
            n = step(v.tensor_scalar(v8[:, :, :], v8[:, :, :], 0.0, None, ALU.max))
            dve.wait_ge(S["small_act"], 1)
            n = step(v.reciprocal(r_bc[:, :, :], r_t[:, :, :]))
            after(n)
            n = step(v.tensor_tensor(r_t[:, :, :], r_bc[:, :, :], r_bc[:, :, :], ALU.mult))
            after(n)
            n = step(v.tensor_tensor(r_t[:, :, :], r_t[:, :, :], ss[:, :, :], ALU.mult))
            after(n)
            n = step(v.tensor_scalar(r_t[:, :, :], r_t[:, :, :], -0.5, 1.5, ALU.mult, ALU.add))
            after(n)
            n = step(v.tensor_tensor(r_bc[:, :, :], r_bc[:, :, :], r_t[:, :, :], ALU.mult))
            dve.wait_ge(S["small_act"], 2)
            n = step(v.tensor_scalar(s8[:, :, :], e8[:, :, :], 2.0, None, ALU.add))
            after(n)
            n = step(v.reciprocal(s8[:, :, :], s8[:, :, :]))
            after(n)
            n = step(v.tensor_tensor(s8[:, :, :], s8[:, :, :], e8[:, :, :], ALU.mult))
            after(n)
            n = step(v.tensor_tensor(e8[:, :, :], s8[:, :, :], s8[:, :, :], ALU.mult))
            after(n)
            n = step(v.tensor_scalar(p8[:, :, :], e8[:, :, :], 1.0 / 15, None, ALU.mult))
            for k in (13, 11, 9, 7, 5, 3):
                after(n)
                n = step(v.scalar_tensor_tensor(out=p8[:, :, :], in0=p8[:, :, :], scalar=1.0 / k, in1=e8[:, :, :], op0=ALU.add, op1=ALU.mult))
            after(n)
            n = step(v.scalar_tensor_tensor(out=p8[:, :, :], in0=p8[:, :, :], scalar=1.0, in1=s8[:, :, :], op0=ALU.add, op1=ALU.mult))
            after(n)
            n = step(v.scalar_tensor_tensor(out=q8[:, :, :], in0=p8[:, :, :], scalar=2.0, in1=v8[:, :, :], op0=ALU.mult, op1=ALU.add))
            after(n)
            dtv = dt_all[:, 0:TH].rearrange("p (t h) -> p t h", h=NH)
            n = step(v.tensor_copy(dtv, q8[:, :, 0:NH]))
            n = step(v.tensor_scalar(q8[:, :, NH:], q8[:, :, NH:], A_FLOOR, -1.0, ALU.max, ALU.mult))
            after(24)
            v.tensor_tensor(adt[:, 0:TH].rearrange("p (t h) -> p t h", h=NH), q8[:, :, NH:], dtv, ALU.mult).then_inc(S["om_shift"], 1)
            dve.wait_ge(S["small_act"], 4)
            v.tensor_scalar(beta[:, 0:TH], beta[:, 0:TH], 1.0, None, ALU.add).then_inc(S["om_shift"], 1)
            v.tensor_scalar(omega[:, 0:TH], omega[:, 0:TH], 1.0, None, ALU.add).then_inc(S["om_shift"], 1)
            dve.wait_ge(S["om_shift"], 3)
            v.reciprocal(beta[:, 0:TH], beta[:, 0:TH]).then_inc(S["om_shift"], 1)
            v.reciprocal(omega[:, 0:TH], omega[:, 0:TH]).then_inc(S["om_shift"], 1)
            dve.wait_ge(S["small_act"], 8)
            n = step(v.tensor_tensor(dece[:, :], bank[6][:, 0:TH], ell[:, 0:TH], ALU.subtract))
            dve.wait_ge(S["ell_mm"], 2)
            n = step(v.tensor_tensor(gg[:, 0:TH], bank[4][:, 0:TH], beta[:, 0:TH], ALU.add))
            after(n)
            n = step(v.tensor_tensor(gg[:, 0:TH], gg[:, 0:TH], dt_all[:, 0:TH], ALU.mult))
            n = step(v.tensor_tensor(beta[:, 0:TH], beta[:, 0:TH], dt_all[:, 0:TH], ALU.mult))
            ub = pr[:, :, C_UB:C_UB + NH]
            uc = pr[:, :, C_UC:C_UC + NH]
            u1v, u2v = (a[:, :].rearrange("p (t h) -> p t h", h=NH) for a in (u1, u2))

            def per_tile(ap):
                return ap.unsqueeze(2).to_broadcast([P, T, NH])

            n = step(v.tensor_tensor(u1v, ub, per_tile(r_bc[:, 0, 0:T]), ALU.mult))
            n = step(v.tensor_tensor(u2v, uc, per_tile(r_bc[:, 1, 0:T]), ALU.mult))
            n = step(v.tensor_tensor(bc0[:, :], bc0[:, :], r_bc[:, 0, 0:T], ALU.mult))
            after(n)
            n = step(v.tensor_tensor(bc0[:, :], bc0[:, :], r_bc[:, 1, 0:T], ALU.mult))
            n = step(v.tensor_tensor(u1[:, :], u1[:, :], u2[:, :], ALU.add))
            after(n)
            n = step(v.tensor_tensor(u1v, u1v, per_tile(bc0[:, :]), ALU.add))
            dve.wait_ge(S["cross_copied"], 2)
            after(n)
            n = step(v.tensor_tensor(u1v, u1v, kappa[:, :].unsqueeze(1).to_broadcast([P, T, NH]), ALU.add))
            after(n)
            n = step(v.tensor_tensor(u1[:, :], u1[:, :], beta[:, 0:TH], ALU.mult))
            after(n)
            n = step(v.tensor_tensor(coef[:, 0:TH].rearrange("p (t h) -> p t h", h=NH), u1v, d_r.unsqueeze(1).to_broadcast([P, T, NH]), ALU.add))
            dve.wait_ge(S["small_act"], 9)
            n = step(v.tensor_tensor(ge[:, 0:TH], gg[:, 0:TH], dece[:, :], ALU.mult))
            after(n)
            n = step(v.memset(ta[:, 0:1], 0.0))
            n = step(v.memset(tk1[:, 0:1], 0.0))
            assert n == 40

            lg = pr[:, :, C_RT:C_RT + NE]
            oh1, oh2, lg2, tmp = (em[:, k // 2, (k % 2) * 256:(k % 2 + 1) * 256].rearrange("p (t e) -> p t e", e=NE) for k in range(4))
            chosen = mm[:, 0:T * NE]
            cnt, upto, reset = y1, y2, y3
            rcount = [0]

            def rstep(ins):
                ins.then_inc(S["route"], 1)
                rcount[0] += 1
                dve.wait_ge(S["route"], rcount[0])

            def by_tile(ap):
                return ap.unsqueeze(2).to_broadcast([P, T, NE])

            def by_expert(ap):
                return ap.unsqueeze(1).to_broadcast([P, T, NE])

            def top(logits, m, oh):
                rstep(v.tensor_reduce(m, logits, AX_X, ALU.max))
                rstep(v.tensor_tensor(tmp, logits, by_tile(m), ALU.is_equal))
                rstep(v.tensor_tensor(tmp, tmp, by_expert(first_row[:, :]), ALU.mult))
                rstep(v.tensor_reduce(rt_k[:, :], tmp, AX_X, ALU.max))
                rstep(v.tensor_tensor(oh, by_tile(rt_k[:, :]), by_expert(first_row[:, :]), ALU.is_equal))

            dve.wait_ge(S["iotas"], 3)
            top(lg, rt_m1[:, :], oh1)
            rstep(v.scalar_tensor_tensor(out=lg2, in0=oh1, scalar=NEVER, in1=lg, op0=ALU.mult, op1=ALU.add))
            top(lg2, rt_m2[:, :], oh2)
            rstep(v.tensor_tensor(rt_m2[:, :], rt_m2[:, :], rt_m1[:, :], ALU.subtract))
            assert rcount[0] == R_DIFF
            rstep(v.tensor_tensor(chosen.rearrange("p (t e) -> p t e", e=NE), oh1, oh2, ALU.add))
            assert rcount[0] == R_CHOSEN
            dve.wait_ge(S["rt_exp"], 1)
            rstep(v.tensor_scalar(rt_m1[:, :], rt_m2[:, :], 1.0, None, ALU.add))
            rstep(v.reciprocal(gate[:, 0, :], rt_m1[:, :]))
            rstep(v.tensor_tensor(gate[:, 1, :], gate[:, 0, :], rt_m2[:, :], ALU.mult))
            rstep(v.memset(reset[:, :], 1.0))
            rstep(v.memset(reset[:, 0:T * NE].rearrange("p (e t) -> p e t", e=NE)[:, :, 0:1], 0.0))
            dve.wait_ge(S["rt_mm"], 2)
            et = cnt[:, :].rearrange("p (e t) -> p e t", e=NE)
            rstep(v.tensor_copy(et, bank[3][:, 0:T * NE].rearrange("p (t e) -> p e t", e=NE)))
            rstep(v.tensor_tensor_scan(upto[:, :], reset[:, :], cnt[:, :], 0.0, ALU.mult, ALU.add))
            ut = upto[:, :].rearrange("p (e t) -> p e t", e=NE)
            rstep(v.tensor_tensor(tmp.rearrange("p t e -> p (t e)").rearrange("p (e t) -> p e t", e=NE), ut[:, :, T - 1:T].to_broadcast([P, NE, T]),
                                  full_row[:, :].unsqueeze(1).to_broadcast([P, NE, T]), ALU.is_gt))
            rstep(v.tensor_reduce(rt_tiles[:, :], tmp.rearrange("p t e -> p (t e)").rearrange("p (e t) -> p e t", e=NE), AX_X, ALU.add))
            rstep(v.tensor_tensor_scan(rt_end[:, :], ones[:, 0:NE], rt_tiles[:, :], 0.0, ALU.mult, ALU.add))
            rstep(v.tensor_tensor(rt_start[:, :], rt_end[:, :], rt_tiles[:, :], ALU.subtract))
            te_ = rp[:, :, :].rearrange("p a n -> p (a n)")[:, 0:XBPAD * NE].rearrange("p (s e) -> p s e", e=NE)
            rstep(v.tensor_tensor(te_, tile_row[:, :].unsqueeze(2).to_broadcast([P, XBPAD, NE]), rt_end[:, :].unsqueeze(1).to_broadcast([P, XBPAD, NE]), ALU.is_ge))
            ts_ = rp[:, :, :].rearrange("p a n -> p (a n)")[:, XBPAD * NE:XBPAD * (NE + 1)]
            rstep(v.tensor_reduce(ts_, te_, AX_X, ALU.add))
            rstep(v.tensor_scalar(tile_expert[:, :], ts_, NE - 1.0, float(U), ALU.min, ALU.mult))
            rstep(v.tensor_scalar(tile_bias[:, :], ts_, NE - 1.0, float(UC), ALU.min, ALU.mult))
            rstep(v.tensor_tensor(cnt[:, :], upto[:, :], cnt[:, :], ALU.subtract))
            rstep(v.scalar_tensor_tensor(out=et, in0=rt_start[:, :].unsqueeze(2).to_broadcast([P, NE, T]), scalar=float(RB), in1=et, op0=ALU.mult, op1=ALU.add))
            rstep(v.tensor_tensor(lg2, bank[2][:, 0:T * NE].rearrange("p (t e) -> p t e", e=NE), cnt[:, :].rearrange("p (e t) -> p t e", e=NE), ALU.add))
            for k, oh in enumerate((oh1, oh2)):
                rstep(v.tensor_tensor(tmp, oh, lg2, ALU.mult))
                rstep(v.tensor_reduce(slot[:, 0:T, k], tmp, AX_X, ALU.add))
            assert rcount[0] == R_ALL, rcount

            with dve.Fori(0, B // 2) as i:
                for par in range(2):
                    n = i * 2 + par
                    dve.wait_ge(S["red1"], n + 1)
                    v.tensor_scalar(tk[par], tk[par], ROUND, None, ALU.subtract).then_inc(S["red2"], 1)
                    dve.wait_ge(S["red2"], n + 1)
                    dve.wait_ge(S["sin_made"], n + 1)
                    dve.wait_ge(S["abs_made"], n + 1)
                    v.scalar_tensor_tensor(out=th[par], in0=tk[par], scalar=-TWO_PI_HI, in1=bank[par][:, :], op0=ALU.mult, op1=ALU.add).then_inc(S["red3"], 1)
                    dve.wait_ge(S["red3"], n + 3)
                    v.scalar_tensor_tensor(out=th[par], in0=tk[par], scalar=-TWO_PI_LO, in1=th[par], op0=ALU.mult, op1=ALU.add).then_inc(S["red4"], 1)
                    dve.wait_ge(S["red4"], n + 3)
                    v.tensor_scalar(th[par], th[par], math.pi, -math.pi, ALU.min, ALU.max).then_inc(S["red5"], 1)

            def add_bias(par, n):
                dve.wait_ge(S["b_norm"], n + 1)
                k4 = kq[:, par, :].rearrange("p (q h n) -> p q h n", q=2, h=NH)
                b4 = kq_bias.rearrange("p (q h n) -> p q h n", q=2, h=NH)
                for q in range(2):
                    s = v.tensor_tensor(k4[:, q], bcn[:, q * P:(q + 1) * P].unsqueeze(1).to_broadcast([P, NH, P]), b4[:, q], ALU.add)
                    s.then_inc(S["kq_biased"], 1)

            def rotate(ct, par, n):
                cv = cs[:, ct].rearrange("p (c n) -> p c n", c=2)
                k4 = kq[:, par, :].rearrange("p (q h n) -> p q h n", q=2, h=NH)
                dve.wait_ge(S["kq_biased"], 2 * n + 2)
                x1, x2 = k4[:, :, :, 0:NA], k4[:, :, :, NA:2 * NA]
                r = [rp[:, k, :].rearrange("p (q h n) -> p q h n", q=2, h=NH) for k in range(4)]
                c, s = (cv[:, k, :].rearrange("p (h n) -> p h n", h=NH).unsqueeze(1).to_broadcast([P, 2, NH, NA]) for k in range(2))
                v.tensor_tensor(r[0], x1, c, ALU.mult)
                v.tensor_tensor(r[1], x2, s, ALU.mult)
                v.tensor_tensor(r[2], x1, s, ALU.mult)
                v.tensor_tensor(r[3], x2, c, ALU.mult).then_inc(S["rotated"], 1)
                dve.wait_ge(S["rotated"], n + 1)
                v.tensor_tensor(x1, r[0], r[1], ALU.subtract).then_inc(S["kq_first"], 1)
                v.tensor_tensor(x2, r[2], r[3], ALU.add).then_inc(S["kq_ready"], 1)

            dve.wait_ge(S["cos_made"], B + 1)
            add_bias(0, 0)
            rotate(slice(0, 2 * P), 0, 0)

            def recurrence(first, last, extra):
              with dve.Fori(first, last) as i:
                for j in range(TB):
                    par = j % 2
                    t, nxt = i * TB + j, i * TB + (j + 1)
                    hs = bass.ds(i * (TB * NH) + j * NH, NH)
                    dve.wait_ge(S["w_mm"], i * 3 + min(j, 3) + 1)
                    add_bias(1 - par, nxt)
                    dve.wait_ge(S["z_tanh"], nxt)
                    dve.wait_ge(S["x_copied"], nxt + 1)
                    v.scalar_tensor_tensor(out=sz[:, par, :], in0=zt[:, :], scalar=1.0, in1=bank[0][:, 0:DI], op0=ALU.add, op1=ALU.mult).then_inc(S["sz_made"], 1)
                    xr = heads(xs_raw[:, par, :])
                    v.tensor_tensor(heads(xw[:, par, :]), xr, tok(ge[:, hs], HD), ALU.mult).then_inc(S["xw_made"], 1)
                    v.tensor_tensor(heads(xg[:, par, :]), xr, tok(gg[:, hs], HD), ALU.mult).then_inc(S["xg_made"], 1)
                    dve.wait_ge(S["s_mm"], nxt)
                    dve.wait_ge(S["e_exp"], nxt + 1)
                    dve.wait_ge(S["intra_mm"], t + 1)
                    v.tensor_tensor(mm[:, :], bank[4][:, :], em[:, par, :], ALU.mult).then_inc(S["m_made"], 1)
                    rotate(bass.ds((i * (TB * 2 * P) + (j + 1) * 2 * P), 2 * P), 1 - par, nxt)
                    dve.wait_ge(S["intra_mm"], nxt + 1)
                    dve.wait_ge(S["xc_made"], nxt + 1)
                    if j == 0:
                        v.tensor_tensor(y2[:, :], bank[5][:, 0:DI], xc[:, par, :], ALU.add).then_inc(S["y_b"], 1)
                    else:
                        v.tensor_tensor(y3[:, :], bank[5][:, 0:DI], xc[:, par, :], ALU.add).then_inc(S["y_c"], 1)
                    if j < 3:
                        dve.wait_ge(S["w_mm"], i * 3 + (j + 1) + 1)
                        if j == 0:
                            v.tensor_copy(st[:, 0, :], bank[6][:, 0:DI]).then_inc(S["st_made"], 1)
                        else:
                            dve.wait_ge(S["st_decayed"], i * 2 + j)
                            v.tensor_tensor(st[:, j % 2, :], std[:, :], bank[6][:, 0:DI], ALU.add).then_inc(S["st_made"], 1)
                    if j:
                        dve.wait_ge(S["y_a"], i * 3 + j + 1)
                        dve.wait_ge(S["y_c"], i * 3 + j)
                        v.tensor_tensor(y2[:, :], y1[:, :], y3[:, :], ALU.add).then_inc(S["y_b"], 1)
                    dve.wait_ge(S["y_b"], nxt + 1)
                    dve.wait_ge(S["yt_mm"], t + 1)
                    v.tensor_tensor(yg[:, :], y2[:, :], sz[:, par, :], ALU.mult).then_inc(S["y_gated"], 1)
                    extra(i, j)

            def combine(i, j):
                i = i - BP1
                dve.wait_ge(gath[j % 2], i * 128 + (64 * (j // 2) + 64))
                for t in range(2):
                    at = bass.ds(i * (8 * P) + (2 * j + t) * P, P)
                    dve.wait_ge(S["combine1"], i * 8 + (2 * j + t + 1))
                    v.scalar_tensor_tensor(out=x_all[:, at], in0=gb[j % 2][:, t, 1, :], scalar=gate[:, 1, bass.ds(i * 8 + (2 * j + t), 1)], in1=x_all[:, at],
                                           op0=ALU.mult, op1=ALU.add).then_inc(S["combine2"], 1)

            recurrence(0, BP1, lambda i, j: None)

            dve.wait_ge(S["intra_mm"], BP1 * TB + 1)
            for k in range(2):
                dve.wait_ge(scat[k], 16 * T + 16)
            for n in range(2 * TB):
                dve.wait_ge(S["wx_hi"], n + 1)
                v.tensor_tensor(piece(n, 1), by_chunk(stage[n % NST]), piece(n, 0), ALU.subtract).then_inc(S["wx_lo"], 1)

            def split_hidden(par, n):
                if not isinstance(n, int):
                    dve.wait_ge(S["down_mm"], n + 1)
                for half in range(2):
                    f = hf[:, half, :].rearrange("p (c n) -> p c n", c=2)
                    h, l = (hh[:, par, q, 2 * half:2 * half + 2, :] for q in range(2))
                    dve.wait_ge(S["gelu"], 2 * n + (half + 2))
                    v.tensor_copy(h, f).then_inc(S["h_hi"], 1)
                    dve.wait_ge(S["h_hi"], 2 * n + (half + 1))
                    v.tensor_tensor(l, f, h, ALU.subtract).then_inc(S["h_lo"], 1)

            def results(k, n):
                dve.wait_ge(S["y_lo"], n + 1)
                v.tensor_tensor(yb[:, 2 * k:2 * k + 2, :], y1[:, :].rearrange("p (t n) -> p t n", t=2),
                                bank[1][:, :].rearrange("p (t q n) -> p t q n", t=2, q=2)[:, :, 0, :], ALU.add).then_inc(S["y_copied"], 1)

            split_hidden(0, 0)
            split_hidden(1, 1)
            with dve.Fori(0, XB // 8) as i:
                for k in range(8):
                    if k % 2 == 0:
                        dve.wait_ge(S[f"y_out{k // 2 % 2}"], i * 32 + (k // 4) * 16 + 1)
                    results(k % 4, i * 8 + k)
                    split_hidden(k % 2, i * 8 + (k + 2))
            for g in range(2):
                dve.wait_ge(S[f"y_out{g}"], 16 * (XT // 8) + 1)
            recurrence(BP1, B, combine)
            dve.wait_ge(S["combine2"], T + 3)
            for b in range(B):
                at = ao_view[:, b * TB:(b + 1) * TB, 0:P]
                dve.wait_ge(S["x_added"], 2 * (B - BP1) + max(b - BP1 + 1, 0))
                v.tensor_tensor(at, at, x_all[:, b * 512:(b + 1) * 512].rearrange("p (t n) -> p t n", t=TB), ALU.add).then_inc(S["out_sum"], 1)

        @block.tensor
        def _(pe):
            te = nc.tensor
            for name in ("intra_mm", "w_mm", "yt_mm"):
                pe.sem_inc(S[name], 1)
            pe.sem_inc(S["theta_mm"], 2)
            pe.wait_ge(S["cross_made"], 3)
            pe.wait_ge(S["const_made"], 5)
            te.matmul(bank[0][:, 0:NH], wbt, cross[:, 0:NH], start=True, stop=True)
            te.matmul(bank[0][:, NH:2 * NH], wct, cross[:, NH:2 * NH], start=True, stop=True)
            te.matmul(bank[1][:, 0:NH], ones[:, :], cross[:, 2 * NH:], start=True, stop=True).then_inc(S["cross_mm"], 1)
            pe.wait_ge(S["w_lo"], 1)
            pe.wait_ge(S["cross_copied"], 2)

            def three(ps, at, cols):
                te.matmul(ps, xh[:, at], wh[:, cols], start=True, stop=False)
                te.matmul(ps, xh[:, at], wl[:, cols], start=False, stop=False)
                return te.matmul(ps, xl[:, at], wh[:, cols], start=False, stop=True)

            def turn(i, j):
                pe.wait_ge(S["xn_made"], i * TB + (j + 1))
                pe.wait_ge(S["xl_made"], i * TB + (j + 1))
                te.transpose(turn_banks[j][:, 0:P], xn[:, j, :], ident[:, :]).then_inc(S["xn_t"], 1)

            def project(i, j):
                pe.wait_ge(S["xl_made"], i * TB + (j + 1) + TB)
                pe.wait_ge(S["sq_done"], 2 * (i * TB + max(j - 1, 0)) + 1)
                three(bank[2 + j % 2][:, 0:NP1], bass.ds(i * 512 + j * P, P), slice(0, NP1)).then_inc(S["proj_mm"], 1)

            with pe.Fori(0, B) as i:
                turn(i, 0)
                for j in range(1, TB):
                    turn(i, j)
                    project(i, j - 1)
                project(i, TB - 1)

            pe.wait_ge(S["om_shift"], 5)
            te.matmul(bank[5][:, 0:TH], upper[:, :], adt[:, 0:TH], start=True, stop=True)
            te.matmul(bank[6][:, 0:TH], ones[:, :], adt[:, 0:TH], start=True, stop=True).then_inc(S["ell_mm"], 1)
            te.matmul(bank[4][:, 0:TH], shift[:, :], omega[:, 0:TH], start=True, stop=False)
            te.matmul(bank[4][:, 0:TH], wrap[:, :], omega[:, NH:TH + NH], start=False, stop=True).then_inc(S["ell_mm"], 1)
            pe.wait_ge(S["small_act"], 5)
            te.transpose(bank[7][:, 0:P], ell[:, 0:TH], ident[:, :]).then_inc(S["ellt_mm"], 1)

            pe.wait_ge(S["route"], R_CHOSEN)
            pe.wait_ge(S["const_made"], 5)
            te.matmul(bank[2][:, 0:T * NE], before[:, :], mm[:, 0:T * NE], start=True, stop=True).then_inc(S["rt_mm"], 1)
            te.matmul(bank[3][:, 0:T * NE], ones[:, :], mm[:, 0:T * NE], start=True, stop=True).then_inc(S["rt_mm"], 1)

            with pe.Fori(0, B // 2) as i:
                for par in range(2):
                    n = i * 2 + par
                    pe.wait_ge(S["ang_made"], n + 1)
                    pe.wait_ge(S["red3"], n + 1)
                    te.matmul(bank[par][:, :], upper[:, :], ang[par], start=True, stop=False)
                    for k in range(1, TB):
                        m = te.matmul(bank[par][:, k * P:], ones[:, :], ang[par][:, 0:(TB - k) * P], start=False, stop=(k == TB - 1))
                    m.then_inc(S["theta_mm"], 1)

            def zx(at):
                three(bank[0][:, :], at, slice(NP1, NP1 + NP2)).then_inc(S["zx_mm"], 1)

            def turn_kq(par, n):
                pe.wait_ge(S["kq_ready"], n + 1)
                pe.wait_ge(S["kq_first"], n + 1)
                pe.wait_ge(S["qt_copied"], n)
                for q in range(2):
                    for h in range(NH):
                        m = te.transpose(bank[2 + q][:, h * P:(h + 1) * P], kq[:, par, (q * NH + h) * P:(q * NH + h + 1) * P], ident[:, :])
                m.then_inc(S["kq_tr"], 1)

            def scores(n):
                pe.wait_ge(S["kt_copied"], n + 1)
                pe.wait_ge(S["qt_copied"], n + 1)
                pe.wait_ge(S["m_made"], n + 1)
                for h in range(NH):
                    m = te.matmul(bank[4][:, h * P:(h + 1) * P], kqt[:, 0, h * P:(h + 1) * P], kqt[:, 1, h * P:(h + 1) * P], start=True, stop=True)
                m.then_inc(S["s_mm"], 1)

            pe.wait_ge(S["red5"], B)
            pe.wait_ge(S["proj_out"], T)
            zx(slice(0, P))
            turn_kq(0, 0)
            scores(0)
            def recurrence(first, last):
              with pe.Fori(first, last) as i:
                for j in range(TB):
                    par = j % 2
                    t, nxt = i * TB + j, i * TB + (j + 1)
                    pe.wait_ge(S["st_made"], i * 3 + j + 1)
                    if j:
                        pe.wait_ge(S["y_a"], i * 3 + j)
                        for h in range(NH):
                            c = slice(h * HD, (h + 1) * HD)
                            m = te.matmul(bank[1][:, c], kqt[:, 1, h * P:(h + 1) * P], st[:, (j - 1) % 2, c], start=True, stop=True)
                        m.then_inc(S["inter_mm"], 1)
                    if j < 3:
                        pe.wait_ge(S["xw_made"], nxt + 1)
                        for h in range(NH):
                            c = slice(h * HD, (h + 1) * HD)
                            m = te.matmul(bank[6][:, c], kq[:, par, h * P:(h + 1) * P], xw[:, par, c], start=True, stop=True)
                        m.then_inc(S["w_mm"], 1)
                    pe.wait_ge(S["x_copied"], nxt + 1)
                    pe.wait_ge(S["sz_made"], nxt + 1)
                    zx(bass.ds(i * 512 + (j + 1) * P, P))
                    pe.wait_ge(S["m_made"], nxt + 1)
                    pe.wait_ge(S["xg_made"], nxt + 1)
                    pe.wait_ge(S["y_b"], t + 1)
                    for h in range(NH):
                        c = slice(h * HD, (h + 1) * HD)
                        m = te.matmul(bank[5][:, c], mm[:, h * P:(h + 1) * P], xg[:, par, c], start=True, stop=True)
                    m.then_inc(S["intra_mm"], 1)
                    turn_kq(1 - par, nxt)
                    pe.wait_ge(S["y_gated"], nxt)
                    pe.wait_ge(S["out_copied"], t + 1)
                    for c in range(2):
                        m = te.transpose(bank[7][:, c * P:(c + 1) * P], yg[:, c * P:(c + 1) * P], ident[:, :])
                    m.then_inc(S["yt_mm"], 1)
                    scores(nxt)
                    pe.wait_ge(S["yt_copied"], nxt)
                    pe.wait_ge(S["wo_half"], 1)
                    for c in range(2):
                        m = te.matmul(bank[7][:, DI:DI + P], ygt[:, c * P:(c + 1) * P], wo[:, c, :], start=(c == 0), stop=(c == 1))
                    m.then_inc(S["out_mm"], 1)

            recurrence(0, BP1)

            def turn_rows(k, n, load):
                if load is not None:
                    pe.wait_ge(S[f"xg_in{k // 2}"], load)
                if n is not None:
                    pe.wait_ge(S["xg_copied"], n)
                for q in range(2):
                    for t in range(2):
                        at = (q * 2 + t) * P
                        m = te.transpose(turned[:, at:at + P], xgb[:, 2 * k + t, q * P:(q + 1) * P], ident16[:, :])
                m.then_inc(S["x_t"], 1)

            def up(par, n, e):
                pe.wait_ge(S["xg_copied"], n + 1)
                if not isinstance(n, int):
                    pe.wait_ge(S["gelu"], 2 * n - 1)
                for c in range(UC):
                    ps = up_banks[par][c // 2][:, (c % 2) * RB:(c % 2 + 1) * RB]
                    w_hi, w_lo = (w[:, c * P:][:, bass.ds(e, P)] for w in (wu_h, wu_l))
                    te.matmul(ps, w_hi, xgt[:, par, 0, :], start=True, stop=False)
                    te.matmul(ps, w_hi, xgt[:, par, 1, :], start=False, stop=False)
                    m = te.matmul(ps, w_lo, xgt[:, par, 0, :], start=False, stop=True)
                    if c % 2:
                        m.then_inc(S["up_mm"], 1)

            wd_flat = wd.rearrange("p m q n -> p (m q n)")

            def down(par, n, e):
                pe.wait_ge(S["y_copied"], n + 1)
                pe.wait_ge(S["h_lo"], 2 * n + 2)
                e2, e4 = pe.snap(e * 2), pe.snap(e // UC)
                for t in range(2):
                    for c in range(UC):
                        w = wd_flat[:, c * 2 * P:]
                        h, l = (hh[:, par, q, c, t * P:(t + 1) * P] for q in range(2))
                        te.matmul(bank[1][:, t * RB:(t + 1) * RB], h, w[:, bass.ds(e2, 2 * P)], start=(c == 0), stop=False)
                        te.matmul(bank[1][:, t * RB:t * RB + P], l, w[:, bass.ds(e2, P)], start=False, stop=False)
                    m = te.matmul(bank[1][:, t * RB:t * RB + P], sel[:, :], bd[:, bass.ds(e4, P)], start=False, stop=True)
                m.then_inc(S["down_mm"], 1)

            def expert(n):
                return pe.value_load(tile_expert[0:1, n], min_val=0, max_val=(NE - 1) * U)

            pe.wait_ge(S["ident_low"], 1)
            turn_rows(0, None, 16)
            turn_rows(1, 1, None)
            pe.wait_ge(S["wx_lo"], TB)
            up(0, 0, expert(slice(0, 1)))
            turn_rows(2, 2, 16)
            up(1, 1, expert(slice(1, 2)))
            pe.wait_ge(S["wx_lo"], 2 * TB)
            pe.wait_ge(S["bd_made"], 7)
            with pe.Fori(0, XB // 8) as i:
                es = [expert(bass.ds(i * 8 + k, 1)) for k in range(2)]
                for k in range(8):
                    ahead = k + 3
                    es.append(expert(bass.ds(i * 8 + (k + 2), 1)))
                    turn_rows(ahead % 4, i * 8 + ahead, i * 32 + (ahead // 4 + 1) * 16 if ahead % 2 == 0 else None)
                    down(k % 2, i * 8 + k, es[k])
                    up(k % 2, i * 8 + (k + 2), es[k + 2])
            recurrence(BP1, B)


def kernel(L0_attn_u, L0_attn_W_in, L0_attn_W_out, L0_attn_dt_bias, L0_attn_B_bias, L0_attn_C_bias,
           L0_attn_B_norm_w, L0_attn_C_norm_w, L0_attn_D, L0_ffn_w_router, L0_ffn_w_up, L0_ffn_b_up,
           L0_ffn_w_down, L0_ffn_b_down):
    import numpy as np
    import concourse.bacc as bacc
    from concourse.bass_utils import run_bass_kernel_spmd

    w = np.asarray(L0_attn_W_in)
    z, xx, bg, cg, rest = w[:, :256], w[:, 256:512], w[:, 512:640], w[:, 640:768], w[:, 768:]
    bb, cb = np.asarray(L0_attn_B_bias), np.asarray(L0_attn_C_bias)
    bw, cw = np.asarray(L0_attn_B_norm_w), np.asarray(L0_attn_C_norm_w)
    arrays = {
        "x": np.asarray(L0_attn_u).reshape(B * L, DM),
        "w_in": np.concatenate([bg, cg, rest, np.asarray(L0_ffn_w_router).T, z, xx], axis=1),
        "cols": np.concatenate([bg.T, cg.T, bw[:, None], cw[:, None], bb.T, cb.T], axis=1),
        "rows": np.concatenate([bw, cw, bb.reshape(-1), cb.reshape(-1), np.asarray(L0_attn_dt_bias), np.asarray(L0_attn_D)]),
        "w_out": np.asarray(L0_attn_W_out),
        "w_up": np.asarray(L0_ffn_w_up).transpose(2, 0, 1).reshape(DM, NE * U),
        "b_up": np.asarray(L0_ffn_b_up).reshape(NE, UC, P).transpose(2, 0, 1).reshape(P, NE * UC),
        "w_dn": np.asarray(L0_ffn_w_down).reshape(NE, DM, UC, P).transpose(3, 0, 2, 1).reshape(P, NE * U),
        "b_dn": np.asarray(L0_ffn_b_down).reshape(-1),
    }
    arrays = {k: np.ascontiguousarray(a) for k, a in arrays.items()}
    nc = bacc.Bacc("TRN2", target_bir_lowering=False, num_devices=1)
    args = [nc.dram_tensor(k, a.shape, F32, kind="ExternalInput").ap() for k, a in arrays.items()]
    out = nc.dram_tensor("out", (B * L, DM), F32, kind="ExternalOutput").ap()
    build(nc, *args, out)
    r = run_bass_kernel_spmd(nc, [arrays], core_ids=[0])
    return r.results[0]["out"].reshape(B, L, DM)
```
